# Optimizing a Trainium2 kernel written in Bass

```python
import numpy as np
import jax
import jax.numpy as jnp

def _softmax(x, axis=-1):
    return jax.nn.softmax(x, axis=axis)

def _gelu(x):
    return jax.nn.gelu(x, approximate=True)

def _silu(x):
    return jax.nn.silu(x)

def _sigmoid(x):
    return jax.nn.sigmoid(x)

def _layernorm(x, axis=-1, eps=1e-05):
    m = jnp.mean(x, axis=axis, keepdims=True)
    v = jnp.var(x, axis=axis, keepdims=True)
    return (x - m) / jnp.sqrt(v + eps)

def _scatter_add(tgt, idx, src, axis=0):
    return tgt.at[idx].add(src)

def _segment_sum(src, seg, n):
    return jax.ops.segment_sum(src, seg, n)
kernel_name = 'mk_adj_ffn_d2_adj_r2_7a9acd'

def setup_inputs(seed: int=0):
    np.random.seed(seed)
    _w = jnp.asarray

    def _rec_inputs():
        import jax
        import jax.numpy as jnp
        _gk = jax.random.key(seed)
        x = -0.0002928 + 1 * jax.random.normal(jax.random.fold_in(_gk, 1), (64, 128, 128), jnp.float32)
        _a = jax.random.bernoulli(jax.random.fold_in(_gk, 2), 0.015625, (64, 128, 128))
        _a = jnp.logical_or(_a, jnp.swapaxes(_a, -1, -2))
        _a = jnp.logical_or(_a, jnp.eye(128, dtype=bool))
        _af = _a.astype(jnp.float32)
        _af = _af * jax.random.uniform(jax.random.fold_in(_gk, 3), (64, 128, 128), jnp.float32, 0.05, 1)
        adj = _af
        _nm = jnp.ones((64, 128), dtype=bool)
        nodemask = jnp.where(_nm, 1.0, 0.0).astype(jnp.float32)
        return (x, adj, nodemask)
    x, adj, nodemask = _rec_inputs()

    def _L0_gnn_setup():
        import jax, jax.numpy as jnp
        import numpy as np
        key = jax.random.key(seed)
        k1, k2, k3, k4 = jax.random.split(key, 4)
        B, N, F_in, F_out = (8, 1024, 128, 128)
        x = jax.random.normal(k1, (B, N, F_in), dtype=jnp.float32)
        adj = jax.random.uniform(k2, (B, N, N), dtype=jnp.float32)
        stdv = 1.0 / np.sqrt(F_out)
        weight = jax.random.uniform(k3, (F_in, F_out), dtype=jnp.float32, minval=-stdv, maxval=stdv)
        bias = jax.random.uniform(k4, (F_out,), dtype=jnp.float32, minval=-stdv, maxval=stdv)
        return {'x': x, 'adj': adj, 'weight': weight, 'bias': bias}
    _L0_gnn_all = _L0_gnn_setup()
    _L0_gnn_in = {k: v for k, v in _L0_gnn_all.items() if k in ('weight', 'bias')}
    del _L0_gnn_all

    def _L0_ffn_setup():
        import jax, jax.numpy as jnp
        import numpy as np
        NUM_EXPERTS = 8
        TOP_K = 2
        B, S, D = (8, 4096, 128)

        def _moe(tokens, router_w, w1, b1, w2, b2):
            N = tokens.shape[0]
            E = router_w.shape[0]
            logits = tokens.astype(jnp.float32) @ router_w.astype(jnp.float32).T
            probs = jax.nn.softmax(logits, axis=-1)
            rw, re = jax.lax.top_k(probs, TOP_K)
            if TOP_K > 1:
                rw = rw / jnp.maximum(rw.sum(-1, keepdims=True), 1e-12)
            rw = rw.astype(tokens.dtype)
            combine = jnp.zeros((N, E), tokens.dtype).at[jnp.arange(N)[:, None], re].set(rw)
            out = tokens
            for e in range(E):
                h = jax.nn.gelu(tokens @ w1[e] + b1[e], approximate=False)
                y = h @ w2[e] + b2[e]
                out = out + combine[:, e:e + 1] * y
            return out
        key = jax.random.key(seed)
        ks = jax.random.split(key, 4)
        scale = 1.0 / np.sqrt(D).astype(np.float32)
        return {'input_embeddings': jax.random.normal(ks[0], (B, S, D), jnp.float32), 'router_w': jax.random.normal(ks[1], (NUM_EXPERTS, D), jnp.float32) * scale, 'w1': jax.random.normal(ks[2], (NUM_EXPERTS, D, D), jnp.float32) * scale, 'b1': jnp.zeros((NUM_EXPERTS, D), jnp.float32), 'w2': jax.random.normal(ks[3], (NUM_EXPERTS, D, D), jnp.float32) * scale, 'b2': jnp.zeros((NUM_EXPERTS, D), jnp.float32)}
    _L0_ffn_all = _L0_ffn_setup()
    _L0_ffn_in = {k: v for k, v in _L0_ffn_all.items() if k in ('router_w', 'w1', 'b1', 'w2', 'b2')}
    del _L0_ffn_all

    def _L1_gnn_setup():
        import jax, jax.numpy as jnp
        import numpy as np
        B, N, IN_DIM, OUT_DIM = (8, 1024, 128, 128)
        EDGE_P = 0.02
        MASK_P = 0.9
        key = jax.random.key(seed)
        ks = jax.random.split(key, 8)
        x = jax.random.normal(ks[0], (B, N, IN_DIM), dtype=jnp.float32)
        adj = (jax.random.uniform(ks[1], (B, N, N)) < EDGE_P).astype(jnp.float32)
        mask = (jax.random.uniform(ks[2], (B, N)) < MASK_P).astype(jnp.float32)
        lim1 = 1.0 / np.sqrt(IN_DIM)
        W = jax.random.uniform(ks[3], (OUT_DIM, IN_DIM), minval=-lim1, maxval=lim1, dtype=jnp.float32)
        b = jax.random.uniform(ks[4], (OUT_DIM,), minval=-lim1, maxval=lim1, dtype=jnp.float32)
        lim2 = 1.0 / np.sqrt(2 * OUT_DIM)
        a1 = jax.random.uniform(ks[5], (OUT_DIM,), minval=-lim2, maxval=lim2, dtype=jnp.float32)
        a2 = jax.random.uniform(ks[6], (OUT_DIM,), minval=-lim2, maxval=lim2, dtype=jnp.float32)
        att_b = jax.random.uniform(ks[7], (), minval=-lim2, maxval=lim2, dtype=jnp.float32)
        return {'x': x, 'adj': adj, 'mask': mask, 'W': W, 'b': b, 'a1': a1, 'a2': a2, 'att_b': att_b}
    _L1_gnn_all = _L1_gnn_setup()
    _L1_gnn_in = {k: v for k, v in _L1_gnn_all.items() if k in ('W', 'b', 'a1', 'a2', 'att_b')}
    del _L1_gnn_all

    def _L1_ffn_setup():
        import math
        import jax, jax.numpy as jnp
        import numpy as np
        CAPACITY_FACTOR = 1.25
        TOP_K = 2
        LN_EPS = 1e-05

        def _layer_norm(x, gamma, beta):
            mu = jnp.mean(x, axis=-1, keepdims=True)
            var = jnp.var(x, axis=-1, keepdims=True)
            return (x - mu) * jax.lax.rsqrt(var + LN_EPS) * gamma + beta
        key = jax.random.key(seed)
        ks = jax.random.split(key, 4)
        B, S, D, F, E = (8, 2048, 128, 256, 8)
        x = jax.random.normal(ks[0], (B, S, D), dtype=jnp.float32)
        Wr = jax.random.normal(ks[1], (D, E), dtype=jnp.float32) / np.sqrt(D)
        br = jnp.zeros((E,), jnp.float32)
        W1 = jax.random.normal(ks[2], (E, D, F), dtype=jnp.float32) / np.sqrt(D)
        b1 = jnp.zeros((E, F), jnp.float32)
        W2 = jax.random.normal(ks[3], (E, F, D), dtype=jnp.float32) / np.sqrt(F)
        b2 = jnp.zeros((E, D), jnp.float32)
        gamma = jnp.ones((D,), jnp.float32)
        beta = jnp.zeros((D,), jnp.float32)
        return {'x': x, 'Wr': Wr, 'br': br, 'W1': W1, 'b1': b1, 'W2': W2, 'b2': b2, 'gamma': gamma, 'beta': beta}
    _L1_ffn_all = _L1_ffn_setup()
    _L1_ffn_in = {k: v for k, v in _L1_ffn_all.items() if k in ('Wr', 'br', 'W1', 'b1', 'W2', 'b2', 'gamma', 'beta')}
    del _L1_ffn_all
    return {'x': x, 'adj': adj, 'nodemask': nodemask, 'L0_gnn_weight': _L0_gnn_in['weight'], 'L0_gnn_bias': _L0_gnn_in['bias'], 'L0_ffn_router_w': _L0_ffn_in['router_w'], 'L0_ffn_w1': _L0_ffn_in['w1'], 'L0_ffn_b1': _L0_ffn_in['b1'], 'L0_ffn_w2': _L0_ffn_in['w2'], 'L0_ffn_b2': _L0_ffn_in['b2'], 'L1_gnn_W': _L1_gnn_in['W'], 'L1_gnn_b': _L1_gnn_in['b'], 'L1_gnn_a1': _L1_gnn_in['a1'], 'L1_gnn_a2': _L1_gnn_in['a2'], 'L1_gnn_att_b': _L1_gnn_in['att_b'], 'L1_ffn_Wr': _L1_ffn_in['Wr'], 'L1_ffn_br': _L1_ffn_in['br'], 'L1_ffn_W1': _L1_ffn_in['W1'], 'L1_ffn_b1': _L1_ffn_in['b1'], 'L1_ffn_W2': _L1_ffn_in['W2'], 'L1_ffn_b2': _L1_ffn_in['b2'], 'L1_ffn_gamma': _L1_ffn_in['gamma'], 'L1_ffn_beta': _L1_ffn_in['beta']}

def reference(x, adj, nodemask, L0_gnn_weight, L0_gnn_bias, L0_ffn_router_w, L0_ffn_w1, L0_ffn_b1, L0_ffn_w2, L0_ffn_b2, L1_gnn_W, L1_gnn_b, L1_gnn_a1, L1_gnn_a2, L1_gnn_att_b, L1_ffn_Wr, L1_ffn_br, L1_ffn_W1, L1_ffn_b1, L1_ffn_W2, L1_ffn_b2, L1_ffn_gamma, L1_ffn_beta):
    import jax
    import jax.numpy as jnp

    def _L0_gnn_ref(x, adj, weight, bias):
        import jax, jax.numpy as jnp
        import numpy as np
        support = jnp.einsum('bni,io->bno', x, weight)
        out = jnp.einsum('bnm,bmo->bno', adj, support)
        return out + bias

    def _L0_ffn_ref(input_embeddings, router_w, w1, b1, w2, b2):
        import jax, jax.numpy as jnp
        import numpy as np
        NUM_EXPERTS = 8
        TOP_K = 2
        B, S, D = (8, 4096, 128)

        def _moe(tokens, router_w, w1, b1, w2, b2):
            N = tokens.shape[0]
            E = router_w.shape[0]
            logits = tokens.astype(jnp.float32) @ router_w.astype(jnp.float32).T
            probs = jax.nn.softmax(logits, axis=-1)
            rw, re = jax.lax.top_k(probs, TOP_K)
            if TOP_K > 1:
                rw = rw / jnp.maximum(rw.sum(-1, keepdims=True), 1e-12)
            rw = rw.astype(tokens.dtype)
            combine = jnp.zeros((N, E), tokens.dtype).at[jnp.arange(N)[:, None], re].set(rw)
            out = tokens
            for e in range(E):
                h = jax.nn.gelu(tokens @ w1[e] + b1[e], approximate=False)
                y = h @ w2[e] + b2[e]
                out = out + combine[:, e:e + 1] * y
            return out
        b, s, d = input_embeddings.shape
        tokens = input_embeddings.reshape(b * s, d)
        return _moe(tokens, router_w, w1, b1, w2, b2).reshape(b, s, d)

    def _L1_gnn_ref(x, adj, mask, W, b, a1, a2, att_b):
        import jax, jax.numpy as jnp
        import numpy as np
        B, N, IN_DIM, OUT_DIM = (8, 1024, 128, 128)
        EDGE_P = 0.02
        MASK_P = 0.9
        h = jnp.einsum('bni,di->bnd', x, W) + b
        s1 = h @ a1
        s2 = h @ a2
        logits = s1[:, :, None] + s2[:, None, :] + att_b
        att = jax.nn.sigmoid(logits) * adj
        att = att * mask[:, :, None] * mask[:, None, :]
        att = att / (jnp.sum(att, axis=-1, keepdims=True) + 1e-08)
        h_new = jnp.einsum('bij,bjd->bid', att, h)
        return h_new * mask[:, :, None]

    def _L1_ffn_ref(x, Wr, br, W1, b1, W2, b2, gamma, beta):
        import math
        import jax, jax.numpy as jnp
        import numpy as np
        CAPACITY_FACTOR = 1.25
        TOP_K = 2
        LN_EPS = 1e-05

        def _layer_norm(x, gamma, beta):
            mu = jnp.mean(x, axis=-1, keepdims=True)
            var = jnp.var(x, axis=-1, keepdims=True)
            return (x - mu) * jax.lax.rsqrt(var + LN_EPS) * gamma + beta
        B, S, D = x.shape
        E = Wr.shape[1]
        N = B * S
        K = TOP_K
        logits = jnp.mean(x, axis=1) @ Wr + br
        routing_weights = jax.nn.softmax(logits, axis=-1)
        capacity = float(math.ceil(N * CAPACITY_FACTOR / E))
        expected_loads = routing_weights.sum(axis=0) * (N / B)
        scale = jnp.where(expected_loads > capacity, capacity / expected_loads, 1.0)
        routing_weights = jax.nn.softmax(routing_weights * scale, axis=-1)
        rw_tok = jnp.broadcast_to(routing_weights[:, None, :], (B, S, E)).reshape(N, E)
        top_w, top_i = jax.lax.top_k(rw_tok, K)
        top_w = jax.nn.softmax(top_w, axis=-1)
        xf = x.reshape(N, D)
        h = jax.nn.gelu(jnp.einsum('nd,edf->enf', xf, W1) + b1[:, None, :], approximate=False)
        y = jnp.einsum('enf,efd->end', h, W2) + b2[:, None, :]
        w_dense = jnp.zeros((N, E), x.dtype).at[jnp.arange(N)[:, None], top_i].add(top_w)
        out = jnp.einsum('ne,end->nd', w_dense, y).reshape(B, S, D)
        out = _layer_norm(out + x, gamma, beta)
        return out
    x = x + _L0_gnn_ref(_layernorm(x, axis=-1), adj, L0_gnn_weight, L0_gnn_bias)
    x = x + _L0_ffn_ref(_layernorm(x, axis=-1), L0_ffn_router_w, L0_ffn_w1, L0_ffn_b1, L0_ffn_w2, L0_ffn_b2)
    x = x + _L1_gnn_ref(_layernorm(x, axis=-1), adj, nodemask, L1_gnn_W, L1_gnn_b, L1_gnn_a1, L1_gnn_a2, L1_gnn_att_b)
    x = x + _L1_ffn_ref(_layernorm(x, axis=-1), L1_ffn_Wr, L1_ffn_br, L1_ffn_W1, L1_ffn_b1, L1_ffn_W2, L1_ffn_b2, L1_ffn_gamma, L1_ffn_beta)
    return x

_drawn_inputs = setup_inputs


def setup_inputs(seed=0):
    import zlib

    import numpy as np

    out = dict(_drawn_inputs(seed))
    spreads = {'L0_ffn_b1': (0.0, 0.1),
     'L0_ffn_b2': (0.0, 0.1),
     'L1_ffn_br': (0.0, 0.1),
     'L1_ffn_b1': (0.0, 0.585),
     'L1_ffn_b2': (0.0, 0.402),
     'L1_ffn_gamma': (1.0, 0.2),
     'L1_ffn_beta': (0.0, 0.1)}
    factors = {'L1_gnn_a1': 55.908}
    for name, (base, spread) in spreads.items():
        noise = np.random.default_rng([zlib.crc32(name.encode()), seed]).standard_normal(out[name].shape)
        drawn = base * np.exp(spread * noise) if base else spread * noise
        out[name] = jnp.asarray(drawn.astype(out[name].dtype))
    for name, factor in factors.items():
        out[name] = (out[name] * factor).astype(out[name].dtype)
    return out
```

```python
import concourse.bass as bass
from concourse import mybir
from contextlib import ExitStack

fp32 = mybir.dt.float32
fp16 = mybir.dt.float16
int32 = mybir.dt.int32
ALU = mybir.AluOpType
ACT = mybir.ActivationFunctionType
AX = mybir.AxisListType


class Count:

    def __init__(self, sem, free=0):
        self.sem, self.free = sem, free

    def wait(self, eng, n):
        eng.wait_ge(self.sem, n + self.free)


class Chain:

    def __init__(self, eng, sem, base=0):
        self.eng, self.sem, self.base, self.n = eng, sem, base, 0

    def __call__(self, ins):
        self.n += 1
        ins.then_inc(self.sem, 1)
        self.eng.wait_ge(self.sem, self.base + self.n)


def graph_network(nc, x, adj, nodemask, g0_w, g0_b, f0_router, f0_w1, f0_b1, f0_w2, f0_b2,
                  g1_w, g1_b, g1_a1, g1_a2, g1_attb, f1_wr, f1_br, f1_w1, f1_b1, f1_w2, f1_b2,
                  gamma, beta, out):
    B, N, D = x.shape
    E = f0_router.shape[0]
    F = f1_w1.shape[2]
    HALVES = F // D
    T = 4
    GW = T * N
    G = B // T
    CAPACITY = float(-(-B * N * 5 // (4 * E)))
    EPS = 1e-5
    WS = 64.0
    BIG = -3.0e38

    ctx = ExitStack()
    with ctx:
        def sb(name, shape, dt=fp32):
            return ctx.enter_context(nc.sbuf_tensor(name, shape, dt))

        credits = []

        def count(name, free=0):
            c = Count(ctx.enter_context(nc.semaphore(name)), free)
            if free:
                credits.append(c)
            return c

        def sem(name):
            return ctx.enter_context(nc.semaphore(name))

        X = sb("X", [128, B * D])
        adjT = sb("adjT", [128, B * N])
        XTh = sb("XTh", [128, B * N], fp16)
        XTl = sb("XTl", [128, B * N], fp16)
        adj_in = sb("adj_in", [128, 4, GW])
        XN = sb("XN", [128, 2, GW])
        ZT = sb("ZT", [128, 2, GW])

        stats = sb("stats", [128, B, 6])
        rstd = sb("rstd", [128, B])
        nmr = sb("nmr", [128, B])
        ln_a = sb("ln_a", [128, B])
        ln_b = sb("ln_b", [128, B])
        ln_c = sb("ln_c", [128, B])

        ident = sb("ident", [128, 128])
        ident16 = sb("ident16", [128, 128], fp16)
        ones = sb("ones", [128, 128])
        selector = sb("selector", [128, E, 128], fp16)
        rank = sb("rank", [128, E])
        two_ones = sb("two_ones", [128, 128], fp16)
        rows_in = sb("rows_in", [128, 128])
        cols = sb("cols", [128, 128])
        g0w = sb("g0w", [128, D])
        g0b = sb("g0b", [128, D])
        g1w = sb("g1w", [128, D])
        g1b = sb("g1b", [128, D])
        avec = sb("avec", [128, 4])
        attb = sb("attb", [128, 1])
        wr = sb("wr", [128, E])
        br = sb("br", [B, E])
        gam = sb("gam", [128, D])
        bet = sb("bet", [128, D])
        epst = sb("epst", [128, 1])
        router_h = sb("router_h", [128, E], fp16)
        router_l = sb("router_l", [128, E], fp16)
        raw = sb("raw", [128, 2 * E * D + 2 * E * F])
        w1raw = raw[:, 0:E * D]
        w2raw = raw[:, E * D:2 * E * D]
        m1raw = raw[:, 2 * E * D:2 * E * D + E * F]
        m2raw = raw[:, 2 * E * D + E * F:]
        w1h, w1l = sb("w1h", [128, E * D], fp16), sb("w1l", [128, E * D], fp16)
        w2h, w2l = sb("w2h", [128, E * D], fp16), sb("w2l", [128, E * D], fp16)
        m1h, m1l = sb("m1h", [128, E * F], fp16), sb("m1l", [128, E * F], fp16)
        m2h, m2l = sb("m2h", [128, E * F], fp16), sb("m2l", [128, E * F], fp16)
        b2raw = sb("b2raw", [128, D])
        b2w = sb("b2w", [128, D], fp16)
        b2t = sb("b2t", [128, D], fp16)
        mb1raw = XTl[:, :].bitcast(fp32)[0:64, 0:E * F]
        mb1 = sb("mb1", [128, E * F], fp16)
        mb2 = sb("mb2", [128, E * D], fp16)
        wTh, wTl = sb("wTh", [128, D], fp16), sb("wTl", [128, D], fp16)
        v12 = sb("v12", [128, 2])
        v1h, v1l = sb("v1h", [128, 128], fp16), sb("v1l", [128, 128], fp16)
        v2h, v2l = sb("v2h", [128, 1], fp16), sb("v2l", [128, 1], fp16)
        att_const = sb("att_const", [128, 1])

        lg = [sb(f"lg{i}", [128, B * E]) for i in range(4)]
        small = [sb(f"small{i}", [128, B]) for i in range(3)]
        cpad = sb("cpad", [128, 2, T, 128], fp16)
        cT = sb("cT", [128, 2, GW], fp16)
        h32 = adj_in[:, 0:2, :]
        hc32 = adj_in[:, 2:4, :]
        hh = sb("hh", [128, 4, GW], fp16)
        hl = sb("hl", [128, 4, GW], fp16)

        def in_raw(k, n=2):
            return raw[:, k * GW:(k + n) * GW].rearrange("p (a c) -> p a c", a=n)
        sig, att, H = in_raw(0), in_raw(2), in_raw(4)
        U = in_raw(6)
        s2c = sb("s2c", [128, 2, T])
        frac = sb("frac", [128, 2, 3 * T])
        xsum = sb("xsum", [128, B])

        r = [sb(f"r{i}", [B, E]) for i in range(6)]
        rc = [sb(f"rc{i}", [B, 1]) for i in range(8)]
        diag = sb("diag", [B, 4, B])
        gate = sb("gate", [128, 4, B])
        index = sb("index", [128, 2 * B], int32)

        PS = ctx.enter_context(nc.psum_tensor("PS", [128, 8, 512], fp32))

        def bank(i):
            return PS[:, i, :]

        def tile(t, b, n=1, w=128):
            return t[:, bass.ds(b * w, n * w)]

        vec = sem("vec_own")
        scl = sem("act_own")
        pool = sem("pool_own")
        weights_loaded = sem("weights_loaded")
        ident_made = sem("ident_made")
        prep_pe = sem("prep_pe")
        prep_hi = sem("prep_hi")
        prep_done = sem("prep_done")
        cols_saved = sem("cols_saved")
        group_loaded = [sem(f"group_loaded{q}") for q in range(4)]
        adj_turned = count("adj_turned", 4)
        adjT_saved = count("adjT_saved", 2)
        moments = sem("moments")
        sqrt_done = sem("sqrt_done")
        ln_ready = sem("ln_ready")
        xn_ready = count("xn_ready")
        z_made = count("z_made", 2)
        z_saved = count("z_saved", 2)
        bias_added = count("bias_added")
        o_made = count("o_made")
        x1_saved = count("x1_saved", 2)
        n2_ready = count("n2_ready")
        n2_turned = count("n2_turned")
        n2h_saved = count("n2h_saved")
        n2l_saved = count("n2l_saved", 2)
        n2_added = count("n2_added", 2)
        adj_masked = sem("adj_masked")
        logits_made = sem("logits_made")
        exp_in = sem("exp_in")
        exp_out = sem("exp_out")
        gates_ready = sem("gates_ready")
        cpad_ready = count("cpad_ready")
        c_turned = count("c_turned", 2)
        c_saved = count("c_saved")
        up_made = count("up_made")
        gelu_done = count("gelu_done", 2)
        cb_made = count("cb_made")
        hc_ready = count("hc_ready", 2)
        hh_ready = count("hh_ready", 2)
        hl_ready = count("hl_ready", 2)
        down_made = count("down_made", 4)
        moe_made = count("moe_made")
        x2_saved = count("x2_saved", 2)
        n3_ready = count("n3_ready")
        n3_turned = count("n3_turned", 2)
        n3h_saved = count("n3h_saved")
        n3l_saved = count("n3l_saved")
        proj_made = count("proj_made")
        s2_saved = count("s2_saved")
        h_saved = count("h_saved", 2)
        sig_ready = count("sig_ready", 2)
        att_ready = count("att_ready", 2)
        att_used = count("att_used", 2)
        u_saved = count("u_saved", 2)
        x3_ready = count("x3_ready", 2)
        n4_ready = count("n4_ready")
        n4_turned = count("n4_turned")
        n4h_saved = count("n4h_saved")
        n4l_saved = count("n4l_saved", 2)
        route_pe = sem("route_pe")
        route_dve = sem("route_dve")
        route_act = sem("route_act")
        route_ready = sem("route_ready")
        f_made = count("f_made")
        g_ready = count("g_ready", 2)
        gh_ready = count("gh_ready", 2)
        gl_ready = count("gl_ready", 2)
        y_made = count("y_made", 2)
        y_saved = count("y_saved", 2)
        norm_ready = count("norm_ready")
        xb_ready = count("xb_ready")
        out_ready = count("out_ready")
        stored = [count(f"stored{q}", 16) for q in range(2)]

        block = ctx.enter_context(nc.Block())

        @block.sync
        def _(sp):
            for c in credits:
                sp.sem_inc(c.sem, c.free)
            n = 0

            def load(dst, src):
                sp.dma_start(dst, src).then_inc(weights_loaded, 16)

            load(rows_in[0:B, :], nodemask)
            load(rows_in[B:B + E, :], f0_router)
            load(rows_in[B + E:B + 2 * E, :], f0_b1)
            load(g1w[:, :], g1_w)
            load(avec[:, 0:1], g1_a1.rearrange("(d o) -> d o", o=1))
            load(avec[:, 1:2], g1_a2.rearrange("(d o) -> d o", o=1))
            load(avec[:, 2:3], g1_b.rearrange("(d o) -> d o", o=1))
            load(attb[:, :], g1_attb.partition_broadcast(128))
            load(g0w[:, :], g0_w)
            load(g0b[:, :], g0_b.partition_broadcast(128))
            load(g1b[:, :], g1_b.partition_broadcast(128))
            load(gam[:, :], gamma.partition_broadcast(128))
            load(bet[:, :], beta.partition_broadcast(128))
            load(wr[:, :], f1_wr)
            load(br[:, :], f1_br.partition_broadcast(B))
            for q in (0, 32, 64):
                load(b2raw[q:q + E, :], f0_b2)
            for q in (0, 32):
                load(mb1raw[q:q + 1, :], f1_b1.rearrange("(o e) f -> o (e f)", o=1))
            load(w1raw.rearrange("p (e f) -> p e f", e=E), f0_w1.rearrange("e d f -> d e f"))
            load(w2raw.rearrange("p (e f) -> p e f", e=E), f0_w2.rearrange("e f d -> f e d"))
            load(m1raw.rearrange("p (e f) -> p e f", e=E), f1_w1.rearrange("e d f -> d e f"))
            load(m2raw.rearrange("p (e h d) -> p e h d", e=E, h=HALVES),
                 f1_w2.rearrange("e (h p) d -> p e h d", p=128))
            with sp.Fori(0, G // 4) as it:
                for q in range(4):
                    adj_turned.wait(sp, it * 4 + (q - 3))
                    g = it * 4 + q
                    sp.dma_start(tile(X, g, 1, GW).rearrange("p (t d) -> p t d", t=T),
                                 x[bass.ds(g * T, T), :, :].rearrange("t p d -> p t d")).then_inc(group_loaded[q], 16)
                    sp.dma_start(adj_in[:, q, :].rearrange("p (t d) -> p t d", t=T),
                                 adj[bass.ds(g * T, T), :, :].rearrange("t p d -> p t d")).then_inc(group_loaded[q], 16)
            sp.wait_ge(prep_done, 1)
            for q in (0, 32):
                load(mb1raw[q:q + 1, 0:E * D], f1_b2.rearrange("(o e) f -> o (e f)", o=1))

            with sp.Fori(0, G // 2) as it:
                for p in range(2):
                    g = it * 2 + p
                    out_ready.wait(sp, g + 1)
                    sp.dma_start(out[bass.ds(g * T, T), :, :].rearrange("t p d -> p t d"),
                                 tile(X, g, 1, GW).rearrange("p (t d) -> p t d", t=T)).then_inc(stored[p].sem, 16)
            for p in range(2):
                stored[p].wait(sp, 16 * (G // 2))

        WEIGHTS = 16 * (15 + 3 + 2 + 4)

        @block.gpsimd
        def _(g_):
            own = Chain(g_, pool)
            own(g_.memset(ident[:, :], 0.0))
            own(g_.affine_select(out=ident[:, :], in_=ident[:, :], compare_op=ALU.not_equal, fill=1.0,
                                 base=0, pattern=[[-1, 128]], channel_multiplier=1))
            own(g_.memset(ones[:, :], 1.0))
            own(g_.memset(epst[:, :], EPS))
            own(g_.memset(two_ones[:, :], 0.0))
            own(g_.memset(two_ones[0:1, :], 1.0))
            own(g_.memset(two_ones[32:33, :], 1.0))
            own(g_.memset(b2w[:, :], 0.0))
            own(g_.memset(mb1[:, :], 0.0))
            own(g_.memset(mb2[:, :], 0.0))
            own(g_.memset(cpad[:, :, :, :], 0.0))
            for e in range(E):
                own(g_.memset(rank[:, e:e + 1], float(E - e)))
            g_.sem_inc(ident_made, 1)

            with g_.Fori(0, G // 2) as it:
                for p in range(2):
                    g = it * 2 + p
                    xn_ready.wait(g_, g + 1)
                    g_.tensor_tensor(tile(X, g, 1, GW).rearrange("p (t d) -> p t d", t=T),
                                     tile(X, g, 1, GW).rearrange("p (t d) -> p t d", t=T),
                                     g0b[:, :].unsqueeze(1).broadcast_to([128, T, D]),
                                     ALU.add).then_inc(bias_added.sem, 1)
            with g_.Fori(0, G // 2) as it:
                for p in range(2):
                    g = it * 2 + p
                    n2_ready.wait(g_, g + 1)
                    g_.tensor_tensor(tile(X, g, 1, GW), tile(X, g, 1, GW), XN[:, p, :], ALU.add).then_inc(n2_added.sem, 1)
                    g_.tensor_tensor(tile(adjT, g, 1, GW).rearrange("p (t d) -> p t d", t=T),
                                     tile(adjT, g, 1, GW).rearrange("p (t d) -> p t d", t=T),
                                     cols[:, bass.ds(g * T, T)].unsqueeze(2).broadcast_to([128, T, D]),
                                     ALU.mult).then_inc(adj_masked, 1)
            with g_.Fori(0, G * E // 8) as it:
                for k in range(8):
                    n = it * 8 + k
                    hh_ready.wait(g_, n + 1)
                    down_made.wait(g_, n - 3)
                    g_.tensor_tensor(hl[:, k % 4, :], hc32[:, k % 2, :], hh[:, k % 4, :],
                                     ALU.subtract).then_inc(hl_ready.sem, 1)
            def attend(g, p):
                sig_ready.wait(g_, g + 1)
                att_used.wait(g_, g - 1)
                g_.tensor_tensor(att[:, p, :], sig[:, p, :], tile(adjT, g, 1, GW), ALU.mult).then_inc(att_ready.sem, 1)

            def residual(g, p):
                u_saved.wait(g_, g + 1)
                g_.tensor_tensor(tile(X, g, 1, GW), U[:, p, :], tile(X, g, 1, GW), ALU.add).then_inc(x3_ready.sem, 1)

            attend(0, 0)
            with g_.Fori(0, G // 2 - 1) as it:
                for p in range(2):
                    attend(it * 2 + (p + 1), 1 - p)
                    residual(it * 2 + p, p)
            attend(G - 1, 1)
            residual(G - 2, 0)
            residual(G - 1, 1)
            with g_.Fori(0, B // 4) as it:
                for k in range(4):
                    b = it * 4 + k
                    gh_ready.wait(g_, b + 1)
                    y_made.wait(g_, b - 1)
                    g_.tensor_tensor(hl[:, k % 2, :], h32[:, k % 2, :], hh[:, k % 2, :],
                                     ALU.subtract).then_inc(gl_ready.sem, 1)
            with g_.Fori(0, G // 2) as it:
                for p in range(2):
                    g = it * 2 + p
                    y_saved.wait(g_, g * T + T)
                    g_.tensor_tensor(tile(X, g, 1, GW).rearrange("p (t d) -> p t d", t=T),
                                     tile(X, g, 1, GW).rearrange("p (t d) -> p t d", t=T),
                                     bet[:, :].unsqueeze(1).broadcast_to([128, T, D]),
                                     ALU.add).then_inc(xb_ready.sem, 1)

        @block.scalar
        def _(act):
            own = Chain(act, scl)
            act.wait_ge(weights_loaded, WEIGHTS)
            act.wait_ge(ident_made, 1)
            own(act.activation(ident16[:, :], ident[:, :], ACT.Copy))
            act.wait_ge(prep_pe, 1)
            own(act.activation(cols[:, 0:B + 2 * E], bank(6)[:, 0:B + 2 * E], ACT.Copy))
            own(act.activation(router_h[:, :], cols[:, B:B + E], ACT.Copy, scale=WS))
            own(act.activation(w1h[:, :], w1raw, ACT.Copy, scale=WS))
            own(act.activation(w2h[:, :], w2raw, ACT.Copy, scale=WS))
            own(act.activation(m1h[:, :], m1raw, ACT.Copy, scale=WS))
            own(act.activation(m2h[:, :], m2raw, ACT.Copy, scale=WS))
            own(act.activation(b2w[0:E, :], b2raw[0:E, :], ACT.Copy, scale=WS))
            own(act.activation(b2w[32:32 + E, :], b2raw[32:32 + E, :], ACT.Copy, scale=WS))
            own(act.activation(b2t[64:64 + E, :], b2raw[64:64 + E, :], ACT.Copy, scale=WS))
            own(act.activation(mb1[0:1, :], mb1raw[0:1, :], ACT.Copy, scale=WS))
            own(act.activation(m2l[32:33, 0:E * F], mb1raw[32:33, :], ACT.Copy, scale=WS))
            own(act.activation(wTh[:, :], bank(6)[:, 128:256], ACT.Copy, scale=WS))
            own(act.activation(v12[:, :], bank(6)[:, 256:258], ACT.Copy, scale=WS))
            own(act.activation(v1h[:, :], v12[:, 0:1].broadcast_to([128, 128]), ACT.Copy))
            own(act.activation(v2h[:, :], v12[:, 1:2], ACT.Copy))
            act.activation(att_const[:, :], bank(6)[:, 258:259], ACT.Identity, bias=attb[:, :]).then_inc(prep_hi, 1)

            with act.Fori(0, G // 2) as it:
                for p in range(2):
                    g = it * 2 + p
                    adj_turned.wait(act, g + 1)
                    act.activation(tile(adjT, g, 1, GW), bank(p), ACT.Copy).then_inc(adjT_saved.sem, 1)

            def sqrt(k):
                act.wait_ge(moments, k)
                act.activation(ln_a[:, :], ln_c[:, :], ACT.Sqrt, bias=epst[:, :]).then_inc(sqrt_done, 1)

            def norm(dst, g, ready, rows=range(T)):
                for j in rows:
                    ins = act.activation(dst[:, j * D:(j + 1) * D], X[:, bass.ds(g * GW + j * D, D)], ACT.Identity,
                                         bias=nmr[:, bass.ds(g * T + j, 1)], scale=rstd[:, bass.ds(g * T + j, 1)])
                ins.then_inc(ready.sem, 1)

            sqrt(1)
            with act.Fori(0, G // 2) as it:
                for p in range(2):
                    g = it * 2 + p
                    z_made.wait(act, g + 1)
                    act.activation(ZT[:, p, :], bank(2 + p), ACT.Copy).then_inc(z_saved.sem, 1)
            sqrt(2)
            act.wait_ge(ln_ready, 2)

            def n2_norm(g, p):
                n2l_saved.wait(act, g - 1)
                n2_added.wait(act, g - 1)
                norm(XN[:, p, :], g, n2_ready)

            def n2_high(g, p):
                n2_turned.wait(act, g + 1)
                act.activation(tile(XTh, g, 1, GW), bank(p), ACT.Copy).then_inc(n2h_saved.sem, 1)

            n2_norm(0, 0)
            with act.Fori(0, G // 2 - 1) as it:
                for p in range(2):
                    n2_norm(it * 2 + (p + 1), 1 - p)
                    n2_high(it * 2 + p, p)
            n2_norm(G - 1, 1)
            n2_high(G - 2, 0)
            n2_high(G - 1, 1)

            act.wait_ge(exp_in, 1)
            act.activation(lg[3][:, :], lg[3][:, :], ACT.Exp).then_inc(exp_out, 1)

            def gelu(n, k):
                up_made.wait(act, n + 1)
                hc_ready.wait(act, n - 1)
                act.activation(h32[:, k % 2, :], bank(k % 2), ACT.Gelu, bias=cols[:, B + E + k % E:B + E + k % E + 1],
                               scale=1.0 / WS).then_inc(gelu_done.sem, 1)

            def high(n, k):
                hc_ready.wait(act, n + 1)
                down_made.wait(act, n - 3)
                act.activation(hh[:, k % 4, :], hc32[:, k % 2, :], ACT.Copy).then_inc(hh_ready.sem, 1)

            gelu(0, 0)
            with act.Fori(0, G - 1) as it:
                for k in range(E):
                    gelu(it * E + (k + 1), (k + 1) % E)
                    high(it * E + k, k)
            for k in range(E):
                if k < E - 1:
                    gelu((G - 1) * E + k + 1, k + 1)
                high((G - 1) * E + k, k)

            sqrt(3)
            act.wait_ge(ln_ready, 3)

            def n3_norm(g, p):
                n3_turned.wait(act, g - 1)
                norm(XN[:, p, :], g, n3_ready)

            def n3_high(g, p):
                n3_turned.wait(act, g + 1)
                proj_made.wait(act, g - 1) if not isinstance(g, int) or g >= 2 else None
                act.activation(hh[:, p, :], bank(p), ACT.Copy).then_inc(n3h_saved.sem, 1)

            def sigmoid(g, p):
                s2_saved.wait(act, g + 1)
                att_ready.wait(act, g - 1)
                for j in range(T):
                    ins = act.activation(sig[:, p, j * N:(j + 1) * N], bank(2)[:, j * N:(j + 1) * N], ACT.Sigmoid,
                                         bias=s2c[:, p, j:j + 1], scale=1.0 / WS)
                ins.then_inc(sig_ready.sem, 1)

            n3_norm(0, 0)
            n3_high(0, 0)
            n3_norm(1, 1)
            sigmoid(0, 0)
            n3_high(1, 1)
            with act.Fori(0, G // 2 - 1) as it:
                for p in range(2):
                    g = it * 2 + p
                    n3_norm(g + 2, p)
                    sigmoid(g + 1, 1 - p)
                    n3_high(g + 2, p)
            sigmoid(G - 1, 1)

            sqrt(4)
            act.wait_ge(ln_ready, 4)

            def n4_norm(g, p):
                n4l_saved.wait(act, g - 1)
                norm(XN[:, p, :], g, n4_ready)

            def n4_high(g, p):
                n4_turned.wait(act, g + 1)
                act.activation(tile(XTh, g, 1, GW), bank(6 + p), ACT.Copy).then_inc(n4h_saved.sem, 1)

            n4_norm(0, 0)
            with act.Fori(0, G // 2 - 1) as it:
                for p in range(2):
                    n4_norm(it * 2 + (p + 1), 1 - p)
                    n4_high(it * 2 + p, p)
            n4_norm(G - 1, 1)
            n4_high(G - 2, 0)
            n4_high(G - 1, 1)

            act.wait_ge(route_dve, 2)
            act.activation(r[1][:, :], r[1][:, :], ACT.Exp).then_inc(route_act, 1)
            act.wait_ge(route_dve, 4)
            act.activation(r[1][:, :], r[1][:, :], ACT.Exp).then_inc(route_act, 1)
            act.wait_ge(route_dve, 5)
            act.activation(rc[5][:, :], rc[5][:, :], ACT.Exp).then_inc(route_act, 1)

            def gelu2(b, k):
                f_made.wait(act, b + 1)
                gl_ready.wait(act, b - 1)
                act.activation(h32[:, k % 2, :], bank(k % 2), ACT.Gelu, scale=1.0 / WS).then_inc(g_ready.sem, 1)

            def high2(b, k):
                g_ready.wait(act, b + 1)
                y_made.wait(act, b - 1)
                act.activation(hh[:, k % 2, :], h32[:, k % 2, :], ACT.Copy).then_inc(gh_ready.sem, 1)

            with act.Fori(0, B // 4) as it:
                for k in range(4):
                    gelu2(it * 4 + k, k)
                    high2(it * 4 + k, k)
            sqrt(5)
            act.wait_ge(ln_ready, 5)
            with act.Fori(0, G // 2) as it:
                for p in range(2):
                    g = it * 2 + p
                    for j in range(T):
                        ins = act.activation(adjT[:, bass.ds(g * GW + j * D, D)], adjT[:, bass.ds(g * GW + j * D, D)],
                                             ACT.Identity, bias=nmr[:, bass.ds(g * T + j, 1)],
                                             scale=rstd[:, bass.ds(g * T + j, 1)])
                    ins.then_inc(norm_ready.sem, 1)

        @block.vector
        def _(dve):
            own = Chain(dve, vec)
            dve.wait_ge(weights_loaded, WEIGHTS)
            dve.wait_ge(ident_made, 1)
            dve.wait_ge(prep_hi, 1)

            def low(dst, src, high_part):
                own(dve.scalar_tensor_tensor(dst, src, WS, high_part, ALU.mult, ALU.subtract))

            low(router_l[:, :], cols[:, B:B + E], router_h[:, :])
            low(w1l[:, :], w1raw, w1h[:, :])
            low(w2l[:, :], w2raw, w2h[:, :])
            low(m1l[:, :], m1raw, m1h[:, :])
            low(mb1[32:33, :], mb1raw[32:33, :], m2l[32:33, 0:E * F])
            own(dve.tensor_copy(selector[:, :, :], ident[:, 0:E].unsqueeze(2).broadcast_to([128, E, 128])))
            own(dve.tensor_tensor(selector[:, :, :], selector[:, :, :],
                                  ident[:, 32:32 + E].unsqueeze(2).broadcast_to([128, E, 128]), ALU.add))
            dve.sem_inc(prep_done, 1)
            low(m2l[:, :], m2raw, m2h[:, :])
            low(b2w[64:64 + E, :], b2raw[64:64 + E, :], b2t[64:64 + E, :])
            low(wTl[:, :], bank(6)[:, 128:256], wTh[:, :])
            own(dve.tensor_tensor(v1l[:, :], v12[:, 0:1].broadcast_to([128, 128]), v1h[:, :], ALU.subtract))
            own(dve.tensor_tensor(v2l[:, :], v12[:, 1:2], v2h[:, :], ALU.subtract))
            dve.wait_ge(weights_loaded, WEIGHTS + 32)
            own(dve.tensor_scalar(mb2[0:1, :], mb1raw[0:1, 0:E * D], WS, None, ALU.mult))
            own(dve.tensor_scalar(XTh[32:33, 0:E * D], mb1raw[32:33, 0:E * D], WS, None, ALU.mult))
            low(mb2[32:33, :], mb1raw[32:33, 0:E * D], XTh[32:33, 0:E * D])

            def finish_stats(k, scale_rows=None):
                me, qe, mo, qo = (stats[:, :, i] for i in (1, 2, 4, 5))
                own(dve.tensor_tensor(ln_b[:, :], me, mo, ALU.subtract))
                own(dve.tensor_tensor(ln_c[:, :], qe, qo, ALU.add))
                own(dve.scalar_tensor_tensor(ln_b[:, :], ln_b[:, :], 0.25, ln_b[:, :], ALU.mult, ALU.mult))
                own(dve.scalar_tensor_tensor(ln_c[:, :], ln_c[:, :], 1.0 / D, ln_b[:, :], ALU.mult, ALU.add))
                dve.sem_inc(moments, 1)
                own(dve.tensor_tensor(ln_b[:, :], me, mo, ALU.add))
                dve.wait_ge(sqrt_done, k)
                own(dve.reciprocal(rstd[:, :], ln_a[:, :]))
                own(dve.scalar_tensor_tensor(nmr[:, :], ln_b[:, :], -0.5, rstd[:, :], ALU.mult, ALU.mult))
                dve.sem_inc(ln_ready, 1)

            def group_stats(g, src=X, done=None):
                for j in range(T):
                    ins = dve.bn_stats(stats[:, bass.ds(g * T + j, 1), :], src[:, bass.ds(g * GW + j * D, D)])
                return ins

            own_stats = sem("group_stats")
            done_stats = 0
            with dve.Fori(0, G // 4) as it:
                for q in range(4):
                    dve.wait_ge(group_loaded[q], 32 * (it + 1))
                    group_stats(it * 4 + q).then_inc(own_stats, 1)
            done_stats += G
            dve.wait_ge(own_stats, done_stats)
            finish_stats(1)

            def n1_norm(g, p):
                z_made.wait(dve, g - 1)
                for j in range(T):
                    ins = dve.tensor_scalar(XN[:, p, j * D:(j + 1) * D], X[:, bass.ds(g * GW + j * D, D)],
                                            rstd[:, bass.ds(g * T + j, 1)], nmr[:, bass.ds(g * T + j, 1)],
                                            ALU.mult, ALU.add)
                ins.then_inc(xn_ready.sem, 1)

            def n1_add(g, p):
                o_made.wait(dve, g + 1)
                bias_added.wait(dve, g + 1)
                dve.tensor_tensor(tile(X, g, 1, GW), bank(4 + p), tile(X, g, 1, GW), ALU.add).then_inc(x1_saved.sem, 1)

            def n1_stats(g):
                x1_saved.wait(dve, g + 1)
                group_stats(g).then_inc(own_stats, 1)

            n1_norm(0, 0)
            with dve.Fori(0, G // 2 - 1) as it:
                for p in range(2):
                    n1_norm(it * 2 + (p + 1), 1 - p)
                    n1_add(it * 2 + p, p)
                    n1_stats(it * 2 + p)
            n1_norm(G - 1, 1)
            for g in (G - 2, G - 1):
                n1_add(g, g % 2)
                n1_stats(g)
            done_stats += G
            dve.wait_ge(own_stats, done_stats)
            finish_stats(2)

            with dve.Fori(0, G // 2) as it:
                for p in range(2):
                    g = it * 2 + p
                    n2h_saved.wait(dve, g + 1)
                    dve.tensor_tensor(tile(XTl, g, 1, GW), bank(p), tile(XTh, g, 1, GW),
                                      ALU.subtract).then_inc(n2l_saved.sem, 1)

            dve.wait_ge(logits_made, 1)

            def v3(t):
                return t[:, :].rearrange("p (b e) -> p b e", e=E)

            def wide(t):
                return t[:, :].unsqueeze(2).broadcast_to([128, B, E])
            L, O, K, M = lg
            m1, m2, kk = small
            rank3 = rank[:, :].unsqueeze(1).broadcast_to([128, B, E])
            own(dve.tensor_scalar(L[:, :], bank(7), 1.0 / WS, None, ALU.mult))
            own(dve.tensor_reduce(m1[:, :], v3(L), AX.X, ALU.max))
            own(dve.tensor_tensor(v3(M), v3(L), wide(m1), ALU.subtract))
            dve.sem_inc(exp_in, 1)
            own(dve.tensor_tensor(v3(K), v3(L), wide(m1), ALU.is_equal))
            own(dve.tensor_tensor(v3(K), v3(K), rank3, ALU.mult))
            own(dve.tensor_reduce(kk[:, :], v3(K), AX.X, ALU.max))
            own(dve.tensor_tensor(v3(O), v3(K), wide(kk), ALU.is_equal))
            own(dve.scalar_tensor_tensor(L[:, :], O[:, :], BIG, L[:, :], ALU.mult, ALU.add))
            own(dve.tensor_reduce(m2[:, :], v3(L), AX.X, ALU.max))
            own(dve.tensor_tensor(v3(K), v3(L), wide(m2), ALU.is_equal))
            own(dve.tensor_tensor(v3(K), v3(K), rank3, ALU.mult))
            own(dve.tensor_reduce(kk[:, :], v3(K), AX.X, ALU.max))
            own(dve.tensor_tensor(v3(K), v3(K), wide(kk), ALU.is_equal))
            own(dve.tensor_tensor(O[:, :], O[:, :], K[:, :], ALU.add))
            dve.wait_ge(exp_out, 1)
            own(dve.tensor_tensor(O[:, :], O[:, :], M[:, :], ALU.mult))
            own(dve.tensor_reduce(m1[:, :], v3(O), AX.X, ALU.add))
            own(dve.reciprocal(m1[:, :], m1[:, :]))
            own(dve.tensor_tensor(v3(O), v3(O), wide(m1), ALU.mult))

            def gates(g, p):
                c_turned.wait(dve, g - 1)
                src = O[:, bass.ds(g * T * E, T * E)].rearrange("p (t e) -> p t e", e=E)
                own_g(dve.tensor_scalar(cpad[:, p, :, 0:E], src, 1.0, None, ALU.mult))
                own_g(dve.tensor_scalar(cpad[:, p, :, 64:64 + E], src, 1.0, None, ALU.mult))
                dve.tensor_tensor(cpad[:, p, :, 32:32 + E], src, cpad[:, p, :, 0:E],
                                  ALU.subtract).then_inc(cpad_ready.sem, 1)

            def gates_copy(g, p):
                c_turned.wait(dve, g + 1)
                if not (isinstance(g, int) and g < 2):
                    down_made.wait(dve, g * E - E)
                dve.tensor_copy(cT[:, p, :], bank(6).bitcast(fp16)[:, 0:GW]).then_inc(c_saved.sem, 1)

            def gate_hidden(n, k):
                gelu_done.wait(dve, n + 1)
                cb_made.wait(dve, n + 1)
                hl_ready.wait(dve, n - 1)
                dve.tensor_tensor(hc32[:, k % 2, :], bank(2 + k % 2), h32[:, k % 2, :],
                                  ALU.mult).then_inc(hc_ready.sem, 1)

            def ffn_add(g, p):
                moe_made.wait(dve, g + 1)
                dve.scalar_tensor_tensor(tile(X, g, 1, GW), bank(4 + p), 1.0 / WS, tile(X, g, 1, GW),
                                         ALU.mult, ALU.add).then_inc(x2_saved.sem, 1)

            def ffn_stats(g):
                x2_saved.wait(dve, g + 1)
                group_stats(g).then_inc(own_stats, 1)

            gate_own = sem("gate_own")
            own_g = Chain(dve, gate_own)
            gates(0, 0)
            gates_copy(0, 0)
            gates(1, 1)
            for k in range(E):
                if k == 4:
                    gates_copy(1, 1)
                gate_hidden(k, k)
            base = own_g.n
            with dve.Fori(0, G // 2 - 1) as it:
                for q in range(2):
                    g = it * 2 + (q + 1)
                    p = (q + 1) % 2
                    own_g = Chain(dve, gate_own, it * 4 + (base + 2 * q))
                    gates(g + 1, 1 - p)
                    for k in range(E):
                        gate_hidden(g * E + k, k)
                        if k == 3:
                            gates_copy(g + 1, 1 - p)
                        if k == 4:
                            ffn_add(g - 1, 1 - p)
                            ffn_stats(g - 1)
            for k in range(E):
                gate_hidden((G - 1) * E + k, k)
                if k == 4:
                    ffn_add(G - 2, 0)
                    ffn_stats(G - 2)
            ffn_add(G - 1, 1)
            ffn_stats(G - 1)
            done_stats += G
            dve.wait_ge(own_stats, done_stats)
            finish_stats(3)

            frac_own = sem("frac_own")

            def n3_low(g, p):
                n3h_saved.wait(dve, g + 1)
                dve.tensor_tensor(hl[:, p, :], bank(p), hh[:, p, :], ALU.subtract).then_inc(n3l_saved.sem, 1)

            def project(g, p):
                proj_made.wait(dve, g + 1)
                sig_ready.wait(dve, g - 1)
                dve.tensor_scalar(s2c[:, p, :], bank(4)[:, 0:T], 1.0 / WS, att_const[:, 0:1], ALU.mult,
                                  ALU.add).then_inc(s2_saved.sem, 1)
                att_used.wait(dve, g - 1)
                dve.scalar_tensor_tensor(H[:, p, :].rearrange("p (t d) -> p t d", t=T),
                                         bank(3).rearrange("p (t d) -> p t d", t=T), 1.0 / WS,
                                         g1b[:, :].unsqueeze(1).broadcast_to([128, T, D]),
                                         ALU.mult, ALU.add).then_inc(h_saved.sem, 1)

            def attended(g, p, chain):
                att_used.wait(dve, g + 1)
                mask = cols[:, bass.ds(g * T, T)]
                f = [frac[:, p, i * T:(i + 1) * T] for i in range(3)]
                chain(dve.tensor_tensor(f[0], bank(4)[:, 8:8 + T], mask, ALU.mult))
                chain(dve.tensor_scalar(f[0], f[0], 1e-8, None, ALU.add))
                chain(dve.reciprocal(f[1], f[0]))
                chain(dve.tensor_tensor(f[2], mask, mask, ALU.mult))
                chain(dve.tensor_tensor(f[2], f[2], f[1], ALU.mult))
                x3_ready.wait(dve, g - 1)
                dve.tensor_tensor(U[:, p, :].rearrange("p (t d) -> p t d", t=T),
                                  bank(5).rearrange("p (t d) -> p t d", t=T),
                                  f[2].unsqueeze(2).broadcast_to([128, T, D]), ALU.mult).then_inc(u_saved.sem, 1)

            def x3_stats(g):
                x3_ready.wait(dve, g + 1)
                group_stats(g).then_inc(own_stats, 1)

            FR = 5
            n3_low(0, 0)
            project(0, 0)
            n3_low(1, 1)
            attended(0, 0, Chain(dve, frac_own))
            project(1, 1)
            n3_low(2, 0)
            with dve.Fori(0, G // 2 - 2) as it:
                for q in range(2):
                    g = it * 2 + (q + 1)
                    p = (q + 1) % 2
                    attended(g, p, Chain(dve, frac_own, it * 2 * FR + (q + 1) * FR))
                    project(g + 1, 1 - p)
                    n3_low(g + 2, p)
                    x3_stats(g - 1)
            attended(G - 3, 1, Chain(dve, frac_own, (G - 3) * FR))
            project(G - 2, 0)
            n3_low(G - 1, 1)
            x3_stats(G - 4)
            attended(G - 2, 0, Chain(dve, frac_own, (G - 2) * FR))
            project(G - 1, 1)
            x3_stats(G - 3)
            attended(G - 1, 1, Chain(dve, frac_own, (G - 1) * FR))
            x3_stats(G - 2)
            x3_stats(G - 1)
            done_stats += G
            dve.wait_ge(own_stats, done_stats)
            finish_stats(4)

            with dve.Fori(0, G // 2) as it:
                for p in range(2):
                    g = it * 2 + p
                    n4_ready.wait(dve, g + 1)
                    dve.tensor_scalar(tile(adjT, g, 1, GW), XN[:, p, :], 1.0, None, ALU.mult)
                    n4h_saved.wait(dve, g + 1)
                    dve.tensor_reduce(xsum[:, bass.ds(g * T, T)], bank(6 + p).rearrange("p (t n) -> p t n", t=T),
                                      AX.X, ALU.add)
                    dve.tensor_tensor(tile(XTl, g, 1, GW), bank(6 + p), tile(XTh, g, 1, GW),
                                      ALU.subtract).then_inc(n4l_saved.sem, 1)

            dve.wait_ge(route_pe, 1)

            def row(t, n=E):
                return t[:, 0:1].broadcast_to([B, n])
            own(dve.scalar_tensor_tensor(r[0][:, :], bank(2)[0:B, 0:E], 1.0 / N, br[:, :], ALU.mult, ALU.add))
            own(dve.tensor_reduce(rc[0][:, :], r[0][:, :], AX.X, ALU.max))
            own(dve.tensor_tensor(r[1][:, :], r[0][:, :], row(rc[0]), ALU.subtract))
            dve.sem_inc(route_dve, 2)
            dve.wait_ge(route_act, 1)
            own(dve.tensor_reduce(rc[1][:, :], r[1][:, :], AX.X, ALU.add))
            own(dve.reciprocal(rc[1][:, :], rc[1][:, :]))
            own(dve.tensor_tensor(r[2][:, :], r[1][:, :], row(rc[1]), ALU.mult))
            dve.sem_inc(route_dve, 1)
            dve.wait_ge(route_pe, 2)
            own(dve.tensor_scalar(r[3][:, :], bank(3)[0:B, 0:E], float(N), CAPACITY, ALU.mult, ALU.max))
            own(dve.reciprocal(r[4][:, :], r[3][:, :]))
            own(dve.tensor_scalar(r[4][:, :], r[4][:, :], CAPACITY, None, ALU.mult))
            own(dve.tensor_scalar(r[3][:, :], r[3][:, :], CAPACITY, None, ALU.is_gt))
            own(dve.tensor_scalar(r[4][:, :], r[4][:, :], -1.0, None, ALU.add))
            own(dve.tensor_tensor(r[4][:, :], r[4][:, :], r[3][:, :], ALU.mult))
            own(dve.tensor_scalar(r[4][:, :], r[4][:, :], 1.0, None, ALU.add))
            own(dve.tensor_tensor(r[0][:, :], r[2][:, :], r[4][:, :], ALU.mult))
            own(dve.tensor_reduce(rc[0][:, :], r[0][:, :], AX.X, ALU.max))
            own(dve.tensor_tensor(r[1][:, :], r[0][:, :], row(rc[0]), ALU.subtract))
            dve.sem_inc(route_dve, 1)
            dve.wait_ge(route_act, 2)
            own(dve.tensor_reduce(rc[1][:, :], r[1][:, :], AX.X, ALU.add))
            own(dve.reciprocal(rc[1][:, :], rc[1][:, :]))
            own(dve.tensor_tensor(r[0][:, :], r[1][:, :], row(rc[1]), ALU.mult))
            for i, (m, k) in enumerate(((rc[0], rc[2]), (rc[1], rc[3]))):
                own(dve.tensor_reduce(m[:, :], r[0][:, :], AX.X, ALU.max))
                own(dve.tensor_tensor(r[2][:, :], r[0][:, :], row(m), ALU.is_equal))
                own(dve.tensor_tensor(r[2][:, :], r[2][:, :], rank[0:B, :], ALU.mult))
                own(dve.tensor_reduce(k[:, :], r[2][:, :], AX.X, ALU.max))
                if i == 0:
                    own(dve.tensor_tensor(r[2][:, :], r[2][:, :], row(k), ALU.is_equal))
                    own(dve.scalar_tensor_tensor(r[0][:, :], r[2][:, :], BIG, r[0][:, :], ALU.mult, ALU.add))
            own(dve.tensor_tensor(rc[5][:, :], rc[1][:, :], rc[0][:, :], ALU.subtract))
            dve.sem_inc(route_dve, 1)
            dve.wait_ge(route_act, 3)
            own(dve.tensor_scalar(rc[6][:, :], rc[5][:, :], 1.0, None, ALU.add))
            own(dve.reciprocal(rc[6][:, :], rc[6][:, :]))
            own(dve.tensor_tensor(rc[7][:, :], rc[5][:, :], rc[6][:, :], ALU.mult))
            own(dve.tensor_scalar(rc[2][:, :], rc[2][:, :], -1.0, float(E), ALU.mult, ALU.add))
            own(dve.tensor_scalar(rc[3][:, :], rc[3][:, :], -1.0, float(E), ALU.mult, ALU.add))
            for i, c in enumerate((rc[6], rc[7], rc[2], rc[3])):
                own(dve.tensor_scalar(diag[:, i, :], ident[0:B, 0:B], c[:, 0:1], None, ALU.mult))
            dve.sem_inc(route_dve, 1)
            dve.wait_ge(route_pe, 3)
            own(dve.tensor_copy(gate[:, :, :], bank(2)[:, 0:4 * B].rearrange("p (i b) -> p i b", i=4)))
            own(dve.tensor_copy(index[:, :].rearrange("p (b k) -> p k b", k=2), gate[:, 2:4, :]))
            own(dve.tensor_scalar(gate[:, 0:2, :], gate[:, 0:2, :], 1.0 / WS, None, ALU.mult))
            dve.sem_inc(route_ready, 1)

            z_own = sem("z_own")
            with dve.Fori(0, B // 4) as it:
                for k in range(4):
                    b = it * 4 + k
                    y_made.wait(dve, b + 1)
                    dve.scalar_tensor_tensor(tile(adjT, b), bank(2 + k % 2)[:, 0:D], gate[:, 0, bass.ds(b, 1)],
                                             tile(adjT, b), ALU.mult, ALU.add).then_inc(z_own, 1)
                    dve.wait_ge(z_own, b * 2 + 1)
                    dve.scalar_tensor_tensor(tile(adjT, b), bank(2 + k % 2)[:, D:2 * D], gate[:, 1, bass.ds(b, 1)],
                                             tile(adjT, b), ALU.mult, ALU.add).then_inc(y_saved.sem, 1)
                    y_saved.wait(dve, b + 1)
                    dve.bn_stats(stats[:, bass.ds(b, 1), :], tile(adjT, b)).then_inc(z_own, 1)
            dve.wait_ge(z_own, 2 * B)
            finish_stats(5)
            with dve.Fori(0, G // 2) as it:
                for p in range(2):
                    g = it * 2 + p
                    norm_ready.wait(dve, g + 1)
                    dve.tensor_tensor(tile(adjT, g, 1, GW).rearrange("p (t d) -> p t d", t=T),
                                      tile(adjT, g, 1, GW).rearrange("p (t d) -> p t d", t=T),
                                      gam[:, :].unsqueeze(1).broadcast_to([128, T, D]), ALU.mult).then_inc(z_own, 1)
                    xb_ready.wait(dve, g + 1)
                    dve.wait_ge(z_own, g + (2 * B + 1))
                    dve.tensor_tensor(tile(X, g, 1, GW), tile(adjT, g, 1, GW), tile(X, g, 1, GW),
                                      ALU.add).then_inc(out_ready.sem, 1)

        @block.tensor
        def _(pe):
            def product(dst, parts, **kw):
                for i, (a, c) in enumerate(parts):
                    ins = pe.matmul(dst, a, c, start=(i == 0), stop=(i == len(parts) - 1))
                return ins

            pe.wait_ge(weights_loaded, WEIGHTS)
            pe.wait_ge(ident_made, 1)
            pe.transpose(bank(6)[:, 0:B + 2 * E], rows_in[0:B + 2 * E, :], ident[0:B + 2 * E, 0:B + 2 * E])
            pe.transpose(bank(6)[:, 128:256], g1w[:, :], ident[:, :])
            pe.matmul(bank(6)[:, 256:258], g1w[:, :], avec[:, 0:2], start=True, stop=True)
            pe.matmul(bank(6)[:, 258:259], avec[:, 2:3].broadcast_to([128, 128]), avec[:, 0:1], start=True, stop=False)
            pe.matmul(bank(6)[:, 258:259], avec[:, 2:3].broadcast_to([128, 128]), avec[:, 1:2], start=False,
                      stop=True).then_inc(prep_pe, 1)

            with pe.Fori(0, G // 4) as it:
                for q in range(4):
                    pe.wait_ge(group_loaded[q], 32 * (it + 1))
                    adjT_saved.wait(pe, it * 4 + (q - 1))
                    for j in range(T):
                        ins = pe.transpose(bank(q % 2)[:, j * N:(j + 1) * N], adj_in[:, q, j * N:(j + 1) * N], ident[:, :])
                    ins.then_inc(adj_turned.sem, 1)
            adjT_saved.wait(pe, G)

            def g0_z(g, p):
                xn_ready.wait(pe, g + 1)
                z_saved.wait(pe, g - 1)
                for j in range(T):
                    ins = pe.matmul(bank(2 + p)[:, j * N:(j + 1) * N], XN[:, p, j * D:(j + 1) * D],
                                    adjT[:, bass.ds(g * GW + j * N, N)], start=True, stop=True)
                ins.then_inc(z_made.sem, 1)

            def g0_out(g, p):
                z_saved.wait(pe, g + 1)
                x1_saved.wait(pe, g - 1)
                for j in range(T):
                    ins = pe.matmul(bank(4 + p)[:, j * D:(j + 1) * D], ZT[:, p, j * N:(j + 1) * N], g0w[:, :],
                                    start=True, stop=True)
                ins.then_inc(o_made.sem, 1)

            g0_z(0, 0)
            with pe.Fori(0, G // 2 - 1) as it:
                for p in range(2):
                    g0_z(it * 2 + (p + 1), 1 - p)
                    g0_out(it * 2 + p, p)
            g0_z(G - 1, 1)
            g0_out(G - 2, 0)
            g0_out(G - 1, 1)

            pe.wait_ge(prep_done, 1)

            def n2_turn(g, p):
                n2_ready.wait(pe, g + 1)
                n2l_saved.wait(pe, g - 1)
                for j in range(T):
                    ins = pe.transpose(bank(p)[:, j * N:(j + 1) * N], XN[:, p, j * D:(j + 1) * D], ident[:, :])
                ins.then_inc(n2_turned.sem, 1)

            def route(g, p):
                n2l_saved.wait(pe, g + 1)
                for j in range(T):
                    xh, xl = (tile(t, g * T + j) for t in (XTh, XTl))
                    ins = product(bank(7)[:, bass.ds(g * T * E + j * E, E)],
                                  [(xh, router_h[:, :]), (xh, router_l[:, :]), (xl, router_h[:, :])])
                return ins

            n2_turn(0, 0)
            with pe.Fori(0, G // 2 - 1) as it:
                for p in range(2):
                    n2_turn(it * 2 + (p + 1), 1 - p)
                    route(it * 2 + p, p)
            n2_turn(G - 1, 1)
            route(G - 2, 0)
            route(G - 1, 1).then_inc(logits_made, 1)

            def turn_gates(g, p):
                cpad_ready.wait(pe, g + 1)
                if not (isinstance(g, int) and g < 1):
                    c_saved.wait(pe, g)
                for j in range(T):
                    ins = pe.transpose(bank(6).bitcast(fp16)[:, j * N:(j + 1) * N], cpad[:, p, j, :], ident16[:, :])
                ins.then_inc(c_turned.sem, 1)

            def up(g, k):
                n = g * E + k
                gelu_done.wait(pe, n - 1)
                e = k % E
                w = slice(e * D, (e + 1) * D)
                xh, xl = (tile(t, g, 1, GW) for t in (XTh, XTl))
                product(bank(k % 2), [(w1h[:, w], xh), (w1l[:, w], xh), (w1h[:, w], xl)]).then_inc(up_made.sem, 1)

            def spread(g, k, p):
                n = g * E + k
                hc_ready.wait(pe, n - 1)
                if k == 0:
                    c_saved.wait(pe, g + 1)
                pe.matmul(bank(2 + k % 2), selector[:, k, :], cT[:, p, :], start=True, stop=True).then_inc(cb_made.sem, 1)

            def down(g, k, p):
                n = g * E + k
                hl_ready.wait(pe, n + 1)
                if k == 0:
                    x2_saved.wait(pe, g - 1)
                w = slice(k * D, (k + 1) * D)
                for j in range(T):
                    s = slice(j * N, (j + 1) * N)
                    o = bank(4 + p)[:, s]
                    for i, (a, c) in enumerate(((hh, w2h), (hh, w2l), (hl, w2h))):
                        ins = pe.matmul(o, a[:, k % 4, s], c[:, w], start=(k == 0 and j == 0 and i == 0),
                                        stop=False, skip_group_check=True)
                ins.then_inc(down_made.sem, 1)
                if k == E - 1:
                    for j in range(T):
                        s = slice(j * N, (j + 1) * N)
                        ins = pe.matmul(bank(4 + p)[:, s], cT[:, p, s], b2w[:, :], start=False, stop=(j == T - 1),
                                        skip_group_check=True)
                    ins.then_inc(moe_made.sem, 1)

            LAG = 3

            def first_step(g, k, p, last=False):
                up(g, k)
                spread(g, k, p)
                if k == 1 and not last:
                    turn_gates(g + 1, 1 - p)

            turn_gates(0, 0)
            for k in range(E):
                first_step(0, k, 0)
                if k >= LAG:
                    down(0, k - LAG, 0)
            with pe.Fori(0, G // 2 - 1) as it:
                for q in range(2):
                    g = it * 2 + (q + 1)
                    p = (q + 1) % 2
                    for k in range(E):
                        first_step(g, k, p)
                        if k >= LAG:
                            down(g, k - LAG, p)
                        else:
                            down(g - 1, E + k - LAG, 1 - p)
            for k in range(E):
                first_step(G - 1, k, 1, last=True)
                if k >= LAG:
                    down(G - 1, k - LAG, 1)
                else:
                    down(G - 2, E + k - LAG, 0)
            for k in range(E - LAG, E):
                down(G - 1, k, 1)

            def n3_turn(g, p):
                n3_ready.wait(pe, g + 1)
                if not (isinstance(g, int) and g < 2):
                    n3l_saved.wait(pe, g - 1)
                for j in range(T):
                    ins = pe.transpose(bank(p)[:, j * N:(j + 1) * N], XN[:, p, j * D:(j + 1) * D], ident[:, :])
                ins.then_inc(n3_turned.sem, 1)

            def g1_project(g, p):
                n3l_saved.wait(pe, g + 1)
                h_saved.wait(pe, g)
                if not (isinstance(g, int) and g < 1):
                    sig_ready.wait(pe, g)
                th, tl = hh[:, p, :], hl[:, p, :]
                product(bank(2), [(v1h[:, :], th), (v1l[:, :], th), (v1h[:, :], tl)])
                for j in range(T):
                    s = slice(j * N, (j + 1) * N)
                    product(bank(3)[:, s], [(th[:, s], wTh[:, :]), (th[:, s], wTl[:, :]), (tl[:, s], wTh[:, :])])
                if not (isinstance(g, int) and g < 1):
                    u_saved.wait(pe, g)
                for j in range(T):
                    s = slice(j * N, (j + 1) * N)
                    ins = product(bank(4)[:, j:j + 1], [(th[:, s], v2h[:, :]), (th[:, s], v2l[:, :]), (tl[:, s], v2h[:, :])])
                ins.then_inc(proj_made.sem, 1)

            def g1_attend(g, p):
                att_ready.wait(pe, g + 1)
                h_saved.wait(pe, g + 1)
                if not (isinstance(g, int) and g < 1):
                    u_saved.wait(pe, g)
                for j in range(T):
                    s = slice(j * N, (j + 1) * N)
                    pe.matmul(bank(5)[:, s], att[:, p, s], H[:, p, s], start=True, stop=True)
                    ins = pe.matmul(bank(4)[:, 8 + j:9 + j], att[:, p, s], ones[:, 0:1], start=True, stop=True)
                ins.then_inc(att_used.sem, 1)

            n3_turn(0, 0)
            g1_project(0, 0)
            n3_turn(1, 1)
            with pe.Fori(0, G // 2 - 1) as it:
                for p in range(2):
                    g = it * 2 + p
                    g1_attend(g, p)
                    g1_project(g + 1, 1 - p)
                    n3_turn(g + 2, p)
            g1_attend(G - 2, 0)
            g1_project(G - 1, 1)
            g1_attend(G - 1, 1)

            with pe.Fori(0, G // 2) as it:
                for p in range(2):
                    g = it * 2 + p
                    n4_ready.wait(pe, g + 1)
                    n4l_saved.wait(pe, g - 1)
                    for j in range(T):
                        ins = pe.transpose(bank(6 + p)[:, j * N:(j + 1) * N], XN[:, p, j * D:(j + 1) * D], ident[:, :])
                    ins.then_inc(n4_turned.sem, 1)

            n4l_saved.wait(pe, G)
            pe.matmul(bank(2)[0:B, 0:E], xsum[:, :], wr[:, :], start=True, stop=True).then_inc(route_pe, 1)
            pe.wait_ge(route_dve, 3)
            pe.matmul(bank(3)[0:B, 0:E], ones[0:B, 0:B], r[2][:, :], start=True, stop=True).then_inc(route_pe, 1)
            pe.wait_ge(route_dve, 6)
            pe.matmul(bank(2)[:, 0:4 * B], ones[0:B, :], diag[:, :, :].rearrange("p i b -> p (i b)"),
                      start=True, stop=True).then_inc(route_pe, 1)
            pe.wait_ge(route_ready, 1)

            def expert(b, i):
                return pe.value_load(index[0:1, bass.ds(b * 2 + i, 1)], min_val=0, max_val=E - 1)

            def ffn_up(b, k, es):
                g_ready.wait(pe, b - 1)
                xh, xl = tile(XTh, b), tile(XTl, b)
                for i, e in enumerate(es):
                    for h in range(HALVES):
                        s = (i * HALVES + h) * N
                        at = bass.ds(e * F + h * D, D)
                        ins = product(bank(k % 2)[:, s:s + N], [(m1h[:, at], xh), (m1l[:, at], xh), (m1h[:, at], xl),
                                                               (mb1[:, at], two_ones[:, :])])
                ins.then_inc(f_made.sem, 1)

            def ffn_down(b, k, es):
                gl_ready.wait(pe, b + 1)
                y_saved.wait(pe, b - 1)
                for i, e in enumerate(es):
                    parts = []
                    for h in range(HALVES):
                        s = slice((i * HALVES + h) * N, (i * HALVES + h + 1) * N)
                        at = bass.ds(e * F + h * D, D)
                        gh, gl = hh[:, k % 2, s], hl[:, k % 2, s]
                        parts += [(gh, m2h[:, at]), (gh, m2l[:, at]), (gl, m2h[:, at])]
                    parts.append((two_ones[:, :], mb2[:, bass.ds(e * D, D)]))
                    ins = product(bank(2 + k % 2)[:, i * D:(i + 1) * D], parts)
                ins.then_inc(y_made.sem, 1)

            ffn_up(0, 0, [expert(0, 0), expert(0, 1)])
            ffn_up(1, 1, [expert(1, 0), expert(1, 1)])
            with pe.Fori(0, B // 4 - 1) as it:
                for k in range(4):
                    b = it * 4 + k
                    ffn_down(b, k, [expert(b, 0), expert(b, 1)])
                    ffn_up(b + 2, k, [expert(b + 2, 0), expert(b + 2, 1)])
            for b in range(B - 4, B):
                ffn_down(b, b, [expert(b, 0), expert(b, 1)])
                if b + 2 < B:
                    ffn_up(b + 2, b, [expert(b + 2, 0), expert(b + 2, 1)])


_INS = ['x', 'adj', 'nodemask', 'L0_gnn_weight', 'L0_gnn_bias', 'L0_ffn_router_w', 'L0_ffn_w1', 'L0_ffn_b1',
        'L0_ffn_w2', 'L0_ffn_b2', 'L1_gnn_W', 'L1_gnn_b', 'L1_gnn_a1', 'L1_gnn_a2', 'L1_gnn_att_b', 'L1_ffn_Wr',
        'L1_ffn_br', 'L1_ffn_W1', 'L1_ffn_b1', 'L1_ffn_W2', 'L1_ffn_b2', 'L1_ffn_gamma', 'L1_ffn_beta']


def kernel(**inputs):
    import numpy as _np
    import concourse.bacc as _bacc
    from concourse import mybir as _mybir
    from concourse.bass_utils import run_bass_kernel_spmd as _run

    nc = _bacc.Bacc("TRN2", target_bir_lowering=False, num_devices=1)
    arrays, args = {}, []
    for name in _INS:
        a = _np.ascontiguousarray(inputs[name])
        if a.ndim == 0:
            a = a.reshape(1)
        arrays[f"in_{name}"] = a
        args.append(nc.dram_tensor(f"in_{name}", a.shape, _mybir.dt.from_np(a.dtype), kind="ExternalInput").ap())
    shape = arrays["in_x"].shape
    args.append(nc.dram_tensor("out_dram", shape, _mybir.dt.float32, kind="ExternalOutput").ap())
    graph_network(nc, *args)
    r = _run(nc, [arrays], core_ids=[0])
    return r.results[0]["out_dram"]
```

```python
import concourse.bass as bass
from concourse import mybir
from contextlib import ExitStack

fp32 = mybir.dt.float32
fp16 = mybir.dt.float16
int32 = mybir.dt.int32
ALU = mybir.AluOpType
ACT = mybir.ActivationFunctionType
AX = mybir.AxisListType


class Count:

    def __init__(self, sem, free=0):
        self.sem, self.free = sem, free

    def wait(self, eng, n):
        eng.wait_ge(self.sem, n + self.free)


class Chain:

    def __init__(self, eng, sem, base=0):
        self.eng, self.sem, self.base, self.n = eng, sem, base, 0

    def __call__(self, ins):
        self.n += 1
        ins.then_inc(self.sem, 1)
        self.eng.wait_ge(self.sem, self.base + self.n)


def graph_network(nc, x, adj, nodemask, g0_w, g0_b, f0_router, f0_w1, f0_b1, f0_w2, f0_b2,
                  g1_w, g1_b, g1_a1, g1_a2, g1_attb, f1_wr, f1_br, f1_w1, f1_b1, f1_w2, f1_b2,
                  gamma, beta, out):
    B, N, D = x.shape
    E = f0_router.shape[0]
    F = f1_w1.shape[2]
    HALVES = F // D
    T = 4
    GW = T * N
    G = B // T
    CAPACITY = float(-(-B * N * 5 // (4 * E)))
    EPS = 1e-5
    WS = 64.0
    BIG = -3.0e38

    ctx = ExitStack()
    with ctx:
        def sb(name, shape, dt=fp32):
            return ctx.enter_context(nc.sbuf_tensor(name, shape, dt))

        credits = []

        def count(name, free=0):
            c = Count(ctx.enter_context(nc.semaphore(name)), free)
            if free:
                credits.append(c)
            return c

        def sem(name):
            return ctx.enter_context(nc.semaphore(name))

        X = sb("X", [128, B * D])
        adjT = sb("adjT", [128, B * N])
        XTh = sb("XTh", [128, B * N], fp16)
        XTl = sb("XTl", [128, B * N], fp16)
        adj_in = sb("adj_in", [128, 4, GW])
        XN = sb("XN", [128, 2, GW])
        ZT = sb("ZT", [128, 2, GW])

        stats = sb("stats", [128, B, 6])
        rstd = sb("rstd", [128, B])
        nmr = sb("nmr", [128, B])
        ln_a = sb("ln_a", [128, B])
        ln_b = sb("ln_b", [128, B])
        ln_c = sb("ln_c", [128, B])

        ident = sb("ident", [128, 128])
        ident16 = sb("ident16", [128, 128], fp16)
        ones = sb("ones", [128, 128])
        selector = sb("selector", [128, E, 128], fp16)
        rank = sb("rank", [128, E])
        two_ones = sb("two_ones", [128, 128], fp16)
        rows_in = sb("rows_in", [128, 128])
        cols = sb("cols", [128, 128])
        g0w = sb("g0w", [128, D])
        g0b = sb("g0b", [128, D])
        g1w = sb("g1w", [128, D])
        g1b = sb("g1b", [128, D])
        avec = sb("avec", [128, 4])
        attb = sb("attb", [128, 1])
        wr = sb("wr", [128, E])
        br = sb("br", [B, E])
        gam = sb("gam", [128, D])
        bet = sb("bet", [128, D])
        epst = sb("epst", [128, 1])
        router_h = sb("router_h", [128, E], fp16)
        router_l = sb("router_l", [128, E], fp16)
        raw = sb("raw", [128, 2 * E * D + 2 * E * F])
        w1raw = raw[:, 0:E * D]
        w2raw = raw[:, E * D:2 * E * D]
        m1raw = raw[:, 2 * E * D:2 * E * D + E * F]
        m2raw = raw[:, 2 * E * D + E * F:]
        w1h, w1l = sb("w1h", [128, E * D], fp16), sb("w1l", [128, E * D], fp16)
        w2h, w2l = sb("w2h", [128, E * D], fp16), sb("w2l", [128, E * D], fp16)
        m1h, m1l = sb("m1h", [128, E * F], fp16), sb("m1l", [128, E * F], fp16)
        b2raw = sb("b2raw", [128, D])
        b2w = sb("b2w", [128, D], fp16)
        b2t = sb("b2t", [128, D], fp16)
        mb1raw = XTl[:, :].bitcast(fp32)[0:64, E * D:E * D + E * F]
        mb1 = sb("mb1", [128, E * F], fp16)
        mb2 = sb("mb2", [E, D])
        mbt = XTh[0:64, 0:E * F]
        wTh, wTl = sb("wTh", [128, D], fp16), sb("wTl", [128, D], fp16)
        v12 = sb("v12", [128, 2])
        v1h, v1l = sb("v1h", [128, 128], fp16), sb("v1l", [128, 128], fp16)
        v2h, v2l = sb("v2h", [128, 1], fp16), sb("v2l", [128, 1], fp16)
        att_const = sb("att_const", [128, 1])

        lg = [ZT[:, 0, :], sb("gates", [128, B * E]), ZT[:, 1, :], adj_in[:, 3, :]]
        small = [sb(f"small{i}", [128, B]) for i in range(3)]
        cpad = sb("cpad", [128, 2, T, 128], fp16)
        cT = sb("cT", [128, 2, GW], fp16)
        h32 = adj_in
        hc32 = ZT
        hh = sb("hh", [128, 4, GW], fp16)
        hl = sb("hl", [128, 4, GW], fp16)

        def in_raw(k, n=2):
            return raw[:, k * GW:(k + n) * GW].rearrange("p (a c) -> p a c", a=n)
        sig, att, H = in_raw(0), in_raw(2), in_raw(4)
        U = in_raw(6)
        s2c = sb("s2c", [128, 2, T])
        frac = sb("frac", [128, 2, 3 * T])
        xsum = sb("xsum", [128, B])

        r = [sb(f"r{i}", [B, E]) for i in range(6)]
        rc = [sb(f"rc{i}", [B, 1]) for i in range(8)]
        diag = sb("diag", [B, 4, B])
        gate = sb("gate", [128, 4, B])
        index = sb("index", [128, 2 * B], int32)
        mix = sb("mix", [B, 2, E])
        mixT = sb("mixT", [E, 2, B])
        b2sum = sb("b2sum", [128, D], fp16)
        b2high = sb("b2high", [128, D], fp16)
        pick = sb("pick", [128, B], fp16)
        hT = sb("hT", [128, 4, 2 * F])

        PS = ctx.enter_context(nc.psum_tensor("PS", [128, 8, 512], fp32))

        def bank(i):
            return PS[:, i, :]

        def tile(t, b, n=1, w=128):
            return t[:, bass.ds(b * w, n * w)]

        vec = sem("vec_own")
        scl = sem("act_own")
        pool = sem("pool_own")
        weights_loaded = sem("weights_loaded")
        big_loaded = sem("big_loaded")
        mid_high = sem("mid_high")
        late_high = sem("late_high")
        late_low = sem("late_low")
        ident_made = sem("ident_made")
        prep_pe = sem("prep_pe")
        prep_hi = sem("prep_hi")
        prep_done = sem("prep_done")
        cols_saved = sem("cols_saved")
        group_loaded = [sem(f"group_loaded{q}") for q in range(4)]
        adj_turned = count("adj_turned", 4)
        adjT_saved = count("adjT_saved", 2)
        moments = sem("moments")
        sqrt_done = sem("sqrt_done")
        ln_ready = sem("ln_ready")
        x_loaded = [sem(f"x_loaded{c}") for c in range(4)]
        xn_act = count("xn_act")
        xn_dve = count("xn_dve")
        z_made = count("z_made", 2)
        z_saved = count("z_saved", 2)
        bias_added = count("bias_added")
        o_made = count("o_made", 2)
        x1_saved = count("x1_saved", 2)
        n2_act = count("n2_act")
        n2_dve = count("n2_dve")
        n2_turned = count("n2_turned", 2)
        n2h_saved = count("n2h_saved")
        n2l_saved = count("n2l_saved", 2)
        n2_added = count("n2_added", 2)
        adj_masked = sem("adj_masked")
        logits_made = sem("logits_made")
        exp_in = sem("exp_in")
        exp_out = sem("exp_out")
        gates_ready = sem("gates_ready")
        cpad_ready = count("cpad_ready")
        c_turned = count("c_turned", 2)
        c_saved = count("c_saved")
        up_made = count("up_made")
        gelu_done = count("gelu_done", 2)
        cb_made = count("cb_made")
        hc_ready = count("hc_ready", 2)
        hh_ready = count("hh_ready", 2)
        hl_ready = count("hl_ready", 2)
        down_made = count("down_made", 4)
        moe_made = count("moe_made")
        x2_saved = count("x2_saved", 2)
        n3_ready = count("n3_ready")
        n3_turned = count("n3_turned", 2)
        n3h_saved = count("n3h_saved")
        n3l_saved = count("n3l_saved")
        proj_made = count("proj_made")
        s2_saved = count("s2_saved")
        sums_read = count("sums_read", 2)
        h_saved = count("h_saved", 2)
        sig_ready = count("sig_ready", 2)
        att_ready = count("att_ready", 2)
        att_used = count("att_used", 2)
        u_saved = count("u_saved", 2)
        x3_ready = count("x3_ready", 2)
        n4_act = count("n4_act")
        n4_dve = count("n4_dve")
        n4_turned = count("n4_turned", 2)
        n4_kept = count("n4_kept", 2)
        n4h_saved = count("n4h_saved")
        n4l_saved = count("n4l_saved", 2)
        route_pe = sem("route_pe")
        route_dve = sem("route_dve")
        route_act = sem("route_act")
        route_ready = sem("route_ready")
        f_made = count("f_made", 4)
        z_moments = sem("z_moments")
        z_sqrt = sem("z_sqrt")
        z_ln = sem("z_ln")
        x_fetched = count("x_fetched")
        g_ready = count("g_ready", 2)
        h_turned = count("h_turned", 4)
        hT_act = count("hT_act", 2)
        hT_dve = count("hT_dve", 2)
        y_made = count("y_made", 4)
        y_saved = count("y_saved", 2)
        norm_ready = count("norm_ready")
        xb_ready = count("xb_ready")
        out_ready = count("out_ready")
        stored = [count(f"stored{q}", 16) for q in range(2)]

        CG = 4
        CB = CG * T
        CHUNKS = B // CB

        block = ctx.enter_context(nc.Block())

        @block.sync
        def _(sp):
            for c in credits:
                sp.sem_inc(c.sem, c.free)
            for c in range(4):
                cb = B // 4
                sp.dma_start(X[:, c * cb * D:(c + 1) * cb * D].rearrange("p (b d) -> p b d", b=cb),
                             x[c * cb:(c + 1) * cb, :, :].rearrange("b p d -> p b d")).then_inc(x_loaded[c], 16)
            with sp.Fori(0, G // 4) as it:
                for q in range(4):
                    g = it * 4 + q
                    adj_turned.wait(sp, it * 4 + (q - 3))
                    sp.dma_start(adj_in[:, q, :].rearrange("p (t d) -> p t d", t=T),
                                 adj[bass.ds(g * T, T), :, :].rearrange("t p d -> p t d")).then_inc(group_loaded[q], 16)
            for dst, src in (
                    (w1raw.rearrange("p (e f) -> p e f", e=E), f0_w1.rearrange("e d f -> d e f")),
                    (w2raw.rearrange("p (e f) -> p e f", e=E), f0_w2.rearrange("e f d -> f e d")),
                    (m1raw.rearrange("p (e f) -> p e f", e=E), f1_w1.rearrange("e d f -> d e f")),
                    (m2raw.rearrange("p (e h d) -> p e h d", e=E, h=HALVES),
                     f1_w2.rearrange("e (h p) d -> p e h d", p=128))):
                sp.dma_start(dst, src).then_inc(big_loaded, 16)

            with sp.Fori(0, G // 2) as it:
                for p in range(2):
                    g = it * 2 + p
                    out_ready.wait(sp, g + 1)
                    sp.dma_start(out[bass.ds(g * T, T), :, :].rearrange("t p d -> p t d"),
                                 tile(X, g, 1, GW).rearrange("p (t d) -> p t d", t=T)).then_inc(stored[p].sem, 16)
            for p in range(2):
                stored[p].wait(sp, 16 * (G // 2))

        SMALL, BIG_LOADS = 16 * (15 + 1 + 3 + 2), 16 * 4

        @block.gpsimd
        def _(g_):
            own = Chain(g_, pool)
            own(g_.memset(ident[:, :], 0.0))
            own(g_.affine_select(out=ident[:, :], in_=ident[:, :], compare_op=ALU.not_equal, fill=1.0,
                                 base=0, pattern=[[-1, 128]], channel_multiplier=1))
            own(g_.memset(ones[:, :], 1.0))
            own(g_.memset(epst[:, :], EPS))
            own(g_.memset(two_ones[:, :], 0.0))
            own(g_.memset(two_ones[0:1, :], 1.0))
            own(g_.memset(two_ones[32:33, :], 1.0))
            own(g_.memset(b2w[:, :], 0.0))
            own(g_.memset(mb1[:, :], 0.0))
            own(g_.memset(cpad[:, :, :, :], 0.0))
            for e in range(E):
                own(g_.memset(rank[:, e:e + 1], float(E - e)))
            g_.sem_inc(ident_made, 1)

            def add_row(g, row):
                return g_.tensor_tensor(tile(X, g, 1, GW).rearrange("p (t d) -> p t d", t=T),
                                        tile(X, g, 1, GW).rearrange("p (t d) -> p t d", t=T),
                                        row[:, :].unsqueeze(1).broadcast_to([128, T, D]), ALU.add)

            g_.wait_ge(weights_loaded, SMALL)
            with g_.Fori(0, G // 2) as it:
                for p in range(2):
                    g = it * 2 + p
                    xn_act.wait(g_, g + 1)
                    xn_dve.wait(g_, g + 1)
                    add_row(g, g0b).then_inc(bias_added.sem, 1)
            with g_.Fori(0, G // 2) as it:
                for p in range(2):
                    g = it * 2 + p
                    n2_act.wait(g_, g + 1)
                    n2_dve.wait(g_, g + 1)
                    g_.tensor_tensor(tile(X, g, 1, GW), tile(X, g, 1, GW), XN[:, p, :], ALU.add).then_inc(n2_added.sem, 1)
            with g_.Fori(0, G * E // 8) as it:
                for k in range(8):
                    n = it * 8 + k
                    hh_ready.wait(g_, n + 1)
                    down_made.wait(g_, n - 3)
                    g_.tensor_tensor(hl[:, k % 4, :], hc32[:, k % 2, :], hh[:, k % 4, :],
                                     ALU.subtract).then_inc(hl_ready.sem, 1)
            def attend(g, p):
                sig_ready.wait(g_, g + 1)
                att_used.wait(g_, g - 1)
                g_.tensor_tensor(att[:, p, :], sig[:, p, :], tile(adjT, g, 1, GW), ALU.mult).then_inc(att_ready.sem, 1)

            def residual(g, p):
                u_saved.wait(g_, g + 1)
                g_.tensor_tensor(tile(X, g, 1, GW), U[:, p, :], tile(X, g, 1, GW), ALU.add).then_inc(x3_ready.sem, 1)

            g_.wait_ge(adj_masked, G)
            attend(0, 0)
            with g_.Fori(0, G // 2 - 1) as it:
                for p in range(2):
                    attend(it * 2 + (p + 1), 1 - p)
                    residual(it * 2 + p, p)
            attend(G - 1, 1)
            residual(G - 2, 0)
            residual(G - 1, 1)
            with g_.Fori(0, G // 2) as it:
                for p in range(2):
                    g = it * 2 + p
                    n4_act.wait(g_, g + 1)
                    n4_dve.wait(g_, g + 1)
                    add_row(g, bet).then_inc(xb_ready.sem, 1)
            def fetch(g, p):
                n4l_saved.wait(g_, g + 1)
                f_made.wait(g_, (g - 1) * T)
                for dst, src in ((hh, XTh), (hl, XTl)):
                    ins = g_.tensor_copy(dst[:, p, :], tile(src, g, 1, GW))
                ins.then_inc(x_fetched.sem, 1)

            with g_.Fori(0, G // 2) as it:
                for p in range(2):
                    fetch(it * 2 + p, p)

        @block.scalar
        def _(act):
            own = Chain(act, scl)

            def load(dst, src):
                act.dma_start(dst, src).then_inc(weights_loaded, 16)

            load(g0w[:, :], g0_w)
            load(g0b[:, :], g0_b.partition_broadcast(128))
            load(rows_in[0:B, :], nodemask)
            load(rows_in[B:B + E, :], f0_router)
            load(rows_in[B + E:B + 2 * E, :], f0_b1)
            load(g1w[:, :], g1_w)
            load(avec[:, 0:1], g1_a1.rearrange("(d o) -> d o", o=1))
            load(avec[:, 1:2], g1_a2.rearrange("(d o) -> d o", o=1))
            load(avec[:, 2:3], g1_b.rearrange("(d o) -> d o", o=1))
            load(attb[:, :], g1_attb.partition_broadcast(128))
            load(g1b[:, :], g1_b.partition_broadcast(128))
            load(gam[:, :], gamma.partition_broadcast(128))
            load(bet[:, :], beta.partition_broadcast(128))
            load(wr[:, :], f1_wr)
            load(br[:, :], f1_br.partition_broadcast(B))
            load(mb2[:, :], f1_b2)
            for q in (0, 32, 64):
                load(b2raw[q:q + E, :], f0_b2)
            for q in (0, 32):
                load(mb1raw[q:q + 1, :], f1_b1.rearrange("(o e) f -> o (e f)", o=1))

            def sqrt(k):
                act.wait_ge(moments, k)
                act.activation(ln_a[:, :], ln_c[:, :], ACT.Sqrt, bias=epst[:, :]).then_inc(sqrt_done, 1)

            def norm(dst, g, ready, rows=range(T)):
                for j in rows:
                    ins = act.activation(dst[:, j * D:(j + 1) * D], X[:, bass.ds(g * GW + j * D, D)], ACT.Identity,
                                         bias=nmr[:, bass.ds(g * T + j, 1)], scale=rstd[:, bass.ds(g * T + j, 1)])
                ins.then_inc(ready.sem, 1)

            act.wait_ge(weights_loaded, SMALL)
            act.wait_ge(ident_made, 1)
            own(act.activation(ident16[:, :], ident[:, :], ACT.Copy))
            act.wait_ge(prep_pe, 1)
            own(act.activation(cols[:, 0:B + 2 * E], bank(6)[:, 0:B + 2 * E], ACT.Copy))
            own(act.activation(wTh[:, :], bank(6)[:, 128:256], ACT.Copy, scale=WS))
            own(act.activation(v12[:, :], bank(6)[:, 256:258], ACT.Copy, scale=WS))
            own(act.activation(v1h[:, :], v12[:, 0:1].broadcast_to([128, 128]), ACT.Copy))
            own(act.activation(v2h[:, :], v12[:, 1:2], ACT.Copy))
            own(act.activation(router_h[:, :], cols[:, B:B + E], ACT.Copy, scale=WS))
            own(act.activation(att_const[:, :], bank(6)[:, 258:259], ACT.Identity, bias=attb[:, :]))
            act.sem_inc(prep_hi, 1)
            sqrt(1)
            act.wait_ge(ln_ready, 1)

            def save_adj(g, q):
                adj_turned.wait(act, g + 1)
                act.activation(tile(adjT, g, 1, GW), bank(q % 2), ACT.Copy).then_inc(adjT_saved.sem, 1)

            def save_z(g, p):
                z_made.wait(act, g + 1)
                o_made.wait(act, g - 1)
                act.activation(ZT[:, p, :], bank(2 + p), ACT.Copy).then_inc(z_saved.sem, 1)

            def n1_norm(g, p):
                z_made.wait(act, g - 1)
                norm(XN[:, p, :], g, xn_act, (0, 1))

            def g0_step(g, q):
                if not (isinstance(g, int) and g + 2 >= G):
                    save_adj(g + 2, q + 2)
                if not (isinstance(g, int) and g + 1 >= G):
                    save_z(g + 1, (q + 1) % 2)
                if not (isinstance(g, int) and g + 2 >= G):
                    n1_norm(g + 2, q % 2)

            n1_norm(0, 0)
            save_adj(0, 0)
            save_adj(1, 1)
            n1_norm(1, 1)
            save_z(0, 0)
            for dst, src in ((mb1[0:1, :], mb1raw[0:1, :]), (mbt[32:33, :], mb1raw[32:33, :])):
                own(act.activation(dst, src, ACT.Copy, scale=WS))
            act.sem_inc(prep_hi, 1)
            with act.Fori(0, G // 4 - 1) as it:
                for q in range(4):
                    g0_step(it * 4 + q, q)
            for q in range(4):
                g0_step(G - 4 + q, q)

            act.wait_ge(big_loaded, BIG_LOADS)
            own(act.activation(w1h[:, :], w1raw, ACT.Copy, scale=WS))
            own(act.activation(w2h[:, :], w2raw, ACT.Copy, scale=WS))
            own(act.activation(b2w[0:E, :], b2raw[0:E, :], ACT.Copy, scale=WS))
            own(act.activation(b2w[32:32 + E, :], b2raw[32:32 + E, :], ACT.Copy, scale=WS))
            own(act.activation(b2t[64:64 + E, :], b2raw[64:64 + E, :], ACT.Copy, scale=WS))
            act.sem_inc(mid_high, 1)
            sqrt(2)
            act.wait_ge(ln_ready, 2)

            def n2_norm(g, p):
                n2_turned.wait(act, g - 1)
                n2_added.wait(act, g - 1)
                norm(XN[:, p, :], g, n2_act, (0, 1))

            def n2_high(g, p):
                n2_turned.wait(act, g + 1)
                act.activation(tile(XTh, g, 1, GW), bank(p), ACT.Copy).then_inc(n2h_saved.sem, 1)

            n2_norm(0, 0)
            with act.Fori(0, G // 2 - 1) as it:
                for p in range(2):
                    n2_norm(it * 2 + (p + 1), 1 - p)
                    n2_high(it * 2 + p, p)
            n2_norm(G - 1, 1)
            n2_high(G - 2, 0)
            n2_high(G - 1, 1)

            act.wait_ge(exp_in, 1)
            act.activation(lg[3], lg[3], ACT.Exp).then_inc(exp_out, 1)

            def gelu(n, k):
                up_made.wait(act, n + 1)
                hc_ready.wait(act, n - 1)
                act.activation(h32[:, k % 2, :], bank(k % 2), ACT.Gelu, bias=cols[:, B + E + k % E:B + E + k % E + 1],
                               scale=1.0 / WS).then_inc(gelu_done.sem, 1)

            def high(n, k):
                hc_ready.wait(act, n + 1)
                down_made.wait(act, n - 3)
                act.activation(hh[:, k % 4, :], hc32[:, k % 2, :], ACT.Copy).then_inc(hh_ready.sem, 1)

            gelu(0, 0)
            for k in range(E):
                gelu(k + 1, (k + 1) % E)
                high(k, k)
            own(act.activation(m1h[:, :], m1raw, ACT.Copy, scale=WS))
            act.sem_inc(late_high, 1)
            with act.Fori(1, G - 1) as it:
                for k in range(E):
                    gelu(it * E + (k + 1), (k + 1) % E)
                    high(it * E + k, k)
            for k in range(E):
                if k < E - 1:
                    gelu((G - 1) * E + k + 1, k + 1)
                high((G - 1) * E + k, k)

            sqrt(3)
            act.wait_ge(ln_ready, 3)

            def n3_norm(g, p):
                n3_turned.wait(act, g - 1)
                norm(XN[:, p, :], g, n3_ready)

            def n3_high(g, p):
                n3_turned.wait(act, g + 1)
                act.activation(hh[:, p, :], bank(0), ACT.Copy).then_inc(n3h_saved.sem, 1)

            def sigmoid(g, p):
                s2_saved.wait(act, g + 1)
                att_ready.wait(act, g - 1)
                for j in range(T):
                    ins = act.activation(sig[:, p, j * N:(j + 1) * N], bank(1 + p)[:, j * N:(j + 1) * N], ACT.Sigmoid,
                                         bias=s2c[:, p, j:j + 1], scale=1.0 / WS)
                ins.then_inc(sig_ready.sem, 1)

            n3_norm(0, 0)
            n3_norm(1, 1)
            n3_high(0, 0)
            sigmoid(0, 0)
            n3_high(1, 1)
            n3_norm(2, 0)
            with act.Fori(0, G // 2 - 2) as it:
                for p in range(2):
                    g = it * 2 + p
                    sigmoid(g + 1, 1 - p)
                    n3_high(g + 2, p)
                    n3_norm(g + 3, 1 - p)
            sigmoid(G - 3, 1)
            n3_high(G - 2, 0)
            n3_norm(G - 1, 1)
            sigmoid(G - 2, 0)
            n3_high(G - 1, 1)
            sigmoid(G - 1, 1)

            sqrt(4)
            act.wait_ge(ln_ready, 4)

            def n4_norm(g, p):
                n4_turned.wait(act, g - 1)
                n4_kept.wait(act, g - 1)
                norm(XN[:, p, :], g, n4_act, (0, 1))

            def n4_high(g, p):
                n4_turned.wait(act, g + 1)
                act.activation(tile(XTh, g, 1, GW), bank(6 + p), ACT.Copy).then_inc(n4h_saved.sem, 1)

            n4_norm(0, 0)
            with act.Fori(0, G // 2 - 1) as it:
                for p in range(2):
                    n4_norm(it * 2 + (p + 1), 1 - p)
                    n4_high(it * 2 + p, p)
            n4_norm(G - 1, 1)
            n4_high(G - 2, 0)
            n4_high(G - 1, 1)

            act.wait_ge(route_dve, 2)
            act.activation(r[1][:, :], r[1][:, :], ACT.Exp).then_inc(route_act, 1)
            act.wait_ge(route_dve, 4)
            act.activation(r[1][:, :], r[1][:, :], ACT.Exp).then_inc(route_act, 1)
            act.wait_ge(route_dve, 5)
            act.activation(rc[5][:, :], rc[5][:, :], ACT.Exp).then_inc(route_act, 1)

            def gelu2(b, k):
                f_made.wait(act, b + 1)
                h_turned.wait(act, b - 3)
                act.activation(h32[:, k % 4, :], bank(k % 2), ACT.Gelu, scale=1.0 / WS).then_inc(g_ready.sem, 1)

            def gated(b, k):
                h_turned.wait(act, b + 1)
                y_made.wait(act, b - 3)
                act.activation(hT[:, k % 4, F:2 * F], bank(3 + k % 2 * 2)[:, 0:F], ACT.Copy,
                               scale=gate[:, 1, bass.ds(b, 1)]).then_inc(hT_act.sem, 1)

            def z_norm(b):
                z = tile(adjT, b)
                act.activation(z, z, ACT.Identity, bias=nmr[:, bass.ds(b, 1)],
                               scale=rstd[:, bass.ds(b, 1)]).then_inc(norm_ready.sem, 1)

            def z_root(c):
                act.wait_ge(z_moments, c + 1)
                at = bass.ds(c * CB, CB)
                act.activation(ln_a[:, at], ln_c[:, at], ACT.Sqrt, bias=epst[:, :]).then_inc(z_sqrt, 1)

            def chunk(c, first=False, last=False):
                for i in range(CG):
                    for k in range(T):
                        b = c * CB + (i * T + k)
                        if not (last and i == CG - 1 and k >= T - 2):
                            gelu2(b + 2, k + 2)
                        if not (last and i == CG - 1 and k == T - 1):
                            gated(b + 1, k + 1)
                        if first:
                            continue
                        if i == 0 and k == 0:
                            z_root(c - 1)
                        if i == 1 and k == 0:
                            act.wait_ge(z_ln, c)
                        if i in (1, 2):
                            for j in range(2):
                                z_norm(c * CB + (((i - 1) * T + k) * 2 + j - CB))

            gelu2(0, 0)
            gelu2(1, 1)
            gated(0, 0)
            chunk(0, first=True)
            with act.Fori(1, CHUNKS - 1) as c:
                chunk(c)
            chunk(CHUNKS - 1, last=True)
            z_root(CHUNKS - 1)
            act.wait_ge(z_ln, CHUNKS)
            for i in range(CB):
                z_norm(B - CB + i)

        @block.vector
        def _(dve):
            own = Chain(dve, vec)

            def low(dst, src, high_part):
                own(dve.scalar_tensor_tensor(dst, src, WS, high_part, ALU.mult, ALU.subtract))

            def finish_stats(k):
                me, qe, mo, qo = (stats[:, :, i] for i in (1, 2, 4, 5))
                own(dve.tensor_tensor(ln_b[:, :], me, mo, ALU.subtract))
                own(dve.tensor_tensor(ln_c[:, :], qe, qo, ALU.add))
                own(dve.scalar_tensor_tensor(ln_b[:, :], ln_b[:, :], 0.25, ln_b[:, :], ALU.mult, ALU.mult))
                own(dve.scalar_tensor_tensor(ln_c[:, :], ln_c[:, :], 1.0 / D, ln_b[:, :], ALU.mult, ALU.add))
                dve.sem_inc(moments, 1)
                own(dve.tensor_tensor(ln_b[:, :], me, mo, ALU.add))
                dve.wait_ge(sqrt_done, k)
                own(dve.reciprocal(rstd[:, :], ln_a[:, :]))
                own(dve.scalar_tensor_tensor(nmr[:, :], ln_b[:, :], -0.5, rstd[:, :], ALU.mult, ALU.mult))
                dve.sem_inc(ln_ready, 1)

            def group_stats(g, src=X, done=None):
                for j in range(T):
                    ins = dve.bn_stats(stats[:, bass.ds(g * T + j, 1), :], src[:, bass.ds(g * GW + j * D, D)])
                return ins

            own_stats = sem("group_stats")
            done_stats = 0
            for c in range(4):
                dve.wait_ge(x_loaded[c], 16)
                with dve.Fori(c * G // 4, (c + 1) * G // 4) as g:
                    group_stats(g).then_inc(own_stats, 1)
            done_stats += G
            dve.wait_ge(own_stats, done_stats)
            finish_stats(1)

            def norm(g, p, ready, rows=(2, 3)):
                for j in rows:
                    ins = dve.tensor_scalar(XN[:, p, j * D:(j + 1) * D], X[:, bass.ds(g * GW + j * D, D)],
                                            rstd[:, bass.ds(g * T + j, 1)], nmr[:, bass.ds(g * T + j, 1)],
                                            ALU.mult, ALU.add)
                ins.then_inc(ready.sem, 1)

            def n1_norm(g, p):
                z_made.wait(dve, g - 1)
                norm(g, p, xn_dve)

            def n1_add(g, p):
                o_made.wait(dve, g + 1)
                bias_added.wait(dve, g + 1)
                dve.tensor_tensor(tile(X, g, 1, GW), bank(4 + p), tile(X, g, 1, GW), ALU.add).then_inc(x1_saved.sem, 1)

            def n1_stats(g):
                x1_saved.wait(dve, g + 1)
                group_stats(g).then_inc(own_stats, 1)

            n1_norm(0, 0)
            n1_norm(1, 1)
            dve.wait_ge(prep_hi, 1)
            low(router_l[:, :], cols[:, B:B + E], router_h[:, :])
            low(wTl[:, :], bank(6)[:, 128:256], wTh[:, :])
            own(dve.tensor_tensor(v1l[:, :], v12[:, 0:1].broadcast_to([128, 128]), v1h[:, :], ALU.subtract))
            own(dve.tensor_tensor(v2l[:, :], v12[:, 1:2], v2h[:, :], ALU.subtract))
            own(dve.tensor_copy(selector[:, :, :], ident[:, 0:E].unsqueeze(2).broadcast_to([128, E, 128])))
            own(dve.tensor_tensor(selector[:, :, :], selector[:, :, :],
                                  ident[:, 32:32 + E].unsqueeze(2).broadcast_to([128, E, 128]), ALU.add))
            own(dve.tensor_tensor(pick[:, :], ident[:, 0:B], ident[:, B:2 * B], ALU.add))
            own(dve.tensor_scalar(pick[:, :], pick[:, :], 1.0 / WS, None, ALU.mult))
            dve.sem_inc(prep_done, 1)
            with dve.Fori(0, G // 2 - 1) as it:
                for p in range(2):
                    n1_norm(it * 2 + (p + 2), p)
                    n1_add(it * 2 + p, p)
                    n1_stats(it * 2 + p)
            for g in (G - 2, G - 1):
                n1_add(g, g % 2)
                n1_stats(g)
            dve.wait_ge(prep_hi, 2)
            low(mb1[32:33, :], mb1raw[32:33, :], mbt[32:33, :])
            done_stats += G
            dve.wait_ge(own_stats, done_stats)
            finish_stats(2)

            def n2_norm(g, p):
                n2_turned.wait(dve, g - 1)
                n2_added.wait(dve, g - 1)
                norm(g, p, n2_dve)

            def n2_low(g, p):
                n2h_saved.wait(dve, g + 1)
                dve.tensor_tensor(tile(XTl, g, 1, GW), bank(p), tile(XTh, g, 1, GW),
                                  ALU.subtract).then_inc(n2l_saved.sem, 1)

            n2_norm(0, 0)
            dve.wait_ge(mid_high, 1)
            low(w1l[:, :], w1raw, w1h[:, :])
            low(w2l[:, :], w2raw, w2h[:, :])
            low(b2w[64:64 + E, :], b2raw[64:64 + E, :], b2t[64:64 + E, :])
            dve.sem_inc(prep_done, 1)
            with dve.Fori(0, G // 2 - 1) as it:
                for p in range(2):
                    n2_norm(it * 2 + (p + 1), 1 - p)
                    n2_low(it * 2 + p, p)
            n2_norm(G - 1, 1)
            n2_low(G - 2, 0)
            n2_low(G - 1, 1)

            dve.wait_ge(logits_made, 1)

            def v3(t):
                return t.rearrange("p (b e) -> p b e", e=E)

            def wide(t):
                return t[:, :].unsqueeze(2).broadcast_to([128, B, E])
            L, O, K, M = lg[0], lg[1][:, :], lg[2], lg[3]
            m1, m2, kk = small
            rank3 = rank[:, :].unsqueeze(1).broadcast_to([128, B, E])
            own(dve.tensor_scalar(L, bank(7), 1.0 / WS, None, ALU.mult))
            own(dve.tensor_reduce(m1[:, :], v3(L), AX.X, ALU.max))
            own(dve.tensor_tensor(v3(M), v3(L), wide(m1), ALU.subtract))
            dve.sem_inc(exp_in, 1)
            own(dve.tensor_tensor(v3(K), v3(L), wide(m1), ALU.is_equal))
            own(dve.tensor_tensor(v3(K), v3(K), rank3, ALU.mult))
            own(dve.tensor_reduce(kk[:, :], v3(K), AX.X, ALU.max))
            own(dve.tensor_tensor(v3(O), v3(K), wide(kk), ALU.is_equal))
            own(dve.scalar_tensor_tensor(L, O, BIG, L, ALU.mult, ALU.add))
            own(dve.tensor_reduce(m2[:, :], v3(L), AX.X, ALU.max))
            own(dve.tensor_tensor(v3(K), v3(L), wide(m2), ALU.is_equal))
            own(dve.tensor_tensor(v3(K), v3(K), rank3, ALU.mult))
            own(dve.tensor_reduce(kk[:, :], v3(K), AX.X, ALU.max))
            own(dve.tensor_tensor(v3(K), v3(K), wide(kk), ALU.is_equal))
            own(dve.tensor_tensor(O, O, K, ALU.add))
            dve.wait_ge(exp_out, 1)
            own(dve.tensor_tensor(O, O, M, ALU.mult))
            own(dve.tensor_reduce(m1[:, :], v3(O), AX.X, ALU.add))
            own(dve.reciprocal(m1[:, :], m1[:, :]))
            own(dve.tensor_tensor(v3(O), v3(O), wide(m1), ALU.mult))

            def gates(g, p):
                c_turned.wait(dve, g - 1)
                src = O[:, bass.ds(g * T * E, T * E)].rearrange("p (t e) -> p t e", e=E)
                own_g(dve.tensor_scalar(cpad[:, p, :, 0:E], src, 1.0, None, ALU.mult))
                own_g(dve.tensor_scalar(cpad[:, p, :, 64:64 + E], src, 1.0, None, ALU.mult))
                dve.tensor_tensor(cpad[:, p, :, 32:32 + E], src, cpad[:, p, :, 0:E],
                                  ALU.subtract).then_inc(cpad_ready.sem, 1)

            def gates_copy(g, p):
                c_turned.wait(dve, g + 1)
                if not (isinstance(g, int) and g < 2):
                    down_made.wait(dve, g * E - E)
                dve.tensor_copy(cT[:, p, :], bank(6).bitcast(fp16)[:, 0:GW]).then_inc(c_saved.sem, 1)

            def gate_hidden(n, k):
                gelu_done.wait(dve, n + 1)
                cb_made.wait(dve, n + 1)
                hl_ready.wait(dve, n - 1)
                dve.tensor_tensor(hc32[:, k % 2, :], bank(2 + k % 2), h32[:, k % 2, :],
                                  ALU.mult).then_inc(hc_ready.sem, 1)

            def ffn_add(g, p):
                dve.tensor_tensor(tile(adjT, g, 1, GW).rearrange("p (t d) -> p t d", t=T),
                                  tile(adjT, g, 1, GW).rearrange("p (t d) -> p t d", t=T),
                                  cols[:, bass.ds(g * T, T)].unsqueeze(2).broadcast_to([128, T, D]),
                                  ALU.mult).then_inc(adj_masked, 1)
                moe_made.wait(dve, g + 1)
                dve.scalar_tensor_tensor(tile(X, g, 1, GW), bank(4 + p), 1.0 / WS, tile(X, g, 1, GW),
                                         ALU.mult, ALU.add).then_inc(x2_saved.sem, 1)

            def ffn_stats(g):
                x2_saved.wait(dve, g + 1)
                group_stats(g).then_inc(own_stats, 1)

            gate_own = sem("gate_own")
            own_g = Chain(dve, gate_own)
            gates(0, 0)
            gates_copy(0, 0)
            gates(1, 1)
            for k in range(E):
                if k == 4:
                    gates_copy(1, 1)
                gate_hidden(k, k)
            base = own_g.n
            dve.wait_ge(late_high, 1)
            low(m1l[:, :], m1raw, m1h[:, :])
            dve.sem_inc(late_low, 1)
            with dve.Fori(0, G // 2 - 1) as it:
                for q in range(2):
                    g = it * 2 + (q + 1)
                    p = (q + 1) % 2
                    own_g = Chain(dve, gate_own, it * 4 + (base + 2 * q))
                    gates(g + 1, 1 - p)
                    for k in range(E):
                        gate_hidden(g * E + k, k)
                        if k == 3:
                            gates_copy(g + 1, 1 - p)
                        if k == 4:
                            ffn_add(g - 1, 1 - p)
                            ffn_stats(g - 1)
            for k in range(E):
                gate_hidden((G - 1) * E + k, k)
                if k == 4:
                    ffn_add(G - 2, 0)
                    ffn_stats(G - 2)
            ffn_add(G - 1, 1)
            ffn_stats(G - 1)
            done_stats += G
            dve.wait_ge(own_stats, done_stats)
            finish_stats(3)

            frac_own = sem("frac_own")

            def n3_low(g, p):
                n3h_saved.wait(dve, g + 1)
                dve.tensor_tensor(hl[:, p, :], bank(0), hh[:, p, :], ALU.subtract).then_inc(n3l_saved.sem, 1)

            def project(g, p):
                proj_made.wait(dve, g + 1)
                sig_ready.wait(dve, g - 1)
                dve.tensor_scalar(s2c[:, p, :], bank(5)[:, 0:T], 1.0 / WS, att_const[:, 0:1], ALU.mult,
                                  ALU.add).then_inc(s2_saved.sem, 1)
                att_used.wait(dve, g - 1)
                dve.scalar_tensor_tensor(H[:, p, :].rearrange("p (t d) -> p t d", t=T),
                                         bank(3 + p).rearrange("p (t d) -> p t d", t=T), 1.0 / WS,
                                         g1b[:, :].unsqueeze(1).broadcast_to([128, T, D]),
                                         ALU.mult, ALU.add).then_inc(h_saved.sem, 1)

            def attended(g, p, chain):
                att_used.wait(dve, g + 1)
                mask = cols[:, bass.ds(g * T, T)]
                f = [frac[:, p, i * T:(i + 1) * T] for i in range(3)]
                chain(dve.tensor_tensor(f[0], bank(5)[:, 8:8 + T], mask, ALU.mult))
                dve.sem_inc(sums_read.sem, 1)
                chain(dve.tensor_scalar(f[0], f[0], 1e-8, None, ALU.add))
                chain(dve.reciprocal(f[1], f[0]))
                chain(dve.tensor_tensor(f[2], mask, mask, ALU.mult))
                chain(dve.tensor_tensor(f[2], f[2], f[1], ALU.mult))
                x3_ready.wait(dve, g - 1)
                dve.tensor_tensor(U[:, p, :].rearrange("p (t d) -> p t d", t=T),
                                  bank(6 + p).rearrange("p (t d) -> p t d", t=T),
                                  f[2].unsqueeze(2).broadcast_to([128, T, D]), ALU.mult).then_inc(u_saved.sem, 1)

            def x3_stats(g):
                x3_ready.wait(dve, g + 1)
                group_stats(g).then_inc(own_stats, 1)

            FR = 5
            n3_low(0, 0)
            project(0, 0)
            n3_low(1, 1)
            project(1, 1)
            n3_low(2, 0)
            attended(0, 0, Chain(dve, frac_own))
            with dve.Fori(0, G // 2 - 2) as it:
                for q in range(2):
                    g = it * 2 + (q + 1)
                    p = (q + 1) % 2
                    project(g + 1, 1 - p)
                    n3_low(g + 2, p)
                    attended(g, p, Chain(dve, frac_own, it * 2 * FR + (q + 1) * FR))
                    x3_stats(g - 1)
            project(G - 2, 0)
            n3_low(G - 1, 1)
            attended(G - 3, 1, Chain(dve, frac_own, (G - 3) * FR))
            x3_stats(G - 4)
            project(G - 1, 1)
            attended(G - 2, 0, Chain(dve, frac_own, (G - 2) * FR))
            x3_stats(G - 3)
            attended(G - 1, 1, Chain(dve, frac_own, (G - 1) * FR))
            x3_stats(G - 2)
            x3_stats(G - 1)
            done_stats += G
            dve.wait_ge(own_stats, done_stats)
            finish_stats(4)

            def n4_norm(g, p):
                n4_turned.wait(dve, g - 1)
                n4_kept.wait(dve, g - 1)
                norm(g, p, n4_dve)

            def n4_low(g, p):
                n4_act.wait(dve, g + 1)
                n4_dve.wait(dve, g + 1)
                dve.tensor_scalar(tile(adjT, g, 1, GW), XN[:, p, :], 1.0, None, ALU.mult).then_inc(n4_kept.sem, 1)
                n4h_saved.wait(dve, g + 1)
                dve.tensor_tensor(tile(XTl, g, 1, GW), bank(6 + p), tile(XTh, g, 1, GW),
                                  ALU.subtract).then_inc(n4l_saved.sem, 1)

            n4_norm(0, 0)
            with dve.Fori(0, G // 2 - 1) as it:
                for p in range(2):
                    n4_norm(it * 2 + (p + 1), 1 - p)
                    n4_low(it * 2 + p, p)
            n4_norm(G - 1, 1)
            n4_low(G - 2, 0)
            n4_low(G - 1, 1)

            dve.wait_ge(route_pe, 1)
            own(dve.tensor_copy(xsum[:, :], bank(5)[:, 0:B]))
            dve.sem_inc(route_dve, 1)
            dve.wait_ge(route_pe, 2)

            def row(t, n=E):
                return t[:, 0:1].broadcast_to([B, n])
            own(dve.scalar_tensor_tensor(r[0][:, :], bank(2)[0:B, 0:E], 1.0 / N, br[:, :], ALU.mult, ALU.add))
            own(dve.tensor_reduce(rc[0][:, :], r[0][:, :], AX.X, ALU.max))
            own(dve.tensor_tensor(r[1][:, :], r[0][:, :], row(rc[0]), ALU.subtract))
            dve.sem_inc(route_dve, 1)
            dve.wait_ge(route_act, 1)
            own(dve.tensor_reduce(rc[1][:, :], r[1][:, :], AX.X, ALU.add))
            own(dve.reciprocal(rc[1][:, :], rc[1][:, :]))
            own(dve.tensor_tensor(r[2][:, :], r[1][:, :], row(rc[1]), ALU.mult))
            dve.sem_inc(route_dve, 1)
            dve.wait_ge(route_pe, 3)
            own(dve.tensor_scalar(r[3][:, :], bank(3)[0:B, 0:E], float(N), CAPACITY, ALU.mult, ALU.max))
            own(dve.reciprocal(r[4][:, :], r[3][:, :]))
            own(dve.tensor_scalar(r[4][:, :], r[4][:, :], CAPACITY, None, ALU.mult))
            own(dve.tensor_scalar(r[3][:, :], r[3][:, :], CAPACITY, None, ALU.is_gt))
            own(dve.tensor_scalar(r[4][:, :], r[4][:, :], -1.0, None, ALU.add))
            own(dve.tensor_tensor(r[4][:, :], r[4][:, :], r[3][:, :], ALU.mult))
            own(dve.tensor_scalar(r[4][:, :], r[4][:, :], 1.0, None, ALU.add))
            own(dve.tensor_tensor(r[0][:, :], r[2][:, :], r[4][:, :], ALU.mult))
            own(dve.tensor_reduce(rc[0][:, :], r[0][:, :], AX.X, ALU.max))
            own(dve.tensor_tensor(r[1][:, :], r[0][:, :], row(rc[0]), ALU.subtract))
            dve.sem_inc(route_dve, 1)
            dve.wait_ge(route_act, 2)
            own(dve.tensor_reduce(rc[1][:, :], r[1][:, :], AX.X, ALU.add))
            own(dve.reciprocal(rc[1][:, :], rc[1][:, :]))
            own(dve.tensor_tensor(r[0][:, :], r[1][:, :], row(rc[1]), ALU.mult))
            for i, (m, k) in enumerate(((rc[0], rc[2]), (rc[1], rc[3]))):
                own(dve.tensor_reduce(m[:, :], r[0][:, :], AX.X, ALU.max))
                own(dve.tensor_tensor(r[2][:, :], r[0][:, :], row(m), ALU.is_equal))
                own(dve.tensor_tensor(r[2][:, :], r[2][:, :], rank[0:B, :], ALU.mult))
                own(dve.tensor_reduce(k[:, :], r[2][:, :], AX.X, ALU.max))
                if i == 0:
                    own(dve.tensor_tensor(r[2][:, :], r[2][:, :], row(k), ALU.is_equal))
                    own(dve.scalar_tensor_tensor(r[0][:, :], r[2][:, :], BIG, r[0][:, :], ALU.mult, ALU.add))
            own(dve.tensor_tensor(rc[5][:, :], rc[1][:, :], rc[0][:, :], ALU.subtract))
            dve.sem_inc(route_dve, 1)
            dve.wait_ge(route_act, 3)
            own(dve.tensor_scalar(rc[6][:, :], rc[5][:, :], 1.0, None, ALU.add))
            own(dve.reciprocal(rc[6][:, :], rc[6][:, :]))
            own(dve.tensor_tensor(rc[7][:, :], rc[5][:, :], rc[6][:, :], ALU.mult))
            for i, (c, w) in enumerate(((rc[2], rc[6]), (rc[3], rc[7]))):
                own(dve.tensor_scalar(mix[:, i, :], rank[0:B, :], c[:, 0:1], w[:, 0:1], ALU.is_equal, ALU.mult))
            own(dve.tensor_tensor(mix[:, 0, :], mix[:, 0, :], mix[:, 1, :], ALU.add))
            for c in (rc[2], rc[3]):
                own(dve.tensor_scalar(c[:, :], c[:, :], -float(F), float(E * F), ALU.mult, ALU.add))
            for i, c in enumerate((rc[6], rc[7], rc[2], rc[3])):
                own(dve.tensor_scalar(diag[:, i, :], ident[0:B, 0:B], c[:, 0:1], None, ALU.mult))
            dve.sem_inc(route_dve, 1)
            dve.wait_ge(route_pe, 4)
            own(dve.tensor_copy(gate[:, :, :], bank(2)[:, 0:4 * B].rearrange("p (i b) -> p i b", i=4)))
            own(dve.tensor_copy(index[:, :].rearrange("p (b k) -> p k b", k=2), gate[:, 2:4, :]))
            dve.sem_inc(route_ready, 1)
            own(dve.tensor_copy(mixT[:, :, :], bank(6)[0:E, 0:B].unsqueeze(1).broadcast_to([E, 2, B])))
            dve.sem_inc(route_dve, 1)
            dve.wait_ge(route_pe, 5)
            own(dve.tensor_scalar(b2high[:, :], bank(7)[:, 0:D], WS, None, ALU.mult))
            own(dve.tensor_copy(b2sum[0:B, :], b2high[0:B, :]))
            low(b2sum[B:2 * B, :], bank(7)[B:2 * B, 0:D], b2high[B:2 * B, :])
            dve.sem_inc(route_ready, 1)

            z_own = sem("z_own")
            out_own = sem("out_own")
            chunk_own = sem("chunk_own")

            def gated(b, k):
                h_turned.wait(dve, b + 1)
                y_made.wait(dve, b - 3)
                dve.tensor_scalar(hT[:, k % 4, 0:F], bank(2 + k % 2 * 2)[:, 0:F], gate[:, 0, bass.ds(b, 1)], None,
                                  ALU.mult).then_inc(hT_dve.sem, 1)

            def z_sum(b, k):
                y_made.wait(dve, b + 1)
                dve.tensor_tensor(tile(adjT, b), bank(6 + k % 2)[:, 0:D], tile(adjT, b), ALU.add).then_inc(y_saved.sem, 1)

            def z_stats(b):
                y_saved.wait(dve, b + 1)
                dve.bn_stats(stats[:, bass.ds(b, 1), :], tile(adjT, b)).then_inc(z_own, 1)

            def z_begin(c, link):
                at = bass.ds(c * CB, CB)
                me, qe, mo, qo = (stats[:, at, i] for i in (1, 2, 4, 5))
                dve.wait_ge(z_own, c * CB + CB)
                link(dve.tensor_tensor(ln_b[:, at], me, mo, ALU.subtract))
                link(dve.tensor_tensor(ln_c[:, at], qe, qo, ALU.add))
                link(dve.scalar_tensor_tensor(ln_b[:, at], ln_b[:, at], 0.25, ln_b[:, at], ALU.mult, ALU.mult))
                link(dve.scalar_tensor_tensor(ln_c[:, at], ln_c[:, at], 1.0 / D, ln_b[:, at], ALU.mult, ALU.add))
                dve.sem_inc(z_moments, 1)
                link(dve.tensor_tensor(ln_b[:, at], me, mo, ALU.add))

            def z_end(c, link):
                at = bass.ds(c * CB, CB)
                dve.wait_ge(z_sqrt, c + 1)
                link(dve.reciprocal(rstd[:, at], ln_a[:, at]))
                link(dve.scalar_tensor_tensor(nmr[:, at], ln_b[:, at], -0.5, rstd[:, at], ALU.mult, ALU.mult))
                dve.sem_inc(z_ln, 1)

            def finish_group(g):
                norm_ready.wait(dve, g * T + T)
                dve.tensor_tensor(tile(adjT, g, 1, GW).rearrange("p (t d) -> p t d", t=T),
                                  tile(adjT, g, 1, GW).rearrange("p (t d) -> p t d", t=T),
                                  gam[:, :].unsqueeze(1).broadcast_to([128, T, D]), ALU.mult).then_inc(out_own, 1)
                xb_ready.wait(dve, g + 1)
                dve.wait_ge(out_own, g + 1)
                dve.tensor_tensor(tile(X, g, 1, GW), tile(adjT, g, 1, GW), tile(X, g, 1, GW),
                                  ALU.add).then_inc(out_ready.sem, 1)

            LINKS = 7

            def chunk(c, first=False, last=False):
                for i in range(CG):
                    for k in range(T):
                        b = c * CB + (i * T + k)
                        if not (last and i == CG - 1 and k == T - 1):
                            gated(b + 1, k + 1)
                        z_sum(b, k)
                        if i or k:
                            z_stats(c * CB + (i * T + k - 1))
                        if first:
                            continue
                        if i == 0 and k == 2:
                            z_end(c - 1, Chain(dve, chunk_own, c * LINKS - 2))
                        for done, at in enumerate(((1, 2), (2, 0), (2, 2), (3, 1))):
                            if (i, k) == at:
                                finish_group(c * CG + (done - CG))
                z_stats(c * CB + (CB - 1))
                z_begin(c, Chain(dve, chunk_own, c * LINKS))

            gated(0, 0)
            chunk(0, first=True)
            with dve.Fori(1, CHUNKS - 1) as c:
                chunk(c)
            chunk(CHUNKS - 1, last=True)
            z_end(CHUNKS - 1, Chain(dve, chunk_own, CHUNKS * LINKS - 2))
            for i in range(CG):
                finish_group(G - CG + i)

        @block.tensor
        def _(pe):
            def product(dst, parts, **kw):
                for i, (a, c) in enumerate(parts):
                    ins = pe.matmul(dst, a, c, start=(i == 0), stop=(i == len(parts) - 1))
                return ins

            def turn_adj(g, loads, q):
                pe.wait_ge(group_loaded[q], loads * 16)
                adjT_saved.wait(pe, g - 1)
                for j in range(T):
                    ins = pe.transpose(bank(q % 2)[:, j * N:(j + 1) * N], adj_in[:, q, j * N:(j + 1) * N], ident[:, :])
                ins.then_inc(adj_turned.sem, 1)

            def prepare():
                pe.wait_ge(weights_loaded, SMALL)
                pe.wait_ge(ident_made, 1)
                pe.transpose(bank(6)[:, 0:B + 2 * E], rows_in[0:B + 2 * E, :], ident[0:B + 2 * E, 0:B + 2 * E])
                pe.transpose(bank(6)[:, 128:256], g1w[:, :], ident[:, :])
                pe.matmul(bank(6)[:, 256:258], g1w[:, :], avec[:, 0:2], start=True, stop=True)
                b_wide = avec[:, 2:3].broadcast_to([128, 128])
                pe.matmul(bank(6)[:, 258:259], b_wide, avec[:, 0:1], start=True, stop=False)
                pe.matmul(bank(6)[:, 258:259], b_wide, avec[:, 1:2], start=False, stop=True).then_inc(prep_pe, 1)

            def g0_z(g, p):
                xn_act.wait(pe, g + 1)
                xn_dve.wait(pe, g + 1)
                adjT_saved.wait(pe, g + 1)
                z_saved.wait(pe, g - 1)
                for j in range(T):
                    ins = pe.matmul(bank(2 + p)[:, j * N:(j + 1) * N], XN[:, p, j * D:(j + 1) * D],
                                    adjT[:, bass.ds(g * GW + j * N, N)], start=True, stop=True)
                ins.then_inc(z_made.sem, 1)

            def g0_out(g, p):
                z_saved.wait(pe, g + 1)
                x1_saved.wait(pe, g - 1)
                for j in range(T):
                    ins = pe.matmul(bank(4 + p)[:, j * D:(j + 1) * D], ZT[:, p, j * N:(j + 1) * N], g0w[:, :],
                                    start=True, stop=True)
                ins.then_inc(o_made.sem, 1)

            def g0_step(g, it, q):
                if q < 2 or not isinstance(g, int):
                    turn_adj(g + 2, it + (1 if q < 2 else 2), (q + 2) % 4)
                if not (isinstance(g, int) and g + 1 >= G):
                    g0_z(g + 1, (q + 1) % 2)
                g0_out(g, q % 2)

            prepare()
            turn_adj(0, 1, 0)
            turn_adj(1, 1, 1)
            g0_z(0, 0)
            with pe.Fori(0, G // 4 - 1) as it:
                for q in range(4):
                    g0_step(it * 4 + q, it, q)
            for q in range(4):
                g0_step(G - 4 + q, G // 4 - 1, q)

            pe.wait_ge(prep_done, 1)

            def n2_turn(g, p):
                n2_act.wait(pe, g + 1)
                n2_dve.wait(pe, g + 1)
                n2l_saved.wait(pe, g - 1)
                for j in range(T):
                    ins = pe.transpose(bank(p)[:, j * N:(j + 1) * N], XN[:, p, j * D:(j + 1) * D], ident[:, :])
                ins.then_inc(n2_turned.sem, 1)

            def route(g, p):
                n2l_saved.wait(pe, g + 1)
                for j in range(T):
                    xh, xl = (tile(t, g * T + j) for t in (XTh, XTl))
                    ins = product(bank(7)[:, bass.ds(g * T * E + j * E, E)],
                                  [(xh, router_h[:, :]), (xh, router_l[:, :]), (xl, router_h[:, :])])
                return ins

            n2_turn(0, 0)
            with pe.Fori(0, G // 2 - 1) as it:
                for p in range(2):
                    n2_turn(it * 2 + (p + 1), 1 - p)
                    route(it * 2 + p, p)
            n2_turn(G - 1, 1)
            route(G - 2, 0)
            route(G - 1, 1).then_inc(logits_made, 1)

            pe.wait_ge(prep_done, 2)

            def turn_gates(g, p):
                cpad_ready.wait(pe, g + 1)
                if not (isinstance(g, int) and g < 1):
                    c_saved.wait(pe, g)
                for j in range(T):
                    ins = pe.transpose(bank(6).bitcast(fp16)[:, j * N:(j + 1) * N], cpad[:, p, j, :], ident16[:, :])
                ins.then_inc(c_turned.sem, 1)

            def up(g, k):
                n = g * E + k
                gelu_done.wait(pe, n - 1)
                e = k % E
                w = slice(e * D, (e + 1) * D)
                xh, xl = (tile(t, g, 1, GW) for t in (XTh, XTl))
                product(bank(k % 2), [(w1h[:, w], xh), (w1l[:, w], xh), (w1h[:, w], xl)]).then_inc(up_made.sem, 1)

            def spread(g, k, p):
                n = g * E + k
                hc_ready.wait(pe, n - 1)
                if k == 0:
                    c_saved.wait(pe, g + 1)
                pe.matmul(bank(2 + k % 2), selector[:, k, :], cT[:, p, :], start=True, stop=True).then_inc(cb_made.sem, 1)

            def down(g, k, p):
                n = g * E + k
                hl_ready.wait(pe, n + 1)
                if k == 0:
                    x2_saved.wait(pe, g - 1)
                w = slice(k * D, (k + 1) * D)
                for j in range(T):
                    s = slice(j * N, (j + 1) * N)
                    o = bank(4 + p)[:, s]
                    for i, (a, c) in enumerate(((hh, w2h), (hh, w2l), (hl, w2h))):
                        ins = pe.matmul(o, a[:, k % 4, s], c[:, w], start=(k == 0 and j == 0 and i == 0),
                                        stop=False, skip_group_check=True)
                ins.then_inc(down_made.sem, 1)
                if k == E - 1:
                    for j in range(T):
                        s = slice(j * N, (j + 1) * N)
                        ins = pe.matmul(bank(4 + p)[:, s], cT[:, p, s], b2w[:, :], start=False, stop=(j == T - 1),
                                        skip_group_check=True)
                    ins.then_inc(moe_made.sem, 1)

            LAG = 3

            def first_step(g, k, p, last=False):
                up(g, k)
                spread(g, k, p)
                if k == 1 and not last:
                    turn_gates(g + 1, 1 - p)

            turn_gates(0, 0)
            for k in range(E):
                first_step(0, k, 0)
                if k >= LAG:
                    down(0, k - LAG, 0)
            with pe.Fori(0, G // 2 - 1) as it:
                for q in range(2):
                    g = it * 2 + (q + 1)
                    p = (q + 1) % 2
                    for k in range(E):
                        first_step(g, k, p)
                        if k >= LAG:
                            down(g, k - LAG, p)
                        else:
                            down(g - 1, E + k - LAG, 1 - p)
            for k in range(E):
                first_step(G - 1, k, 1, last=True)
                if k >= LAG:
                    down(G - 1, k - LAG, 1)
                else:
                    down(G - 2, E + k - LAG, 0)
            for k in range(E - LAG, E):
                down(G - 1, k, 1)

            def n3_turn(g, p):
                n3_ready.wait(pe, g + 1)
                if not (isinstance(g, int) and g < 1):
                    n3l_saved.wait(pe, g)
                for j in range(T):
                    ins = pe.transpose(bank(0)[:, j * N:(j + 1) * N], XN[:, p, j * D:(j + 1) * D], ident[:, :])
                ins.then_inc(n3_turned.sem, 1)

            def g1_project(g, p):
                n3l_saved.wait(pe, g + 1)
                sig_ready.wait(pe, g - 1)
                h_saved.wait(pe, g - 1)
                th, tl = hh[:, p, :], hl[:, p, :]
                product(bank(1 + p), [(v1h[:, :], th), (v1l[:, :], th), (v1h[:, :], tl)])
                for j in range(T):
                    s = slice(j * N, (j + 1) * N)
                    product(bank(3 + p)[:, s], [(th[:, s], wTh[:, :]), (th[:, s], wTl[:, :]), (tl[:, s], wTh[:, :])])
                sums_read.wait(pe, g - 1)
                for j in range(T):
                    s = slice(j * N, (j + 1) * N)
                    ins = product(bank(5)[:, j:j + 1], [(th[:, s], v2h[:, :]), (th[:, s], v2l[:, :]), (tl[:, s], v2h[:, :])])
                ins.then_inc(proj_made.sem, 1)

            def g1_attend(g, p, last=False):
                att_ready.wait(pe, g + 1)
                h_saved.wait(pe, g + 1)
                u_saved.wait(pe, g - 1)
                for j in range(T):
                    s = slice(j * N, (j + 1) * N)
                    pe.matmul(bank(6 + p)[:, s], att[:, p, s], H[:, p, s], start=True, stop=True)
                if last:
                    sums_read.wait(pe, g)
                else:
                    s2_saved.wait(pe, g + 2)
                for j in range(T):
                    s = slice(j * N, (j + 1) * N)
                    ins = pe.matmul(bank(5)[:, 8 + j:9 + j], att[:, p, s], ones[:, 0:1], start=True, stop=True)
                ins.then_inc(att_used.sem, 1)

            n3_turn(0, 0)
            g1_project(0, 0)
            n3_turn(1, 1)
            with pe.Fori(0, G // 2 - 1) as it:
                for p in range(2):
                    g = it * 2 + p
                    g1_project(g + 1, 1 - p)
                    n3_turn(g + 2, p)
                    g1_attend(g, p)
            g1_project(G - 1, 1)
            g1_attend(G - 2, 0)
            g1_attend(G - 1, 1, last=True)

            sums_read.wait(pe, G)
            u_saved.wait(pe, G)
            with pe.Fori(0, G // 2) as it:
                for p in range(2):
                    g = it * 2 + p
                    n4_act.wait(pe, g + 1)
                    n4_dve.wait(pe, g + 1)
                    n4l_saved.wait(pe, g - 1)
                    for j in range(T):
                        pe.matmul(bank(5)[:, bass.ds(g * T + j, 1)], XN[:, p, j * D:(j + 1) * D], ones[:, 0:1],
                                  start=True, stop=True)
                    for j in range(T):
                        ins = pe.transpose(bank(6 + p)[:, j * N:(j + 1) * N], XN[:, p, j * D:(j + 1) * D], ident[:, :])
                    ins.then_inc(n4_turned.sem, 1)

            n4_turned.wait(pe, G)
            pe.sem_inc(route_pe, 1)
            pe.wait_ge(route_dve, 1)
            pe.matmul(bank(2)[0:B, 0:E], xsum[:, :], wr[:, :], start=True, stop=True).then_inc(route_pe, 1)
            pe.wait_ge(route_dve, 3)
            pe.matmul(bank(3)[0:B, 0:E], ones[0:B, 0:B], r[2][:, :], start=True, stop=True).then_inc(route_pe, 1)
            pe.wait_ge(route_dve, 6)
            pe.matmul(bank(2)[:, 0:4 * B], ones[0:B, :], diag[:, :, :].rearrange("p i b -> p (i b)"),
                      start=True, stop=True)
            n4l_saved.wait(pe, G)
            pe.transpose(bank(6)[0:E, 0:B], mix[:, 0, :], ident[0:B, 0:B]).then_inc(route_pe, 1)
            pe.wait_ge(route_dve, 7)
            pe.matmul(bank(7)[:, 0:D], mixT[:, :, :].rearrange("e k b -> e (k b)"), mb2[:, :],
                      start=True, stop=True).then_inc(route_pe, 1)
            pe.wait_ge(route_ready, 1)
            pe.wait_ge(late_low, 1)

            AHEAD = 2

            def experts(b, n):
                _, v = nc.values_load_multi_w_load_instructions(
                    index[0:1, bass.ds(b * 2, 2 * n)], engines=(mybir.EngineType.PE,), min_val=0, max_val=(E - 1) * F,
                    skip_runtime_bounds_check_because="the index of an expert's first column")
                return [(v[2 * i], v[2 * i + 1]) for i in range(n)]

            def ffn_up(b, k, es):
                g_ready.wait(pe, b - 1)
                s = slice(k % T * N, (k % T + 1) * N)
                xh, xl = hh[:, k // T % 2, s], hl[:, k // T % 2, s]
                for i, e in enumerate(es):
                    at = bass.ds(e, F)
                    ins = product(bank(k % 2)[:, i * F:(i + 1) * F], [(xh, m1h[:, at]), (xh, m1l[:, at]), (xl, m1h[:, at]),
                                                                      (two_ones[:, :], mb1[:, at])])
                ins.then_inc(f_made.sem, 1)

            def ffn_turn(b, k):
                g_ready.wait(pe, b + 1)
                hT_act.wait(pe, b - 1)
                hT_dve.wait(pe, b - 1)
                for i in range(2 * HALVES):
                    ins = pe.transpose(bank(2 + k % 2 * 2 + i // HALVES)[:, i % HALVES * N:(i % HALVES + 1) * N],
                                       h32[:, k % 4, i * N:(i + 1) * N], ident[:, :])
                ins.then_inc(h_turned.sem, 1)

            def ffn_down(b, k, es):
                hT_act.wait(pe, b + 1)
                hT_dve.wait(pe, b + 1)
                y_saved.wait(pe, b - 1)
                parts = [(hT[:, k % 4, (i * HALVES + h) * N:(i * HALVES + h + 1) * N], m2raw[:, bass.ds(e + h * D, D)])
                         for i, e in enumerate(es) for h in range(HALVES)]
                parts.append((pick[:, bass.ds(b, 1)].broadcast_to([128, N]), b2sum[:, :]))
                product(bank(6 + k % 2)[:, 0:D], parts).then_inc(y_made.sem, 1)

            first = experts(0, AHEAD)
            x_fetched.wait(pe, 1)
            ffn_up(0, 0, first[0])
            ffn_up(1, 1, first[1])
            ffn_turn(0, 0)
            pe.wait_ge(route_ready, 2)

            def group_round(it, q, last=False):
                es = experts(it * (2 * T) + q * T, T if last else T + AHEAD)
                for k in range(T):
                    if not (last and k >= T - AHEAD):
                        if k == T - AHEAD:
                            x_fetched.wait(pe, it * 2 + (q + 2))
                        ffn_up(it * (2 * T) + (q * T + k + AHEAD), q * T + k + AHEAD, es[k + AHEAD])
                    if not (last and k == T - 1):
                        ffn_turn(it * (2 * T) + (q * T + k + 1), k + 1)
                    ffn_down(it * (2 * T) + (q * T + k), k, es[k])

            with pe.Fori(0, B // (2 * T) - 1) as it:
                group_round(it, 0)
                group_round(it, 1)
            group_round(B // (2 * T) - 1, 0)
            group_round(B // (2 * T) - 1, 1, last=True)


_INS = ['x', 'adj', 'nodemask', 'L0_gnn_weight', 'L0_gnn_bias', 'L0_ffn_router_w', 'L0_ffn_w1', 'L0_ffn_b1',
        'L0_ffn_w2', 'L0_ffn_b2', 'L1_gnn_W', 'L1_gnn_b', 'L1_gnn_a1', 'L1_gnn_a2', 'L1_gnn_att_b', 'L1_ffn_Wr',
        'L1_ffn_br', 'L1_ffn_W1', 'L1_ffn_b1', 'L1_ffn_W2', 'L1_ffn_b2', 'L1_ffn_gamma', 'L1_ffn_beta']


def kernel(**inputs):
    import numpy as _np
    import concourse.bacc as _bacc
    from concourse import mybir as _mybir
    from concourse.bass_utils import run_bass_kernel_spmd as _run

    nc = _bacc.Bacc("TRN2", target_bir_lowering=False, num_devices=1)
    arrays, args = {}, []
    for name in _INS:
        a = _np.ascontiguousarray(inputs[name])
        if a.ndim == 0:
            a = a.reshape(1)
        arrays[f"in_{name}"] = a
        args.append(nc.dram_tensor(f"in_{name}", a.shape, _mybir.dt.from_np(a.dtype), kind="ExternalInput").ap())
    shape = arrays["in_x"].shape
    args.append(nc.dram_tensor("out_dram", shape, _mybir.dt.float32, kind="ExternalOutput").ap())
    graph_network(nc, *args)
    r = _run(nc, [arrays], core_ids=[0])
    return r.results[0]["out_dram"]
```

```python
import concourse.bass as bass
from concourse import mybir
from contextlib import ExitStack

fp32 = mybir.dt.float32
fp16 = mybir.dt.float16
int32 = mybir.dt.int32
ALU = mybir.AluOpType
ACT = mybir.ActivationFunctionType
AX = mybir.AxisListType


class Count:

    def __init__(self, sem, free=0):
        self.sem, self.free = sem, free

    def wait(self, eng, n):
        eng.wait_ge(self.sem, n + self.free)


class Chain:

    def __init__(self, eng, sem, base=0):
        self.eng, self.sem, self.base, self.n = eng, sem, base, 0

    def __call__(self, ins):
        self.n += 1
        ins.then_inc(self.sem, 1)
        self.eng.wait_ge(self.sem, self.base + self.n)


def graph_network(nc, x, adj, nodemask, g0_w, g0_b, f0_router, f0_w1, f0_b1, f0_w2, f0_b2,
                  g1_w, g1_b, g1_a1, g1_a2, g1_attb, f1_wr, f1_br, f1_w1, f1_b1, f1_w2, f1_b2,
                  gamma, beta, out):
    B, N, D = x.shape
    E = f0_router.shape[0]
    F = f1_w1.shape[2]
    HALVES = F // D
    T = 4
    GW = T * N
    G = B // T
    CAPACITY = float(-(-B * N * 5 // (4 * E)))
    EPS = 1e-5
    WS = 64.0
    BIG = -3.0e38

    ctx = ExitStack()
    with ctx:
        def sb(name, shape, dt=fp32):
            return ctx.enter_context(nc.sbuf_tensor(name, shape, dt))

        credits = []

        def count(name, free=0):
            c = Count(ctx.enter_context(nc.semaphore(name)), free)
            if free:
                credits.append(c)
            return c

        def sem(name):
            return ctx.enter_context(nc.semaphore(name))

        X = sb("X", [128, B * D])
        adjT = sb("adjT", [128, B * N])
        XTh = sb("XTh", [128, B * N], fp16)
        XTl = sb("XTl", [128, B * N], fp16)
        adj_in = sb("adj_in", [128, 4, GW])
        XN = sb("XN", [128, 2, GW])
        ZT = sb("ZT", [128, 2, GW])

        stats = sb("stats", [128, B, 6])
        rstd = sb("rstd", [128, B])
        nmr = sb("nmr", [128, B])
        ln_a = sb("ln_a", [128, B])
        ln_b = sb("ln_b", [128, B])
        ln_c = sb("ln_c", [128, B])

        ident = sb("ident", [128, 128])
        ident16 = sb("ident16", [128, 128], fp16)
        ones = sb("ones", [128, 128])
        selector = sb("selector", [128, E, 128], fp16)
        pair = sb("pair", [128, E])
        rank = sb("rank", [128, E])
        two_ones = sb("two_ones", [128, 128], fp16)
        rows_in = sb("rows_in", [128, 128])
        cols = sb("cols", [128, 128])
        g0w = sb("g0w", [128, D])
        g0b = sb("g0b", [128, D])
        g1w = sb("g1w", [128, D])
        g1b = sb("g1b", [128, D])
        avec = sb("avec", [128, 3])
        attb = sb("attb", [128, 1])
        wr = sb("wr", [128, E])
        br = sb("br", [B, E])
        gam = sb("gam", [128, D])
        bet = sb("bet", [128, D])
        epst = sb("epst", [128, 1])
        router = sb("router", [128, 2 * E], fp16)
        raw = sb("raw", [128, 2 * E * D + 2 * E * F])
        w1raw = raw[:, 0:E * D]
        w2raw = raw[:, E * D:2 * E * D]
        m1raw = raw[:, 2 * E * D:2 * E * D + E * F]
        m2raw = raw[:, 2 * E * D + E * F:]
        w1h, w1l = sb("w1h", [128, E * D], fp16), sb("w1l", [128, E * D], fp16)
        w2h, w2l = sb("w2h", [128, E * D], fp16), sb("w2l", [128, E * D], fp16)
        m1h, m1l = sb("m1h", [128, E * F], fp16), sb("m1l", [128, E * F], fp16)
        b2raw = sb("b2raw", [128, D])
        b2w = sb("b2w", [128, D], fp16)
        b2t = sb("b2t", [128, D], fp16)
        mb1raw = XTl[:, :].bitcast(fp32)[0:64, E * D:E * D + E * F]
        mb1 = sb("mb1", [128, E * F], fp16)
        mb2 = sb("mb2", [E, D])
        mbt = XTh[0:64, 0:E * F]
        wTh, wTl = sb("wTh", [128, D], fp16), sb("wTl", [128, D], fp16)
        v12 = sb("v12", [128, 2])
        v1h, v1l = sb("v1h", [128, 128], fp16), sb("v1l", [128, 128], fp16)
        v2h, v2l = sb("v2h", [128, 128], fp16), sb("v2l", [128, 128], fp16)
        att_const = sb("att_const", [128, 1])

        lg = [ZT[:, 0, :], sb("gates", [128, B * E]), ZT[:, 1, :], adj_in[:, 3, :]]
        small = [sb(f"small{i}", [128, B]) for i in range(4)]
        cpad = sb("cpad", [128, 2, T, 128], fp16)
        cT = sb("cT", [128, 2, GW], fp16)
        h32 = adj_in
        hc32 = ZT
        hh = sb("hh", [128, 4, GW], fp16)
        hl = sb("hl", [128, 4, GW], fp16)

        def in_raw(k, n=2):
            return raw[:, k * GW:(k + n) * GW].rearrange("p (a c) -> p a c", a=n)
        sig, att = in_raw(0), in_raw(2)
        H = raw[:, 4 * GW:4 * GW + 2 * T * (D + 1)].rearrange("p (a t d) -> p a t d", a=2, t=T)
        g1b_rows = sb("g1b_rows", [128, T, D], fp16)
        mask2 = sb("mask2", [128, B])
        frac = sb("frac", [128, 2, 2 * T])
        xsum = sb("xsum", [128, B])

        r = [sb(f"r{i}", [B, E]) for i in range(4)]
        rc = [sb(f"rc{i}", [B, 1]) for i in range(8)]
        diag = sb("diag", [B, 4, B])
        gate = sb("gate", [128, 4, B])
        index = sb("index", [128, 2 * B], int32)
        mix = sb("mix", [B, 2, E])
        mixT = sb("mixT", [E, 2, B])
        b2sum = sb("b2sum", [128, D], fp16)
        b2high = sb("b2high", [128, D], fp16)
        pick = sb("pick", [128, B], fp16)
        hT = sb("hT", [128, 4, 2 * F])
        wT_scaled = hT[:, 0, 0:D]
        U = hT

        PS = ctx.enter_context(nc.psum_tensor("PS", [128, 8, 512], fp32))

        def bank(i):
            return PS[:, i, :]

        logits = PS[:, 6:8, :].rearrange("p a c -> p (a c)")

        def first_three(t):
            return t[:, 0:(T - 1) * (D + 1)].rearrange("p (t d) -> p t d", t=T - 1)

        def tile(t, b, n=1, w=128):
            return t[:, bass.ds(b * w, n * w)]

        vec = sem("vec_own")
        scl = sem("act_own")
        pool = sem("pool_own")
        g0_loaded = sem("g0_loaded")
        weights_loaded = sem("weights_loaded")
        b1_loaded = sem("b1_loaded")
        late_loaded = sem("late_loaded")
        big_loaded = sem("big_loaded")
        split_high = sem("split_high")
        split_low = sem("split_low")
        ident_made = sem("ident_made")
        prep_pe = sem("prep_pe")
        prep_hi = sem("prep_hi")
        prep_done = sem("prep_done")
        group_loaded = [sem(f"group_loaded{q}") for q in range(4)]
        adj_turned = count("adj_turned", 4)
        adjT_saved = count("adjT_saved", 2)
        moments = sem("moments")
        sqrt_done = sem("sqrt_done")
        ln_ready = sem("ln_ready")
        x_loaded = [sem(f"x_loaded{c}") for c in range(4)]
        xn_act = count("xn_act")
        xn_dve = count("xn_dve")
        z_made = count("z_made", 2)
        z_saved = count("z_saved", 2)
        bias_added = count("bias_added")
        o_made = count("o_made", 2)
        x1_saved = count("x1_saved", 2)
        n2_act = count("n2_act")
        n2_dve = count("n2_dve")
        n2_turned = count("n2_turned", 2)
        n2h_saved = count("n2h_saved")
        n2l_saved = count("n2l_saved", 2)
        n2_added = count("n2_added", 2)
        adj_masked = sem("adj_masked")
        logits_made = sem("logits_made")
        exp_in = sem("exp_in")
        exp_out = sem("exp_out")
        cpad_ready = count("cpad_ready")
        c_turned = count("c_turned", 2)
        c_saved = count("c_saved")
        up_made = count("up_made")
        gelu_done = count("gelu_done", 2)
        cb_made = count("cb_made")
        hc_ready = count("hc_ready", 2)
        hh_ready = count("hh_ready", 2)
        hl_ready = count("hl_ready", 2)
        down_made = count("down_made", 4)
        moe_made = count("moe_made")
        x2_saved = count("x2_saved", 2)
        n3_ready = count("n3_ready")
        n3_dve = sem("n3_dve")
        n3_turned = count("n3_turned", 2)
        n3h_saved = count("n3h_saved")
        n3l_saved = count("n3l_saved")
        ones_made = sem("ones_made")
        scores_made = count("scores_made")
        proj_made = count("proj_made")
        last_read = count("last_read")
        h_saved = count("h_saved", 2)
        sig_ready = count("sig_ready", 2)
        att_ready = count("att_ready", 2)
        att_used = count("att_used", 2)
        u_saved = count("u_saved", 2)
        x3_ready = count("x3_ready", 2)
        n4_act = count("n4_act")
        n4_dve = count("n4_dve")
        n4_turned = count("n4_turned", 2)
        n4_kept = count("n4_kept", 2)
        n4h_saved = count("n4h_saved")
        n4l_saved = count("n4l_saved", 2)
        route_pe = sem("route_pe")
        route_dve = sem("route_dve")
        route_act = sem("route_act")
        route_ready = sem("route_ready")
        f_made = count("f_made", 4)
        z_moments = sem("z_moments")
        z_sqrt = sem("z_sqrt")
        z_ln = sem("z_ln")
        x_fetched = count("x_fetched")
        g_ready = count("g_ready", 2)
        h_turned = count("h_turned", 4)
        hT_act = count("hT_act", 2)
        hT_dve = count("hT_dve", 2)
        y_made = count("y_made", 4)
        y_saved = count("y_saved", 2)
        norm_ready = count("norm_ready")
        xb_ready = count("xb_ready")
        out_ready = count("out_ready")
        stored = [count(f"stored{q}", 16) for q in range(2)]

        X_CHUNKS = (0, 1, G // 4, G // 2 + 1, G)
        MOST, LAST = slice(0, B - 2 * T), slice(B - 2 * T, B)
        CG = 4
        CB = CG * T
        CHUNKS = B // CB

        block = ctx.enter_context(nc.Block())

        @block.sync
        def _(sp):
            for c, (lo, hi) in enumerate(zip(X_CHUNKS, X_CHUNKS[1:])):
                sp.dma_start(X[:, lo * GW:hi * GW].rearrange("p (b d) -> p b d", b=(hi - lo) * T),
                             x[lo * T:hi * T, :, :].rearrange("b p d -> p b d")).then_inc(x_loaded[c], 16)
            for c in credits:
                sp.sem_inc(c.sem, c.free)
            with sp.Fori(0, G // 4) as it:
                for q in range(4):
                    g = it * 4 + q
                    adj_turned.wait(sp, it * 4 + (q - 3))
                    sp.dma_start(adj_in[:, q, :].rearrange("p (t d) -> p t d", t=T),
                                 adj[bass.ds(g * T, T), :, :].rearrange("t p d -> p t d")).then_inc(group_loaded[q], 16)

            def load(dst, src):
                sp.dma_start(dst, src).then_inc(weights_loaded, 16)

            load(g1w[:, :], g1_w)
            load(avec[:, 0:1], g1_a1.rearrange("(d o) -> d o", o=1))
            load(avec[:, 1:2], g1_a2.rearrange("(d o) -> d o", o=1))
            load(avec[:, 2:3], g1_b.rearrange("(d o) -> d o", o=1))
            load(attb[:, :], g1_attb.partition_broadcast(128))
            load(g1b[:, :], g1_b.partition_broadcast(128))
            for q in (0, 32, 64):
                load(b2raw[q:q + E, :], f0_b2)
            for dst, src in (
                    (w1raw.rearrange("p (e f) -> p e f", e=E), f0_w1.rearrange("e d f -> d e f")),
                    (w2raw.rearrange("p (e f) -> p e f", e=E), f0_w2.rearrange("e f d -> f e d")),
                    (m1raw.rearrange("p (e f) -> p e f", e=E), f1_w1.rearrange("e d f -> d e f")),
                    (m2raw.rearrange("p (e h d) -> p e h d", e=E, h=HALVES),
                     f1_w2.rearrange("e (h p) d -> p e h d", p=128))):
                sp.dma_start(dst, src).then_inc(big_loaded, 16)

            with sp.Fori(0, G // 2) as it:
                for p in range(2):
                    g = it * 2 + p
                    out_ready.wait(sp, g + 1)
                    sp.dma_start(out[bass.ds(g * T, T), :, :].rearrange("t p d -> p t d"),
                                 tile(X, g, 1, GW).rearrange("p (t d) -> p t d", t=T)).then_inc(stored[p].sem, 16)
            for p in range(2):
                stored[p].wait(sp, 16 * (G // 2))

        G0_LOADS, B1_LOADS, SMALL, LATE, BIG_LOADS = 16 * 2, 16 * 2, 16 * (9 + 3), 16 * 5, 16 * 4

        @block.gpsimd
        def _(g_):
            own = Chain(g_, pool)
            own(g_.memset(ident[:, :], 0.0))
            own(g_.affine_select(out=ident[:, :], in_=ident[:, :], compare_op=ALU.not_equal, fill=1.0,
                                 base=0, pattern=[[-1, 128]], channel_multiplier=1))
            own(g_.memset(ones[:, :], 1.0))
            own(g_.memset(epst[:, :], EPS))
            own(g_.memset(two_ones[:, :], 0.0))
            own(g_.memset(two_ones[0:1, :], 1.0))
            own(g_.memset(two_ones[32:33, :], 1.0))
            own(g_.memset(b2w[:, :], 0.0))
            own(g_.memset(mb1[:, :], 0.0))
            own(g_.memset(cpad[:, :, :, :], 0.0))
            for e in range(E):
                own(g_.memset(rank[:, e:e + 1], float(E - e)))
            own(g_.tensor_tensor(pair[:, :], ident[:, 0:E], ident[:, 32:32 + E], ALU.add))
            g_.sem_inc(ident_made, 1)

            def add_row(g, row):
                return g_.tensor_tensor(tile(X, g, 1, GW).rearrange("p (t d) -> p t d", t=T),
                                        tile(X, g, 1, GW).rearrange("p (t d) -> p t d", t=T),
                                        row[:, :].unsqueeze(1).broadcast_to([128, T, D]), ALU.add)

            def low(dst, src, high):
                own(g_.tensor_scalar(src, src, WS, None, ALU.mult))
                own(g_.tensor_tensor(dst, src, high, ALU.subtract))
                g_.sem_inc(split_low, 1)

            g_.wait_ge(split_high, 1)
            low(mb1[32:33, :], mb1raw[32:33, :], mbt[32:33, :])
            g_.wait_ge(g0_loaded, G0_LOADS)
            with g_.Fori(0, G // 2) as it:
                for p in range(2):
                    g = it * 2 + p
                    xn_act.wait(g_, g + 1)
                    xn_dve.wait(g_, g + 1)
                    add_row(g, g0b).then_inc(bias_added.sem, 1)
            with g_.Fori(0, G // 2) as it:
                for p in range(2):
                    g = it * 2 + p
                    n2_act.wait(g_, g + 1)
                    n2_dve.wait(g_, g + 1)
                    g_.tensor_tensor(tile(X, g, 1, GW), tile(X, g, 1, GW), XN[:, p, :], ALU.add).then_inc(n2_added.sem, 1)
            g_.wait_ge(split_high, 2)
            low(w1l[:, :], w1raw, w1h[:, :])
            g_.wait_ge(split_high, 3)
            low(w2l[:, :], w2raw, w2h[:, :])
            with g_.Fori(0, G * E // 8) as it:
                for k in range(8):
                    n = it * 8 + k
                    hh_ready.wait(g_, n + 1)
                    down_made.wait(g_, n - 3)
                    g_.tensor_tensor(hl[:, k % 4, :], hc32[:, k % 2, :], hh[:, k % 4, :],
                                     ALU.subtract).then_inc(hl_ready.sem, 1)
            def attend(g, p):
                sig_ready.wait(g_, g + 1)
                att_used.wait(g_, g - 1)
                g_.tensor_tensor(att[:, p, :], sig[:, p, :], tile(adjT, g, 1, GW), ALU.mult).then_inc(att_ready.sem, 1)

            def residual(g, p):
                u_saved.wait(g_, g + 1)
                g_.tensor_tensor(tile(X, g, 1, GW), U[:, p, :], tile(X, g, 1, GW), ALU.add).then_inc(x3_ready.sem, 1)

            g_.wait_ge(adj_masked, G)
            g_.memset(H[:, :, :, D:D + 1], 1.0).then_inc(ones_made, 1)
            attend(0, 0)
            with g_.Fori(0, G // 2 - 1) as it:
                for p in range(2):
                    attend(it * 2 + (p + 1), 1 - p)
                    residual(it * 2 + p, p)
            attend(G - 1, 1)
            residual(G - 2, 0)
            residual(G - 1, 1)
            g_.wait_ge(late_loaded, LATE)
            with g_.Fori(0, G // 2) as it:
                for p in range(2):
                    g = it * 2 + p
                    n4_act.wait(g_, g + 1)
                    n4_dve.wait(g_, g + 1)
                    add_row(g, bet).then_inc(xb_ready.sem, 1)
            def fetch(g, p):
                n4l_saved.wait(g_, g + 1)
                f_made.wait(g_, (g - 1) * T)
                for dst, src in ((hh, XTh), (hl, XTl)):
                    ins = g_.tensor_copy(dst[:, p, :], tile(src, g, 1, GW))
                ins.then_inc(x_fetched.sem, 1)

            with g_.Fori(0, G // 2) as it:
                for p in range(2):
                    fetch(it * 2 + p, p)

        @block.scalar
        def _(act):
            own = Chain(act, scl)

            def load(dst, src, loaded=weights_loaded):
                act.dma_start(dst, src).then_inc(loaded, 16)

            for q in (0, 32):
                load(mb1raw[q:q + 1, :], f1_b1.rearrange("(o e) f -> o (e f)", o=1), b1_loaded)
            load(g0w[:, :], g0_w, g0_loaded)
            load(g0b[:, :], g0_b.partition_broadcast(128), g0_loaded)
            load(rows_in[0:B, :], nodemask)
            load(rows_in[B:B + E, :], f0_router)
            load(rows_in[B + E:B + 2 * E, :], f0_b1)
            load(gam[:, :], gamma.partition_broadcast(128), late_loaded)
            load(bet[:, :], beta.partition_broadcast(128), late_loaded)
            load(wr[:, :], f1_wr, late_loaded)
            load(br[:, :], f1_br.partition_broadcast(B), late_loaded)
            load(mb2[:, :], f1_b2, late_loaded)

            def sqrt(k, at=slice(0, B)):
                act.wait_ge(moments, k)
                act.activation(ln_a[:, at], ln_c[:, at], ACT.Sqrt, bias=epst[:, :]).then_inc(sqrt_done, 1)

            def norm(dst, g, ready, rows=range(T)):
                for j in rows:
                    ins = act.activation(dst[:, j * D:(j + 1) * D], X[:, bass.ds(g * GW + j * D, D)], ACT.Identity,
                                         bias=nmr[:, bass.ds(g * T + j, 1)], scale=rstd[:, bass.ds(g * T + j, 1)])
                ins.then_inc(ready.sem, 1)

            def highs(*pairs):
                for dst, src in pairs:
                    own(act.activation(dst, src, ACT.Copy, scale=WS))
                act.sem_inc(split_high, 1)

            act.wait_ge(ident_made, 1)
            act.wait_ge(b1_loaded, B1_LOADS)
            highs((mb1[0:1, :], mb1raw[0:1, :]), (mbt[32:33, :], mb1raw[32:33, :]))
            sqrt(1)
            act.wait_ge(ln_ready, 1)

            def save_adj(g, q):
                adj_turned.wait(act, g + 1)
                act.activation(tile(adjT, g, 1, GW), bank(q % 2), ACT.Copy).then_inc(adjT_saved.sem, 1)

            def save_z(g, p):
                z_made.wait(act, g + 1)
                o_made.wait(act, g - 1)
                act.activation(ZT[:, p, :], bank(2 + p), ACT.Copy).then_inc(z_saved.sem, 1)

            def n1_norm(g, p):
                z_made.wait(act, g - 1)
                norm(XN[:, p, :], g, xn_act, (0, 1, 2))

            def g0_step(g, q):
                if not (isinstance(g, int) and g + 2 >= G):
                    n1_norm(g + 2, q % 2)
                if not (isinstance(g, int) and g + 1 >= G):
                    save_z(g + 1, (q + 1) % 2)
                if not (isinstance(g, int) and g + 2 >= G):
                    save_adj(g + 2, q + 2)

            n1_norm(0, 0)
            save_adj(0, 0)
            save_adj(1, 1)
            n1_norm(1, 1)
            save_z(0, 0)
            with act.Fori(0, G // 4 - 1) as it:
                for q in range(4):
                    g0_step(it * 4 + q, q)
            for q in range(4):
                g0_step(G - 4 + q, q)

            act.wait_ge(weights_loaded, SMALL)
            own(act.activation(ident16[:, :], ident[:, :], ACT.Copy))
            act.wait_ge(prep_pe, 1)
            own(act.activation(cols[:, 0:B + 2 * E], bank(6)[:, 0:B + 2 * E], ACT.Copy))
            own(act.activation(wT_scaled, bank(6)[:, 128:256], ACT.Copy, scale=WS))
            own(act.activation(wTh[:, :], bank(6)[:, 128:256], ACT.Copy, scale=WS))
            own(act.activation(v12[:, :], bank(6)[:, 256:258], ACT.Copy, scale=WS))
            own(act.activation(v1h[:, :], v12[:, 0:1].broadcast_to([128, 128]), ACT.Copy))
            own(act.activation(v2h[:, :], v12[:, 1:2].broadcast_to([128, 128]), ACT.Copy))
            own(act.activation(router[:, 0:E], cols[:, B:B + E], ACT.Copy, scale=WS))
            own(act.activation(att_const[:, :], bank(6)[:, 258:259], ACT.Identity, bias=attb[:, :]))
            act.sem_inc(prep_hi, 1)

            act.wait_ge(split_low, 1)
            sqrt(2)
            act.wait_ge(ln_ready, 2)

            def n2_norm(g, p):
                n2_turned.wait(act, g - 1)
                n2_added.wait(act, g - 1)
                norm(XN[:, p, :], g, n2_act, (0, 1))

            def n2_high(g, p):
                n2_turned.wait(act, g + 1)
                act.activation(tile(XTh, g, 1, GW), bank(p), ACT.Copy).then_inc(n2h_saved.sem, 1)

            n2_norm(0, 0)
            with act.Fori(0, G // 4 - 1) as it:
                for q in range(4):
                    n2_norm(it * 4 + (q + 1), (q + 1) % 2)
                    n2_high(it * 4 + q, q % 2)
            for g in (G - 4, G - 3):
                n2_norm(g + 1, (g + 1) % 2)
                n2_high(g, g % 2)
            n2_norm(G - 1, 1)
            n2_high(G - 2, 0)
            n2_high(G - 1, 1)

            act.wait_ge(big_loaded, BIG_LOADS)
            highs((w1h[:, :], w1raw))
            highs((w2h[:, :], w2raw), (b2w[0:E, :], b2raw[0:E, :]), (b2w[32:32 + E, :], b2raw[32:32 + E, :]),
                  (b2t[64:64 + E, :], b2raw[64:64 + E, :]))
            own(act.activation(g1b_rows[:, :, :], g1b[:, :].unsqueeze(1).broadcast_to([128, T, D]), ACT.Copy, scale=WS))
            own(act.activation(selector[:, :, :], pair[:, :].unsqueeze(2).broadcast_to([128, E, 128]), ACT.Copy))
            highs((m1h[:, :], m1raw))
            act.wait_ge(exp_in, 1)
            act.activation(small[3][:, :], small[1][:, :], ACT.Exp, scale=1.0 / WS).then_inc(exp_out, 1)

            def gelu(n, k):
                up_made.wait(act, n + 1)
                hc_ready.wait(act, n - 1)
                act.activation(h32[:, k % 2, :], bank(k % 2), ACT.Gelu, bias=cols[:, B + E + k % E:B + E + k % E + 1],
                               scale=1.0 / WS).then_inc(gelu_done.sem, 1)

            def high(n, k):
                hc_ready.wait(act, n + 1)
                down_made.wait(act, n - 3)
                act.activation(hh[:, k % 4, :], hc32[:, k % 2, :], ACT.Copy).then_inc(hh_ready.sem, 1)

            gelu(0, 0)
            for k in range(E):
                gelu(k + 1, (k + 1) % E)
                high(k, k)
            with act.Fori(1, G - 1) as it:
                for k in range(E):
                    gelu(it * E + (k + 1), (k + 1) % E)
                    high(it * E + k, k)
            for k in range(E):
                if k < E - 1:
                    gelu((G - 1) * E + k + 1, k + 1)
                high((G - 1) * E + k, k)
                if k == 3:
                    sqrt(3, MOST)

            act.wait_ge(ln_ready, 3)

            def n3_norm(g, p):
                n3_turned.wait(act, g - 1)
                norm(XN[:, p, :], g, n3_ready)

            def n3_high(g, p):
                n3_turned.wait(act, g + 1)
                act.activation(hh[:, p, :], bank(0), ACT.Copy).then_inc(n3h_saved.sem, 1)

            def sigmoid(g, p):
                scores_made.wait(act, g + 1)
                att_ready.wait(act, g - 1)
                act.activation(sig[:, p, :], bank(1 + p), ACT.Sigmoid, bias=att_const[:, 0:1],
                               scale=1.0 / WS).then_inc(sig_ready.sem, 1)

            def save_h(g, p):
                proj_made.wait(act, g + 1)
                att_used.wait(act, g - 1)
                act.activation(H[:, p, :, 0:D], bank(3 + p).rearrange("p (t d) -> p t d", t=T), ACT.Copy,
                               scale=1.0 / WS).then_inc(h_saved.sem, 1)

            n3_norm(0, 0)
            n3_high(0, 0)
            act.wait_ge(n3_dve, 1)
            act.sem_inc(n3_ready.sem, 1)
            n3_norm(2, 0)
            sqrt(4, LAST)
            sigmoid(0, 0)
            n3_high(1, 1)
            save_h(0, 0)
            n3_norm(3, 1)
            act.wait_ge(ln_ready, 4)
            with act.Fori(0, G // 2 - 2) as it:
                for p in range(2):
                    g = it * 2 + p
                    n3_high(g + 2, p)
                    sigmoid(g + 1, 1 - p)
                    n3_norm(g + 4, p)
                    save_h(g + 1, 1 - p)
            n3_high(G - 2, 0)
            sigmoid(G - 3, 1)
            save_h(G - 3, 1)
            n3_high(G - 1, 1)
            sigmoid(G - 2, 0)
            save_h(G - 2, 0)
            sigmoid(G - 1, 1)
            save_h(G - 1, 1)

            sqrt(5)
            act.wait_ge(ln_ready, 5)

            def n4_norm(g, p):
                n4_turned.wait(act, g - 1)
                n4_kept.wait(act, g - 1)
                norm(XN[:, p, :], g, n4_act, (0, 1, 2))

            def n4_high(g, p):
                n4_turned.wait(act, g + 1)
                act.activation(tile(XTh, g, 1, GW), bank(6 + p), ACT.Copy).then_inc(n4h_saved.sem, 1)

            n4_norm(0, 0)
            with act.Fori(0, G // 2 - 1) as it:
                for p in range(2):
                    n4_norm(it * 2 + (p + 1), 1 - p)
                    n4_high(it * 2 + p, p)
            n4_norm(G - 1, 1)
            n4_high(G - 2, 0)
            n4_high(G - 1, 1)

            act.wait_ge(route_dve, 2)
            act.activation(r[1][:, :], r[1][:, :], ACT.Exp).then_inc(route_act, 1)
            act.wait_ge(route_dve, 4)
            act.activation(r[1][:, :], r[1][:, :], ACT.Exp).then_inc(route_act, 1)
            act.wait_ge(route_dve, 5)
            act.activation(rc[5][:, :], rc[5][:, :], ACT.Exp).then_inc(route_act, 1)

            def gelu2(b, k):
                f_made.wait(act, b + 1)
                h_turned.wait(act, b - 3)
                act.activation(h32[:, k % 4, :], bank(k % 2), ACT.Gelu, scale=1.0 / WS).then_inc(g_ready.sem, 1)

            def gated(b, k):
                h_turned.wait(act, b + 1)
                y_made.wait(act, b - 3)
                act.activation(hT[:, k % 4, F:2 * F], bank(3 + k % 2 * 2)[:, 0:F], ACT.Copy,
                               scale=gate[:, 1, bass.ds(b, 1)]).then_inc(hT_act.sem, 1)

            def z_norm(b):
                z = tile(adjT, b)
                act.activation(z, z, ACT.Identity, bias=nmr[:, bass.ds(b, 1)],
                               scale=rstd[:, bass.ds(b, 1)]).then_inc(norm_ready.sem, 1)

            def z_root(c):
                act.wait_ge(z_moments, c + 1)
                at = bass.ds(c * CB, CB)
                act.activation(ln_a[:, at], ln_c[:, at], ACT.Sqrt, bias=epst[:, :]).then_inc(z_sqrt, 1)

            def chunk(c, first=False, last=False):
                for i in range(CG):
                    for k in range(T):
                        b = c * CB + (i * T + k)
                        if not (last and i == CG - 1 and k >= T - 2):
                            gelu2(b + 2, k + 2)
                        if not (last and i == CG - 1 and k == T - 1):
                            gated(b + 1, k + 1)
                        if first:
                            continue
                        if i == 0 and k == 0:
                            z_root(c - 1)
                        if i == 1 and k == 0:
                            act.wait_ge(z_ln, c)
                        if i in (1, 2):
                            for j in range(2):
                                z_norm(c * CB + (((i - 1) * T + k) * 2 + j - CB))

            gelu2(0, 0)
            gelu2(1, 1)
            gated(0, 0)
            chunk(0, first=True)
            with act.Fori(1, CHUNKS - 1) as c:
                chunk(c)
            chunk(CHUNKS - 1, last=True)
            z_root(CHUNKS - 1)
            act.wait_ge(z_ln, CHUNKS)
            for i in range(CB):
                z_norm(B - CB + i)

        @block.vector
        def _(dve):
            own = Chain(dve, vec)

            def low(dst, src, high_part):
                own(dve.scalar_tensor_tensor(dst, src, WS, high_part, ALU.mult, ALU.subtract))

            def begin_finish(at=slice(0, B)):
                me, qe, mo, qo = (stats[:, at, i] for i in (1, 2, 4, 5))
                own(dve.tensor_tensor(ln_b[:, at], me, mo, ALU.subtract))
                own(dve.tensor_tensor(ln_c[:, at], qe, qo, ALU.add))
                own(dve.scalar_tensor_tensor(ln_b[:, at], ln_b[:, at], 0.25, ln_b[:, at], ALU.mult, ALU.mult))
                own(dve.scalar_tensor_tensor(ln_c[:, at], ln_c[:, at], 1.0 / D, ln_b[:, at], ALU.mult, ALU.add))
                dve.sem_inc(moments, 1)
                own(dve.tensor_tensor(ln_b[:, at], me, mo, ALU.add))

            def end_finish(k, at=slice(0, B)):
                dve.wait_ge(sqrt_done, k)
                own(dve.reciprocal(rstd[:, at], ln_a[:, at]))
                own(dve.scalar_tensor_tensor(nmr[:, at], ln_b[:, at], -0.5, rstd[:, at], ALU.mult, ALU.mult))
                dve.sem_inc(ln_ready, 1)

            def finish_stats(k):
                begin_finish()
                end_finish(k)

            def group_stats(g, rows=range(T)):
                for j in rows:
                    ins = dve.bn_stats(stats[:, bass.ds(g * T + j, 1), :], tile(X, g * T + j))
                return ins

            own_stats = sem("group_stats")
            done_stats = 0
            for c, (lo, hi) in enumerate(zip(X_CHUNKS, X_CHUNKS[1:])):
                dve.wait_ge(x_loaded[c], 16)
                for g in range(lo, hi):
                    group_stats(g).then_inc(own_stats, 1)
            done_stats += G
            dve.wait_ge(own_stats, done_stats)
            finish_stats(1)

            def norm(g, p, ready, rows=(2, 3)):
                for j in rows:
                    ins = dve.tensor_scalar(XN[:, p, j * D:(j + 1) * D], X[:, bass.ds(g * GW + j * D, D)],
                                            rstd[:, bass.ds(g * T + j, 1)], nmr[:, bass.ds(g * T + j, 1)],
                                            ALU.mult, ALU.add)
                return ins.then_inc(ready.sem, 1) if ready else ins

            def n1_norm(g, p):
                z_made.wait(dve, g - 1)
                norm(g, p, xn_dve, (3,))

            def n1_add(g, p):
                o_made.wait(dve, g + 1)
                bias_added.wait(dve, g + 1)
                dve.tensor_tensor(tile(X, g, 1, GW), bank(4 + p), tile(X, g, 1, GW), ALU.add).then_inc(x1_saved.sem, 1)

            def n1_stats(g):
                x1_saved.wait(dve, g + 1)
                group_stats(g).then_inc(own_stats, 1)

            n1_norm(0, 0)
            n1_norm(1, 1)
            n1_norm(2, 0)
            n1_add(0, 0)
            n1_norm(3, 1)
            n1_stats(0)
            n1_add(1, 1)
            with dve.Fori(1, G // 2 - 1) as it:
                for p in range(2):
                    n1_norm(it * 2 + (p + 2), p)
                    n1_stats(it * 2 + (p - 1))
                    n1_add(it * 2 + p, p)
            for g in (G - 2, G - 1):
                n1_stats(g - 1)
                n1_add(g, g % 2)
            n1_stats(G - 1)
            done_stats += G
            dve.wait_ge(own_stats, done_stats)
            finish_stats(2)

            def n2_norm(g, p):
                n2_turned.wait(dve, g - 1)
                n2_added.wait(dve, g - 1)
                norm(g, p, n2_dve)

            def n2_low(g, p):
                n2h_saved.wait(dve, g + 1)
                dve.tensor_tensor(tile(XTl, g, 1, GW), bank(p), tile(XTh, g, 1, GW),
                                  ALU.subtract).then_inc(n2l_saved.sem, 1)

            n2_norm(0, 0)
            dve.wait_ge(prep_hi, 1)
            low(router[:, E:2 * E], cols[:, B:B + E], router[:, 0:E])
            dve.sem_inc(prep_done, 1)
            with dve.Fori(0, G // 4 - 1) as it:
                for q in range(4):
                    n2_norm(it * 4 + (q + 1), (q + 1) % 2)
                    n2_low(it * 4 + q, q % 2)
            for g in (G - 4, G - 3):
                n2_norm(g + 1, (g + 1) % 2)
                n2_low(g, g % 2)
            n2_norm(G - 1, 1)
            n2_low(G - 2, 0)
            n2_low(G - 1, 1)

            dve.wait_ge(logits_made, 1)

            def v3(t):
                return t.rearrange("p (b e) -> p b e", e=E)

            def wide(t):
                return t[:, :].unsqueeze(2).broadcast_to([128, B, E])
            L, O, K, M = lg[0], lg[1][:, :], lg[2], lg[3]
            m1, m2, kk, e2 = small
            rank3 = rank[:, :].unsqueeze(1).broadcast_to([128, B, E])
            halves = logits.rearrange("p (b i e) -> p b i e", i=2, e=E)
            own(dve.tensor_copy(v3(L), halves[:, :, 0, :]))
            own(dve.tensor_tensor(v3(L), halves[:, :, 1, :], v3(L), ALU.add))
            own(dve.tensor_reduce(m1[:, :], v3(L), AX.X, ALU.max))
            own(dve.tensor_tensor(v3(M), v3(L), wide(m1), ALU.subtract))
            own(dve.scalar_tensor_tensor(v3(K), v3(M), 0.0, rank3, ALU.is_equal, ALU.mult))
            own(dve.tensor_reduce(kk[:, :], v3(K), AX.X, ALU.max))
            own(dve.tensor_tensor(v3(O), v3(K), wide(kk), ALU.is_equal))
            own(dve.scalar_tensor_tensor(L, O, BIG, M, ALU.mult, ALU.add))
            own(dve.tensor_reduce(m2[:, :], v3(L), AX.X, ALU.max))
            dve.sem_inc(exp_in, 1)
            own(dve.tensor_tensor(v3(K), v3(L), wide(m2), ALU.is_equal))
            own(dve.tensor_tensor(v3(K), v3(K), rank3, ALU.mult))
            own(dve.tensor_reduce(kk[:, :], v3(K), AX.X, ALU.max))
            own(dve.tensor_tensor(v3(K), v3(K), wide(kk), ALU.is_equal))
            dve.wait_ge(exp_out, 1)
            own(dve.tensor_scalar(m1[:, :], e2[:, :], 1.0, None, ALU.add))
            own(dve.reciprocal(m1[:, :], m1[:, :]))
            own(dve.tensor_tensor(m2[:, :], e2[:, :], m1[:, :], ALU.mult))
            own(dve.tensor_tensor(v3(O), v3(O), wide(m1), ALU.mult))
            own(dve.tensor_tensor(v3(K), v3(K), wide(m2), ALU.mult))
            own(dve.tensor_tensor(O, O, K, ALU.add))

            def gates(g, p):
                c_turned.wait(dve, g - 1)
                src = O[:, bass.ds(g * T * E, T * E)].rearrange("p (t e) -> p t e", e=E)
                own_g(dve.tensor_scalar(cpad[:, p, :, 0:E], src, 1.0, None, ALU.mult))
                own_g(dve.tensor_scalar(cpad[:, p, :, 64:64 + E], src, 1.0, None, ALU.mult))
                dve.tensor_tensor(cpad[:, p, :, 32:32 + E], src, cpad[:, p, :, 0:E],
                                  ALU.subtract).then_inc(cpad_ready.sem, 1)

            def gates_copy(g, p):
                c_turned.wait(dve, g + 1)
                if not (isinstance(g, int) and g < 2):
                    down_made.wait(dve, g * E - E)
                dve.tensor_copy(cT[:, p, :], bank(6).bitcast(fp16)[:, 0:GW]).then_inc(c_saved.sem, 1)

            def gate_hidden(n, k):
                gelu_done.wait(dve, n + 1)
                cb_made.wait(dve, n + 1)
                hl_ready.wait(dve, n - 1)
                dve.tensor_tensor(hc32[:, k % 2, :], bank(2 + k % 2), h32[:, k % 2, :],
                                  ALU.mult).then_inc(hc_ready.sem, 1)

            def mask_adj(g):
                dve.tensor_tensor(tile(adjT, g, 1, GW).rearrange("p (t d) -> p t d", t=T),
                                  tile(adjT, g, 1, GW).rearrange("p (t d) -> p t d", t=T),
                                  cols[:, bass.ds(g * T, T)].unsqueeze(2).broadcast_to([128, T, D]),
                                  ALU.mult).then_inc(adj_masked, 1)

            def ffn_add(g, p):
                moe_made.wait(dve, g + 1)
                dve.scalar_tensor_tensor(tile(X, g, 1, GW), bank(4 + p), 1.0 / WS, tile(X, g, 1, GW),
                                         ALU.mult, ALU.add).then_inc(x2_saved.sem, 1)

            def ffn_stats(g, rows):
                x2_saved.wait(dve, g + 1)
                ins = group_stats(g, rows)
                if T - 1 in rows:
                    ins.then_inc(own_stats, 1)

            def extras(g, k, p):
                if k == 1:
                    mask_adj(g)
                elif k == 4:
                    ffn_add(g - 1, p)
                elif k in (5, 6):
                    ffn_stats(g - 1, range(k * 2 - 10, k * 2 - 8))

            gate_own = sem("gate_own")
            own_g = Chain(dve, gate_own)
            gates(0, 0)
            gates_copy(0, 0)
            gates(1, 1)
            for k in range(E):
                if k == 4:
                    gates_copy(1, 1)
                gate_hidden(k, k)
                if k == 0:
                    own(dve.tensor_tensor(wTl[:, :], wT_scaled, wTh[:, :], ALU.subtract))
                elif k == 1:
                    own(dve.tensor_tensor(v1l[:, :], v12[:, 0:1].broadcast_to([128, 128]), v1h[:, :], ALU.subtract))
                elif k == 2:
                    own(dve.tensor_tensor(v2l[:, :], v12[:, 1:2].broadcast_to([128, 128]), v2h[:, :], ALU.subtract))
                elif k == 3:
                    dve.wait_ge(split_high, 3)
                    low(b2w[64:64 + E, :], b2raw[64:64 + E, :], b2t[64:64 + E, :])
                elif k == 5:
                    low(g1b_rows[32:33, :, :], g1b[32:33, :].unsqueeze(1).broadcast_to([1, T, D]), g1b_rows[32:33, :, :])
                elif k == 4:
                    own(dve.tensor_tensor(mask2[:, :], cols[:, 0:B], cols[:, 0:B], ALU.mult))
                    own(dve.tensor_tensor(pick[:, :], ident[:, 0:B], ident[:, B:2 * B], ALU.add))
                    own(dve.tensor_scalar(pick[:, :], pick[:, :], 1.0 / WS, None, ALU.mult))
                elif k >= 6:
                    dve.wait_ge(split_high, 4)
                    half = slice((k - 6) * E * F // 2, (k - 5) * E * F // 2)
                    low(m1l[:, half], m1raw[:, half], m1h[:, half])
            base = own_g.n
            mask_adj(0)
            dve.sem_inc(prep_done, 1)
            with dve.Fori(0, G // 2 - 1) as it:
                for q in range(2):
                    g = it * 2 + (q + 1)
                    p = (q + 1) % 2
                    own_g = Chain(dve, gate_own, it * 4 + (base + 2 * q))
                    gates(g + 1, 1 - p)
                    for k in range(E):
                        gate_hidden(g * E + k, k)
                        if k == 3:
                            gates_copy(g + 1, 1 - p)
                        extras(g, k, 1 - p)
            for k in range(E):
                gate_hidden((G - 1) * E + k, k)
                extras(G - 1, k, 0)
                if k == 2:
                    dve.wait_ge(own_stats, done_stats + G - 2)
                    begin_finish(MOST)
                if k == 5:
                    end_finish(3, MOST)
            norm(1, 1, None, range(T)).then_inc(n3_dve, 1)
            ffn_add(G - 1, 1)

            frac_own = sem("frac_own")

            def n3_low(g, p):
                n3h_saved.wait(dve, g + 1)
                dve.tensor_tensor(hl[:, p, :], bank(0), hh[:, p, :], ALU.subtract).then_inc(n3l_saved.sem, 1)

            def attended(g, p, chain):
                att_used.wait(dve, g + 1)
                here = [frac[:, p, i * T:(i + 1) * T] for i in range(2)]
                chain(dve.tensor_tensor(here[0][:, 0:T - 1].unsqueeze(2), first_three(bank(6 + p))[:, :, D:D + 1],
                                        cols[:, bass.ds(g * T, T - 1)].unsqueeze(2), ALU.mult))
                chain(dve.tensor_tensor(here[0][:, T - 1:T], bank(5)[:, D:D + 1], cols[:, bass.ds(g * T + T - 1, 1)],
                                        ALU.mult))
                chain(dve.tensor_scalar(here[0], here[0], 1e-8, None, ALU.add))
                chain(dve.reciprocal(here[1], here[0]))
                chain(dve.tensor_tensor(here[1], mask2[:, bass.ds(g * T, T)], here[1], ALU.mult))
                x3_ready.wait(dve, g - 1)
                dve.tensor_scalar(U[:, p, (T - 1) * D:], bank(5)[:, 0:D], here[1][:, T - 1:T], None,
                                  ALU.mult).then_inc(last_read.sem, 1)
                dve.tensor_tensor(U[:, p, 0:(T - 1) * D].rearrange("p (t d) -> p t d", t=T - 1),
                                  first_three(bank(6 + p))[:, :, 0:D],
                                  here[1][:, 0:T - 1].unsqueeze(2).broadcast_to([128, T - 1, D]),
                                  ALU.mult).then_inc(u_saved.sem, 1)

            def x3_stats(g):
                x3_ready.wait(dve, g + 1)
                group_stats(g).then_inc(own_stats, 1)

            LINKS3 = 5

            def g1_step(g, q, base):
                if 1 <= base <= G:
                    attended(g - 1, (q - 1) % 2, Chain(dve, frac_own, (g - 1) * LINKS3))
                if base + 2 < G:
                    n3_low(g + 2, q % 2)
                if base >= 2:
                    x3_stats(g - 2)

            n3_low(0, 0)
            ffn_stats(G - 1, range(T))
            done_stats += G
            dve.wait_ge(own_stats, done_stats)
            begin_finish(LAST)
            n3_low(1, 1)
            end_finish(4, LAST)
            g1_step(0, 0, 0)
            g1_step(1, 1, 1)
            with dve.Fori(1, G // 2 - 1) as it:
                for p in range(2):
                    g1_step(it * 2 + p, p, 2)
            for g in range(G - 2, G + 2):
                g1_step(g, g % 2, g)
            done_stats += G
            dve.wait_ge(own_stats, done_stats)
            finish_stats(5)

            def n4_norm(g, p):
                n4_turned.wait(dve, g - 1)
                n4_kept.wait(dve, g - 1)
                norm(g, p, n4_dve, (3,))

            def n4_low(g, p):
                n4_act.wait(dve, g + 1)
                n4_dve.wait(dve, g + 1)
                dve.tensor_scalar(tile(adjT, g, 1, GW), XN[:, p, :], 1.0, None, ALU.mult).then_inc(n4_kept.sem, 1)
                n4h_saved.wait(dve, g + 1)
                dve.tensor_reduce(xsum[:, bass.ds(g * T, T)], bank(6 + p).rearrange("p (t n) -> p t n", t=T),
                                  AX.X, ALU.add)
                dve.tensor_tensor(tile(XTl, g, 1, GW), bank(6 + p), tile(XTh, g, 1, GW),
                                  ALU.subtract).then_inc(n4l_saved.sem, 1)

            n4_norm(0, 0)
            with dve.Fori(0, G // 2 - 1) as it:
                for p in range(2):
                    n4_norm(it * 2 + (p + 1), 1 - p)
                    n4_low(it * 2 + p, p)
            n4_norm(G - 1, 1)
            n4_low(G - 2, 0)
            n4_low(G - 1, 1)
            n4l_saved.wait(dve, G)
            dve.sem_inc(route_dve, 1)

            dve.wait_ge(late_loaded, LATE)
            dve.wait_ge(route_pe, 1)

            def row(t, n=E):
                return t[:, 0:1].broadcast_to([B, n])
            own(dve.scalar_tensor_tensor(r[0][:, :], bank(2)[0:B, 0:E], 1.0 / N, br[:, :], ALU.mult, ALU.add))
            own(dve.tensor_reduce(rc[0][:, :], r[0][:, :], AX.X, ALU.max))
            own(dve.tensor_tensor(r[1][:, :], r[0][:, :], row(rc[0]), ALU.subtract))
            dve.sem_inc(route_dve, 1)
            dve.wait_ge(route_act, 1)
            own(dve.tensor_reduce(rc[1][:, :], r[1][:, :], AX.X, ALU.add))
            own(dve.reciprocal(rc[1][:, :], rc[1][:, :]))
            own(dve.tensor_tensor(r[2][:, :], r[1][:, :], row(rc[1]), ALU.mult))
            dve.sem_inc(route_dve, 1)
            dve.wait_ge(route_pe, 2)
            own(dve.tensor_scalar(r[3][:, :], bank(3)[0:B, 0:E], float(N) / CAPACITY, 1.0, ALU.mult, ALU.max))
            own(dve.reciprocal(r[3][:, :], r[3][:, :]))
            own(dve.tensor_tensor(r[0][:, :], r[2][:, :], r[3][:, :], ALU.mult))
            own(dve.tensor_reduce(rc[0][:, :], r[0][:, :], AX.X, ALU.max))
            own(dve.tensor_tensor(r[1][:, :], r[0][:, :], row(rc[0]), ALU.subtract))
            dve.sem_inc(route_dve, 1)
            dve.wait_ge(route_act, 2)
            own(dve.tensor_reduce(rc[1][:, :], r[1][:, :], AX.X, ALU.add))
            own(dve.reciprocal(rc[1][:, :], rc[1][:, :]))
            own(dve.tensor_tensor(r[0][:, :], r[1][:, :], row(rc[1]), ALU.mult))
            for i, (m, k) in enumerate(((rc[0], rc[2]), (rc[1], rc[3]))):
                own(dve.tensor_reduce(m[:, :], r[0][:, :], AX.X, ALU.max))
                own(dve.tensor_tensor(r[2][:, :], r[0][:, :], row(m), ALU.is_equal))
                own(dve.tensor_tensor(r[2][:, :], r[2][:, :], rank[0:B, :], ALU.mult))
                own(dve.tensor_reduce(k[:, :], r[2][:, :], AX.X, ALU.max))
                if i == 0:
                    own(dve.tensor_tensor(r[2][:, :], r[2][:, :], row(k), ALU.is_equal))
                    own(dve.scalar_tensor_tensor(r[0][:, :], r[2][:, :], BIG, r[0][:, :], ALU.mult, ALU.add))
            own(dve.tensor_tensor(rc[5][:, :], rc[1][:, :], rc[0][:, :], ALU.subtract))
            dve.sem_inc(route_dve, 1)
            dve.wait_ge(route_act, 3)
            own(dve.tensor_scalar(rc[6][:, :], rc[5][:, :], 1.0, None, ALU.add))
            own(dve.reciprocal(rc[6][:, :], rc[6][:, :]))
            own(dve.tensor_tensor(rc[7][:, :], rc[5][:, :], rc[6][:, :], ALU.mult))
            for i, (c, w) in enumerate(((rc[2], rc[6]), (rc[3], rc[7]))):
                own(dve.tensor_scalar(mix[:, i, :], rank[0:B, :], c[:, 0:1], w[:, 0:1], ALU.is_equal, ALU.mult))
            own(dve.tensor_tensor(mix[:, 0, :], mix[:, 0, :], mix[:, 1, :], ALU.add))
            for c in (rc[2], rc[3]):
                own(dve.tensor_scalar(c[:, :], c[:, :], -float(F), float(E * F), ALU.mult, ALU.add))
            for i, c in enumerate((rc[6], rc[7], rc[2], rc[3])):
                own(dve.tensor_scalar(diag[:, i, :], ident[0:B, 0:B], c[:, 0:1], None, ALU.mult))
            dve.sem_inc(route_dve, 1)
            dve.wait_ge(route_pe, 3)
            own(dve.tensor_copy(gate[:, :, :], bank(2)[:, 0:4 * B].rearrange("p (i b) -> p i b", i=4)))
            own(dve.tensor_copy(index[:, :].rearrange("p (b k) -> p k b", k=2), gate[:, 2:4, :]))
            dve.sem_inc(route_ready, 1)
            own(dve.tensor_copy(mixT[:, :, :], bank(6)[0:E, 0:B].unsqueeze(1).broadcast_to([E, 2, B])))
            dve.sem_inc(route_dve, 1)
            dve.wait_ge(route_pe, 4)
            own(dve.tensor_scalar(b2high[:, :], bank(7)[:, 0:D], WS, None, ALU.mult))
            own(dve.tensor_copy(b2sum[0:B, :], b2high[0:B, :]))
            low(b2sum[B:2 * B, :], bank(7)[B:2 * B, 0:D], b2high[B:2 * B, :])
            dve.sem_inc(route_ready, 1)

            z_own = sem("z_own")
            out_own = sem("out_own")
            chunk_own = sem("chunk_own")

            def gated(b, k):
                h_turned.wait(dve, b + 1)
                y_made.wait(dve, b - 3)
                dve.tensor_scalar(hT[:, k % 4, 0:F], bank(2 + k % 2 * 2)[:, 0:F], gate[:, 0, bass.ds(b, 1)], None,
                                  ALU.mult).then_inc(hT_dve.sem, 1)

            def z_sum(b, k):
                y_made.wait(dve, b + 1)
                dve.tensor_tensor(tile(adjT, b), bank(6 + k % 2)[:, 0:D], tile(adjT, b), ALU.add).then_inc(y_saved.sem, 1)

            def z_stats(b):
                y_saved.wait(dve, b + 1)
                dve.bn_stats(stats[:, bass.ds(b, 1), :], tile(adjT, b)).then_inc(z_own, 1)

            def z_begin(c, link):
                at = bass.ds(c * CB, CB)
                me, qe, mo, qo = (stats[:, at, i] for i in (1, 2, 4, 5))
                dve.wait_ge(z_own, c * CB + CB)
                link(dve.tensor_tensor(ln_b[:, at], me, mo, ALU.subtract))
                link(dve.tensor_tensor(ln_c[:, at], qe, qo, ALU.add))
                link(dve.scalar_tensor_tensor(ln_b[:, at], ln_b[:, at], 0.25, ln_b[:, at], ALU.mult, ALU.mult))
                link(dve.scalar_tensor_tensor(ln_c[:, at], ln_c[:, at], 1.0 / D, ln_b[:, at], ALU.mult, ALU.add))
                dve.sem_inc(z_moments, 1)
                link(dve.tensor_tensor(ln_b[:, at], me, mo, ALU.add))

            def z_end(c, link):
                at = bass.ds(c * CB, CB)
                dve.wait_ge(z_sqrt, c + 1)
                link(dve.reciprocal(rstd[:, at], ln_a[:, at]))
                link(dve.scalar_tensor_tensor(nmr[:, at], ln_b[:, at], -0.5, rstd[:, at], ALU.mult, ALU.mult))
                dve.sem_inc(z_ln, 1)

            def finish_group(g):
                norm_ready.wait(dve, g * T + T)
                dve.tensor_tensor(tile(adjT, g, 1, GW).rearrange("p (t d) -> p t d", t=T),
                                  tile(adjT, g, 1, GW).rearrange("p (t d) -> p t d", t=T),
                                  gam[:, :].unsqueeze(1).broadcast_to([128, T, D]), ALU.mult).then_inc(out_own, 1)
                xb_ready.wait(dve, g + 1)
                dve.wait_ge(out_own, g + 1)
                dve.tensor_tensor(tile(X, g, 1, GW), tile(adjT, g, 1, GW), tile(X, g, 1, GW),
                                  ALU.add).then_inc(out_ready.sem, 1)

            LINKS = 7

            def chunk(c, first=False, last=False):
                for i in range(CG):
                    for k in range(T):
                        b = c * CB + (i * T + k)
                        if not (last and i == CG - 1 and k == T - 1):
                            gated(b + 1, k + 1)
                        z_sum(b, k)
                        if i or k:
                            z_stats(c * CB + (i * T + k - 1))
                        if first:
                            continue
                        if i == 0 and k == 2:
                            z_end(c - 1, Chain(dve, chunk_own, c * LINKS - 2))
                        for done, at in enumerate(((1, 2), (2, 0), (2, 2), (3, 1))):
                            if (i, k) == at:
                                finish_group(c * CG + (done - CG))
                z_stats(c * CB + (CB - 1))
                z_begin(c, Chain(dve, chunk_own, c * LINKS))

            gated(0, 0)
            chunk(0, first=True)
            with dve.Fori(1, CHUNKS - 1) as c:
                chunk(c)
            chunk(CHUNKS - 1, last=True)
            z_end(CHUNKS - 1, Chain(dve, chunk_own, CHUNKS * LINKS - 2))
            for i in range(CG):
                finish_group(G - CG + i)

        @block.tensor
        def _(pe):
            def product(dst, parts, **kw):
                for i, (a, c) in enumerate(parts):
                    ins = pe.matmul(dst, a, c, start=(i == 0), stop=(i == len(parts) - 1))
                return ins

            def turn_adj(g, loads, q):
                pe.wait_ge(group_loaded[q], loads * 16)
                adjT_saved.wait(pe, g - 1)
                for j in range(T):
                    ins = pe.transpose(bank(q % 2)[:, j * N:(j + 1) * N], adj_in[:, q, j * N:(j + 1) * N], ident[:, :])
                ins.then_inc(adj_turned.sem, 1)

            def prepare():
                pe.wait_ge(weights_loaded, SMALL)
                pe.transpose(bank(6)[:, 0:B + 2 * E], rows_in[0:B + 2 * E, :], ident[0:B + 2 * E, 0:B + 2 * E])
                pe.transpose(bank(6)[:, 128:256], g1w[:, :], ident[:, :])
                pe.matmul(bank(6)[:, 256:258], g1w[:, :], avec[:, 0:2], start=True, stop=True)
                b_wide = avec[:, 2:3].broadcast_to([128, 128])
                pe.matmul(bank(6)[:, 258:259], b_wide, avec[:, 0:1], start=True, stop=False)
                pe.matmul(bank(6)[:, 258:259], b_wide, avec[:, 1:2], start=False, stop=True).then_inc(prep_pe, 1)

            def g0_z(g, p):
                xn_act.wait(pe, g + 1)
                xn_dve.wait(pe, g + 1)
                adjT_saved.wait(pe, g + 1)
                z_saved.wait(pe, g - 1)
                for j in range(T):
                    ins = pe.matmul(bank(2 + p)[:, j * N:(j + 1) * N], XN[:, p, j * D:(j + 1) * D],
                                    adjT[:, bass.ds(g * GW + j * N, N)], start=True, stop=True)
                ins.then_inc(z_made.sem, 1)

            def g0_out(g, p):
                z_saved.wait(pe, g + 1)
                x1_saved.wait(pe, g - 1)
                for j in range(T):
                    ins = pe.matmul(bank(4 + p)[:, j * D:(j + 1) * D], ZT[:, p, j * N:(j + 1) * N], g0w[:, :],
                                    start=True, stop=True)
                ins.then_inc(o_made.sem, 1)

            def g0_step(g, it, q):
                if not (isinstance(g, int) and g + 1 >= G):
                    g0_z(g + 1, (q + 1) % 2)
                if q < 1 or not isinstance(g, int):
                    turn_adj(g + 3, it + (1 if q < 1 else 2), (q + 3) % 4)
                g0_out(g, q % 2)

            pe.wait_ge(ident_made, 1)
            turn_adj(0, 1, 0)
            turn_adj(1, 1, 1)
            pe.wait_ge(g0_loaded, G0_LOADS)
            g0_z(0, 0)
            turn_adj(2, 1, 2)
            with pe.Fori(0, G // 4 - 1) as it:
                for q in range(4):
                    g0_step(it * 4 + q, it, q)
            for q in range(4):
                g0_step(G - 4 + q, G // 4 - 1, q)
            prepare()

            pe.wait_ge(prep_done, 1)

            def n2_turn(g, p):
                n2_act.wait(pe, g + 1)
                n2_dve.wait(pe, g + 1)
                n2l_saved.wait(pe, g - 1)
                for j in range(T):
                    ins = pe.transpose(bank(p)[:, j * N:(j + 1) * N], XN[:, p, j * D:(j + 1) * D], ident[:, :])
                ins.then_inc(n2_turned.sem, 1)

            def route(g):
                n2l_saved.wait(pe, g + 1)
                for j in range(T):
                    xh, xl = (tile(t, g * T + j) for t in (XTh, XTl))
                    pe.matmul(logits[:, bass.ds((g * T + j) * 2 * E, 2 * E)], xh, router[:, :],
                              start=True, stop=False, skip_group_check=True)
                    ins = pe.matmul(logits[:, bass.ds((g * T + j) * 2 * E, E)], xl, router[:, 0:E],
                                    start=False, stop=True, skip_group_check=True)
                return ins

            n2_turn(0, 0)
            n2_turn(1, 1)
            with pe.Fori(0, G // 4 - 1) as it:
                for q in range(4):
                    n2_turn(it * 4 + (q + 2), q % 2)
                    route(it * 4 + q)
            for g in (G - 4, G - 3):
                n2_turn(g + 2, g % 2)
                route(g)
            route(G - 2)
            route(G - 1).then_inc(logits_made, 1)

            pe.wait_ge(split_low, 2)

            def turn_gates(g, p):
                cpad_ready.wait(pe, g + 1)
                if not (isinstance(g, int) and g < 1):
                    c_saved.wait(pe, g)
                for j in range(T):
                    ins = pe.transpose(bank(6).bitcast(fp16)[:, j * N:(j + 1) * N], cpad[:, p, j, :], ident16[:, :])
                ins.then_inc(c_turned.sem, 1)

            def up(g, k):
                n = g * E + k
                gelu_done.wait(pe, n - 1)
                e = k % E
                w = slice(e * D, (e + 1) * D)
                xh, xl = (tile(t, g, 1, GW) for t in (XTh, XTl))
                product(bank(k % 2), [(w1h[:, w], xh), (w1l[:, w], xh), (w1h[:, w], xl)]).then_inc(up_made.sem, 1)

            def spread(g, k, p):
                n = g * E + k
                hc_ready.wait(pe, n - 1)
                if k == 0:
                    c_saved.wait(pe, g + 1)
                pe.matmul(bank(2 + k % 2), selector[:, k, :], cT[:, p, :], start=True, stop=True).then_inc(cb_made.sem, 1)

            def down(g, k, p):
                n = g * E + k
                hl_ready.wait(pe, n + 1)
                if k == 0:
                    x2_saved.wait(pe, g - 1)
                w = slice(k * D, (k + 1) * D)
                for j in range(T):
                    s = slice(j * N, (j + 1) * N)
                    o = bank(4 + p)[:, s]
                    for i, (a, c) in enumerate(((hh, w2h), (hh, w2l), (hl, w2h))):
                        ins = pe.matmul(o, a[:, k % 4, s], c[:, w], start=(k == 0 and j == 0 and i == 0),
                                        stop=False, skip_group_check=True)
                ins.then_inc(down_made.sem, 1)
                if k == E - 1:
                    for j in range(T):
                        s = slice(j * N, (j + 1) * N)
                        ins = pe.matmul(bank(4 + p)[:, s], cT[:, p, s], b2w[:, :], start=False, stop=(j == T - 1),
                                        skip_group_check=True)
                    ins.then_inc(moe_made.sem, 1)

            LAG = 3

            def first_step(g, k, p, last=False):
                up(g, k)
                spread(g, k, p)
                if k == 1 and not last:
                    turn_gates(g + 1, 1 - p)

            turn_gates(0, 0)
            for k in range(E):
                first_step(0, k, 0)
                if k == LAG:
                    pe.wait_ge(split_low, 3)
                if k >= LAG:
                    down(0, k - LAG, 0)
            pe.wait_ge(prep_done, 2)
            with pe.Fori(0, G // 2 - 1) as it:
                for q in range(2):
                    g = it * 2 + (q + 1)
                    p = (q + 1) % 2
                    for k in range(E):
                        first_step(g, k, p)
                        if k >= LAG:
                            down(g, k - LAG, p)
                        else:
                            down(g - 1, E + k - LAG, 1 - p)
            for k in range(E):
                first_step(G - 1, k, 1, last=True)
                if k >= LAG:
                    down(G - 1, k - LAG, 1)
                else:
                    down(G - 2, E + k - LAG, 0)
            for k in range(E - LAG, E):
                down(G - 1, k, 1)

            def n3_turn(g, p):
                n3_ready.wait(pe, g + 1)
                if not (isinstance(g, int) and g < 1):
                    n3l_saved.wait(pe, g)
                for j in range(T):
                    ins = pe.transpose(bank(0)[:, j * N:(j + 1) * N], XN[:, p, j * D:(j + 1) * D], ident[:, :])
                ins.then_inc(n3_turned.sem, 1)

            def g1_project(g, p):
                n3l_saved.wait(pe, g + 1)
                sig_ready.wait(pe, g - 1)
                th, tl = hh[:, p, :], hl[:, p, :]
                for i, (a, c) in enumerate(((v1h, th), (v1l, th), (v1h, tl))):
                    pe.matmul(bank(1 + p), a[:, :], c, start=(i == 0), stop=False, skip_group_check=True)
                for j in range(T):
                    s = slice(j * N, (j + 1) * N)
                    for i, (a, c) in enumerate(((th, v2h), (th, v2l), (tl, v2h))):
                        ins = pe.matmul(bank(1 + p)[:, s], a[:, s], c[:, :], start=False,
                                        stop=(j == T - 1 and i == 2), skip_group_check=True)
                ins.then_inc(scores_made.sem, 1)
                h_saved.wait(pe, g - 1)
                pe.matmul(bank(3 + p), two_ones[:, :], g1b_rows[:, :, :].rearrange("p t d -> p (t d)"),
                          start=True, stop=False, skip_group_check=True)
                for j in range(T):
                    s = slice(j * N, (j + 1) * N)
                    for i, (a, c) in enumerate(((th, wTh), (th, wTl), (tl, wTh))):
                        ins = pe.matmul(bank(3 + p)[:, s], a[:, s], c[:, :], start=False,
                                        stop=(j == T - 1 and i == 2), skip_group_check=True)
                ins.then_inc(proj_made.sem, 1)

            def g1_attend(g, p):
                att_ready.wait(pe, g + 1)
                h_saved.wait(pe, g + 1)
                u_saved.wait(pe, g - 1)
                for j in range(T - 1):
                    pe.matmul(first_three(bank(6 + p))[:, j, :], att[:, p, j * N:(j + 1) * N], H[:, p, j, :],
                              start=True, stop=True)
                if not (isinstance(g, int) and g < 1):
                    last_read.wait(pe, g)
                pe.matmul(bank(5)[:, 0:D + 1], att[:, p, (T - 1) * N:], H[:, p, T - 1, :],
                          start=True, stop=True).then_inc(att_used.sem, 1)

            n3_turn(0, 0)
            g1_project(0, 0)
            pe.wait_ge(ones_made, 1)
            x2_saved.wait(pe, G)
            n3_turn(1, 1)
            n3_turn(2, 0)
            g1_project(1, 1)
            g1_attend(0, 0)
            with pe.Fori(0, G // 2 - 2) as it:
                for q in range(2):
                    g = it * 2 + (q + 1)
                    n3_turn(g + 2, (q + 1) % 2)
                    g1_project(g + 1, q)
                    g1_attend(g, (q + 1) % 2)
            n3_turn(G - 1, 1)
            g1_project(G - 2, 0)
            g1_attend(G - 3, 1)
            g1_project(G - 1, 1)
            g1_attend(G - 2, 0)
            g1_attend(G - 1, 1)

            last_read.wait(pe, G)
            u_saved.wait(pe, G)
            with pe.Fori(0, G // 2) as it:
                for p in range(2):
                    g = it * 2 + p
                    n4_act.wait(pe, g + 1)
                    n4_dve.wait(pe, g + 1)
                    n4l_saved.wait(pe, g - 1)
                    for j in range(T):
                        ins = pe.transpose(bank(6 + p)[:, j * N:(j + 1) * N], XN[:, p, j * D:(j + 1) * D], ident[:, :])
                    ins.then_inc(n4_turned.sem, 1)

            pe.wait_ge(route_dve, 1)
            pe.wait_ge(late_loaded, LATE)
            pe.matmul(bank(2)[0:B, 0:E], xsum[:, :], wr[:, :], start=True, stop=True).then_inc(route_pe, 1)
            pe.wait_ge(route_dve, 3)
            pe.matmul(bank(3)[0:B, 0:E], ones[0:B, 0:B], r[2][:, :], start=True, stop=True).then_inc(route_pe, 1)
            pe.wait_ge(route_dve, 6)
            pe.matmul(bank(2)[:, 0:4 * B], ones[0:B, :], diag[:, :, :].rearrange("p i b -> p (i b)"),
                      start=True, stop=True)
            n4l_saved.wait(pe, G)
            pe.transpose(bank(6)[0:E, 0:B], mix[:, 0, :], ident[0:B, 0:B]).then_inc(route_pe, 1)
            pe.wait_ge(route_dve, 7)
            pe.matmul(bank(7)[:, 0:D], mixT[:, :, :].rearrange("e k b -> e (k b)"), mb2[:, :],
                      start=True, stop=True).then_inc(route_pe, 1)
            pe.wait_ge(route_ready, 1)
            pe.wait_ge(prep_done, 2)

            AHEAD = 2

            def experts(b, n):
                _, v = nc.values_load_multi_w_load_instructions(
                    index[0:1, bass.ds(b * 2, 2 * n)], engines=(mybir.EngineType.PE,), min_val=0, max_val=(E - 1) * F,
                    skip_runtime_bounds_check_because="the index of an expert's first column")
                return [(v[2 * i], v[2 * i + 1]) for i in range(n)]

            def ffn_up(b, k, es):
                g_ready.wait(pe, b - 1)
                s = slice(k % T * N, (k % T + 1) * N)
                xh, xl = hh[:, k // T % 2, s], hl[:, k // T % 2, s]
                for i, e in enumerate(es):
                    at = bass.ds(e, F)
                    ins = product(bank(k % 2)[:, i * F:(i + 1) * F], [(xh, m1h[:, at]), (xh, m1l[:, at]), (xl, m1h[:, at]),
                                                                      (two_ones[:, :], mb1[:, at])])
                ins.then_inc(f_made.sem, 1)

            def ffn_turn(b, k):
                g_ready.wait(pe, b + 1)
                hT_act.wait(pe, b - 1)
                hT_dve.wait(pe, b - 1)
                for i in range(2 * HALVES):
                    ins = pe.transpose(bank(2 + k % 2 * 2 + i // HALVES)[:, i % HALVES * N:(i % HALVES + 1) * N],
                                       h32[:, k % 4, i * N:(i + 1) * N], ident[:, :])
                ins.then_inc(h_turned.sem, 1)

            def ffn_down(b, k, es):
                hT_act.wait(pe, b + 1)
                hT_dve.wait(pe, b + 1)
                y_saved.wait(pe, b - 1)
                parts = [(hT[:, k % 4, (i * HALVES + h) * N:(i * HALVES + h + 1) * N], m2raw[:, bass.ds(e + h * D, D)])
                         for i, e in enumerate(es) for h in range(HALVES)]
                parts.append((pick[:, bass.ds(b, 1)].broadcast_to([128, N]), b2sum[:, :]))
                product(bank(6 + k % 2)[:, 0:D], parts).then_inc(y_made.sem, 1)

            first = experts(0, AHEAD)
            x_fetched.wait(pe, 1)
            ffn_up(0, 0, first[0])
            ffn_up(1, 1, first[1])
            ffn_turn(0, 0)
            pe.wait_ge(route_ready, 2)

            def group_round(it, q, last=False):
                es = experts(it * (2 * T) + q * T, T if last else T + AHEAD)
                for k in range(T):
                    if not (last and k >= T - AHEAD):
                        if k == T - AHEAD:
                            x_fetched.wait(pe, it * 2 + (q + 2))
                        ffn_up(it * (2 * T) + (q * T + k + AHEAD), q * T + k + AHEAD, es[k + AHEAD])
                    if not (last and k == T - 1):
                        ffn_turn(it * (2 * T) + (q * T + k + 1), k + 1)
                    ffn_down(it * (2 * T) + (q * T + k), k, es[k])

            with pe.Fori(0, B // (2 * T) - 1) as it:
                group_round(it, 0)
                group_round(it, 1)
            group_round(B // (2 * T) - 1, 0)
            group_round(B // (2 * T) - 1, 1, last=True)


_INS = ['x', 'adj', 'nodemask', 'L0_gnn_weight', 'L0_gnn_bias', 'L0_ffn_router_w', 'L0_ffn_w1', 'L0_ffn_b1',
        'L0_ffn_w2', 'L0_ffn_b2', 'L1_gnn_W', 'L1_gnn_b', 'L1_gnn_a1', 'L1_gnn_a2', 'L1_gnn_att_b', 'L1_ffn_Wr',
        'L1_ffn_br', 'L1_ffn_W1', 'L1_ffn_b1', 'L1_ffn_W2', 'L1_ffn_b2', 'L1_ffn_gamma', 'L1_ffn_beta']


def kernel(**inputs):
    import numpy as _np
    import concourse.bacc as _bacc
    from concourse import mybir as _mybir
    from concourse.bass_utils import run_bass_kernel_spmd as _run

    nc = _bacc.Bacc("TRN2", target_bir_lowering=False, num_devices=1)
    arrays, args = {}, []
    for name in _INS:
        a = _np.ascontiguousarray(inputs[name])
        if a.ndim == 0:
            a = a.reshape(1)
        arrays[f"in_{name}"] = a
        args.append(nc.dram_tensor(f"in_{name}", a.shape, _mybir.dt.from_np(a.dtype), kind="ExternalInput").ap())
    shape = arrays["in_x"].shape
    args.append(nc.dram_tensor("out_dram", shape, _mybir.dt.float32, kind="ExternalOutput").ap())
    graph_network(nc, *args)
    r = _run(nc, [arrays], core_ids=[0])
    return r.results[0]["out_dram"]
```
